# Optimizing a Trainium2 kernel written in Bass

```python
import numpy as np
import jax
import jax.numpy as jnp

def _softmax(x, axis=-1):
    return jax.nn.softmax(x, axis=axis)

def _gelu(x):
    return jax.nn.gelu(x, approximate=True)

def _silu(x):
    return jax.nn.silu(x)

def _sigmoid(x):
    return jax.nn.sigmoid(x)

def _layernorm(x, axis=-1, eps=1e-05):
    m = jnp.mean(x, axis=axis, keepdims=True)
    v = jnp.var(x, axis=axis, keepdims=True)
    return (x - m) / jnp.sqrt(v + eps)

def _scatter_add(tgt, idx, src, axis=0):
    return tgt.at[idx].add(src)

def _segment_sum(src, seg, n):
    return jax.ops.segment_sum(src, seg, n)
kernel_name = 'mk_seq_preln_d4_jaxref_r8_4e0b3b'

def setup_inputs(seed: int=0):
    np.random.seed(seed)
    _w = jnp.asarray

    def _L0_attn_setup():
        import jax, jax.numpy as jnp
        import numpy as np
        B, L, E, H = (2, 128, 128, 16)
        D = E // H
        EPS = 1e-06

        def rmsnorm(x, w, eps=1e-06):
            var = jnp.mean(jnp.square(x), axis=-1, keepdims=True)
            return x * jax.lax.rsqrt(var + eps) * w

        def cosformer_attn(x, qkv_w, qkv_b, out_w, out_b):
            b, l, e = x.shape
            qkv = x @ qkv_w + qkv_b
            q, k, v = jnp.split(qkv, 3, axis=-1)
            q = q.reshape(b, l, H, D).transpose(0, 2, 1, 3)
            k = k.reshape(b, l, H, D).transpose(0, 2, 1, 3)
            v = v.reshape(b, l, H, D).transpose(0, 2, 1, 3)
            positions = jnp.arange(l, dtype=jnp.float32).reshape(1, 1, l, 1)
            cos_w = jnp.cos(jnp.pi / 2 * positions / l)
            sin_w = jnp.sin(jnp.pi / 2 * positions / l)
            q_prime = jax.nn.relu(q)
            k_prime = jax.nn.relu(k)
            q_cos, q_sin = (q_prime * cos_w, q_prime * sin_w)
            k_cos, k_sin = (k_prime * cos_w, k_prime * sin_w)
            kv_cos_cumsum = jnp.cumsum(jnp.einsum('bhld,bhle->bhlde', k_cos, v), axis=2)
            context_cos = jnp.einsum('bhld,bhlde->bhle', q_cos, kv_cos_cumsum)
            kv_sin_cumsum = jnp.cumsum(jnp.einsum('bhld,bhle->bhlde', k_sin, v), axis=2)
            context_sin = jnp.einsum('bhld,bhlde->bhle', q_sin, kv_sin_cumsum)
            context = context_cos + context_sin
            k_cos_cumsum = jnp.cumsum(k_cos, axis=2)
            k_sin_cumsum = jnp.cumsum(k_sin, axis=2)
            norm = jnp.einsum('bhld,bhld->bhl', q_cos, k_cos_cumsum) + jnp.einsum('bhld,bhld->bhl', q_sin, k_sin_cumsum)
            output = context / (norm[..., None] + EPS)
            output = output.transpose(0, 2, 1, 3).reshape(b, l, e)
            return output @ out_w + out_b
        key = jax.random.key(seed)
        ks = jax.random.split(key, 6)
        x = jax.random.normal(ks[0], (B, L, E), dtype=jnp.float32)
        qkv_w = jax.random.normal(ks[1], (E, 3 * E), dtype=jnp.float32) / np.sqrt(E)
        qkv_b = jnp.zeros((3 * E,), dtype=jnp.float32)
        out_w = jax.random.normal(ks[2], (E, E), dtype=jnp.float32) / np.sqrt(E)
        out_b = jnp.zeros((E,), dtype=jnp.float32)
        norm1_w = jnp.ones((E,), dtype=jnp.float32)
        norm2_w = jnp.ones((E,), dtype=jnp.float32)
        mlp_w1 = jax.random.normal(ks[3], (E, 4 * E), dtype=jnp.float32) / np.sqrt(E)
        mlp_b1 = jnp.zeros((4 * E,), dtype=jnp.float32)
        mlp_w2 = jax.random.normal(ks[4], (4 * E, E), dtype=jnp.float32) / np.sqrt(4 * E)
        mlp_b2 = jnp.zeros((E,), dtype=jnp.float32)
        return dict(x=x, qkv_w=qkv_w, qkv_b=qkv_b, out_w=out_w, out_b=out_b, norm1_w=norm1_w, norm2_w=norm2_w, mlp_w1=mlp_w1, mlp_b1=mlp_b1, mlp_w2=mlp_w2, mlp_b2=mlp_b2)
    _L0_attn_in = _L0_attn_setup()

    def _L0_ffn_setup():
        import jax, jax.numpy as jnp
        import numpy as np
        DIM = 128

        def _reference_tuple_inner(x, W_r, W_k, W_v, mu_r, mu_k):
            B, T, C = x.shape
            x_prev = jnp.concatenate([jnp.zeros((B, 1, C), x.dtype), x[:, :-1, :]], axis=1)
            xr = mu_r * x + (1.0 - mu_r) * x_prev
            xk = mu_k * x + (1.0 - mu_k) * x_prev
            r = jax.nn.sigmoid(jnp.einsum('btc,dc->btd', xr, W_r))
            k = jnp.einsum('btc,dc->btd', xk, W_k)
            k_act = jnp.square(jax.nn.relu(k))
            out = r * jnp.einsum('btc,dc->btd', k_act, W_v)
            new_state = x[:, -1, :]
            return (out, new_state)
        key = jax.random.key(seed)
        ks = jax.random.split(key, 6)
        B, T, C = (8, 256, DIM)
        x = jax.random.normal(ks[0], (B, T, C), dtype=jnp.float32)
        s = 1.0 / np.sqrt(C)
        W_r = jax.random.uniform(ks[1], (C, C), jnp.float32, -s, s)
        W_k = jax.random.uniform(ks[2], (C, C), jnp.float32, -s, s)
        W_v = jax.random.uniform(ks[3], (C, C), jnp.float32, -s, s)
        mu_r = jax.random.uniform(ks[4], (C,), jnp.float32)
        mu_k = jax.random.uniform(ks[5], (C,), jnp.float32)
        return {'x': x, 'W_r': W_r, 'W_k': W_k, 'W_v': W_v, 'mu_r': mu_r, 'mu_k': mu_k}
    _L0_ffn_in = _L0_ffn_setup()

    def _L1_attn_setup():
        import jax, jax.numpy as jnp
        import numpy as np
        B, L, D = (2, 256, 128)
        H, HD = (16, 64)
        LD = 32
        key = jax.random.key(seed)
        ks = jax.random.split(key, 6)
        s = lambda fan_in: 1.0 / np.sqrt(fan_in)
        x_bld = jax.random.normal(ks[0], (B, L, D), dtype=jnp.float32)
        Wq = jax.random.normal(ks[1], (D, H, HD), dtype=jnp.float32) * s(D)
        Wkv_down = jax.random.normal(ks[2], (D, LD), dtype=jnp.float32) * s(D)
        Wk_up = jax.random.normal(ks[3], (LD, H, HD), dtype=jnp.float32) * s(LD)
        Wv_up = jax.random.normal(ks[4], (LD, H, HD), dtype=jnp.float32) * s(LD)
        Wout = jax.random.normal(ks[5], (H, HD, D), dtype=jnp.float32) * s(H * HD)
        return {'x_bld': x_bld, 'Wq': Wq, 'Wkv_down': Wkv_down, 'Wk_up': Wk_up, 'Wv_up': Wv_up, 'Wout': Wout}
    _L1_attn_in = _L1_attn_setup()

    def _L1_ffn_setup():
        import jax, jax.numpy as jnp
        from jax import lax
        import numpy as np
        D_MODEL = 128
        HIDDEN = 64
        N_EXPERTS = 32
        TOP_K = 2
        B, S = (1, 512)

        def _moe_group(x2, router_w, wg, wu, wd, top_k):
            T = x2.shape[0]
            n_experts = router_w.shape[1]
            logits = x2 @ router_w
            scores = jax.nn.softmax(logits, axis=-1)
            expert_weights, expert_indices = lax.top_k(scores, top_k)
            flat_e = expert_indices.reshape(-1)
            flat_w = expert_weights.reshape(-1)
            flat_t = jnp.repeat(jnp.arange(T), top_k)
            order = jnp.argsort(flat_e)
            tok = flat_t[order]
            xs = x2[tok]
            group_sizes = jnp.bincount(flat_e, length=n_experts).astype(jnp.int32)
            gate = lax.ragged_dot(xs, wg, group_sizes)
            up = lax.ragged_dot(xs, wu, group_sizes)
            ys = lax.ragged_dot(jax.nn.silu(gate) * up, wd, group_sizes)
            ys = ys * flat_w[order][:, None]
            return jnp.zeros_like(x2).at[tok].add(ys)
        key = jax.random.key(seed)
        ks = jax.random.split(key, 9)
        w = lambda k, shape: jax.random.normal(k, shape, dtype=jnp.float32) * 0.02
        return {'x': jax.random.normal(ks[0], (B, S, D_MODEL), dtype=jnp.float32), 'router_w0': w(ks[1], (D_MODEL, N_EXPERTS)), 'wg0': w(ks[2], (N_EXPERTS, D_MODEL, HIDDEN)), 'wu0': w(ks[3], (N_EXPERTS, D_MODEL, HIDDEN)), 'wd0': w(ks[4], (N_EXPERTS, HIDDEN, D_MODEL)), 'router_w1': w(ks[5], (D_MODEL, N_EXPERTS)), 'wg1': w(ks[6], (N_EXPERTS, D_MODEL, HIDDEN)), 'wu1': w(ks[7], (N_EXPERTS, D_MODEL, HIDDEN)), 'wd1': w(ks[8], (N_EXPERTS, HIDDEN, D_MODEL))}
    _L1_ffn_in = _L1_ffn_setup()

    def _L2_attn_setup():
        import jax, jax.numpy as jnp
        import numpy as np
        N_HEAD = 16
        ROPE_BASE = 10000.0

        def _rope(Y, d_param):
            b, h, t, dh = Y.shape
            mid = d_param // 2
            Y1 = Y[:, :mid]
            Y2 = Y[:, mid:]
            Ym1 = jnp.concatenate([Y1, Y2], axis=1)
            Ym2 = jnp.concatenate([-Y2, Y1], axis=1)
            j = jnp.arange(t, dtype=Y.dtype)[:, None]
            i = jnp.arange(dh // 2, dtype=Y.dtype)[None, :]
            theta = j * jnp.power(jnp.asarray(ROPE_BASE, Y.dtype), -2.0 * i / dh)
            cos = jnp.cos(theta)
            sin = jnp.sin(theta)
            theta1 = jnp.concatenate([cos, cos], axis=1)
            theta2 = jnp.concatenate([sin, sin], axis=1)
            return Ym1 * theta1 + Ym2 * theta2
        key = jax.random.key(seed)
        ks = jax.random.split(key, 9)
        b, t, e = (2, 256, 128)
        s = 1.0 / np.sqrt(e)
        return {'x': jax.random.normal(ks[0], (b, t, e), dtype=jnp.float32), 'Wq': jax.random.normal(ks[1], (e, e), dtype=jnp.float32) * s, 'bq': jax.random.normal(ks[2], (e,), dtype=jnp.float32) * 0.01, 'Wk': jax.random.normal(ks[3], (e, e), dtype=jnp.float32) * s, 'bk': jax.random.normal(ks[4], (e,), dtype=jnp.float32) * 0.01, 'Wv': jax.random.normal(ks[5], (e, e), dtype=jnp.float32) * s, 'bv': jax.random.normal(ks[6], (e,), dtype=jnp.float32) * 0.01, 'Wo': jax.random.normal(ks[7], (e, e), dtype=jnp.float32) * s, 'bo': jax.random.normal(ks[8], (e,), dtype=jnp.float32) * 0.01}
    _L2_attn_in = _L2_attn_setup()

    def _L2_ffn_setup():
        import jax, jax.numpy as jnp
        import numpy as np
        K_TOP = 2
        key = jax.random.key(seed)
        k1, k2, k3 = jax.random.split(key, 3)
        B, S, H, E = (4, 256, 128, 8)
        hidden_states = jax.random.normal(k1, (B, S, H), dtype=jnp.float32)
        router_w = jax.random.normal(k2, (E, H), dtype=jnp.float32) * 0.02
        expert_weights = jax.random.normal(k3, (E, H, H), dtype=jnp.float32) * 0.02
        return {'hidden_states': hidden_states, 'router_w': router_w, 'expert_weights': expert_weights}
    _L2_ffn_in = _L2_ffn_setup()

    def _L3_attn_setup():
        import jax, jax.numpy as jnp
        import numpy as np
        D_MODEL = 128
        D_STATE = 128
        D_CONV = 4
        EXPAND = 2
        HEADDIM = 64
        D_INNER = EXPAND * D_MODEL
        NHEADS = D_INNER // HEADDIM
        NGROUPS = 1
        CONV_DIM = D_INNER + 2 * NGROUPS * D_STATE
        D_IN_PROJ = 2 * D_INNER + 2 * NGROUPS * D_STATE + NHEADS
        EPS = 1e-05

        def rmsnorm(x, w):
            var = jnp.mean(jnp.square(x), axis=-1, keepdims=True)
            return x * jax.lax.rsqrt(var + EPS) * w

        def causal_dwconv(x, w, b):
            B, S, C = x.shape
            K = w.shape[1]
            xt = jnp.transpose(x, (0, 2, 1))
            xt = jnp.pad(xt, ((0, 0), (0, 0), (K - 1, 0)))
            out = jax.lax.conv_general_dilated(xt, w[:, None, :], window_strides=(1,), padding='VALID', feature_group_count=C)
            return jnp.transpose(out + b[:, None], (0, 2, 1))

        def ssd_scan(dt, xh, Bm, Cm, A):
            B, S, H = dt.shape
            P = xh.shape[-1]
            N = Bm.shape[-1]

            def step(h, inp):
                dt_t, x_t, B_t, C_t = inp
                decay = jnp.exp(dt_t * A)
                upd = dt_t[:, :, None, None] * x_t[:, :, :, None] * B_t[:, None, None, :]
                h = h * decay[:, :, None, None] + upd
                y_t = jnp.einsum('bhpn,bn->bhp', h, C_t)
                return (h, y_t)
            h0 = jnp.zeros((B, H, P, N), dtype=xh.dtype)
            xs = (jnp.moveaxis(dt, 1, 0), jnp.moveaxis(xh, 1, 0), jnp.moveaxis(Bm, 1, 0), jnp.moveaxis(Cm, 1, 0))
            _, ys = jax.lax.scan(step, h0, xs)
            return jnp.moveaxis(ys, 0, 1)
        key = jax.random.key(seed)
        ks = jax.random.split(key, 10)
        B, S = (8, 256)
        x = jax.random.normal(ks[0], (B, S, D_MODEL), dtype=jnp.float32)
        norm_w = jnp.ones((D_MODEL,), jnp.float32)
        in_proj_w = jax.random.normal(ks[1], (D_IN_PROJ, D_MODEL), jnp.float32) * D_MODEL ** (-0.5)
        conv_w = jax.random.normal(ks[2], (CONV_DIM, D_CONV), jnp.float32) * D_CONV ** (-0.5)
        conv_b = jnp.zeros((CONV_DIM,), jnp.float32)
        dt_bias = jnp.log(jnp.expm1(jax.random.uniform(ks[3], (NHEADS,), minval=0.001, maxval=0.1)))
        A_log = jnp.log(jax.random.uniform(ks[4], (NHEADS,), minval=1.0, maxval=16.0))
        D_param = jnp.ones((NHEADS,), jnp.float32)
        gate_w = jnp.ones((D_INNER,), jnp.float32)
        out_proj_w = jax.random.normal(ks[5], (D_MODEL, D_INNER), jnp.float32) * D_INNER ** (-0.5)
        return {'x': x, 'norm_w': norm_w, 'in_proj_w': in_proj_w, 'conv_w': conv_w, 'conv_b': conv_b, 'dt_bias': dt_bias, 'A_log': A_log, 'D_param': D_param, 'gate_w': gate_w, 'out_proj_w': out_proj_w}
    _L3_attn_in = _L3_attn_setup()

    def _L3_ffn_setup():
        import jax, jax.numpy as jnp
        import numpy as np
        D = 128
        H = 16
        HD = D // H
        L = 64
        E = 8
        B, T = (4, 256)
        EPS = 1e-06

        def _glorot(k, shape):
            fan_in, fan_out = (shape[-2], shape[-1])
            lim = np.sqrt(6.0 / (fan_in + fan_out)).astype(np.float32)
            return jax.random.uniform(k, shape, jnp.float32, -lim, lim)

        def _rmsnorm(x, gamma):
            return gamma * x * jax.lax.rsqrt(jnp.mean(x * x, axis=-1, keepdims=True) + EPS)
        key = jax.random.key(seed)
        ks = jax.random.split(key, 8)
        return {'x': jax.random.normal(ks[0], (B, T, D), jnp.float32), 'gamma1': jnp.ones((D,), jnp.float32), 'Wq': _glorot(ks[1], (D, D)), 'bq': jnp.zeros((D,), jnp.float32), 'Wdown': _glorot(ks[2], (D, L)), 'bdown': jnp.zeros((L,), jnp.float32), 'Wup': _glorot(ks[3], (L, 2 * D)), 'bup': jnp.zeros((2 * D,), jnp.float32), 'Wo': _glorot(ks[4], (D, D)), 'bo': jnp.zeros((D,), jnp.float32), 'gamma2': jnp.ones((D,), jnp.float32), 'Wg': _glorot(ks[5], (D, E)), 'bg': jnp.zeros((E,), jnp.float32), 'We': _glorot(ks[6], (E, D, D))}
    _L3_ffn_in = _L3_ffn_setup()
    _d = {'L0_attn_x': _L0_attn_in['x'], 'L0_attn_qkv_w': _L0_attn_in['qkv_w'], 'L0_attn_qkv_b': _L0_attn_in['qkv_b'], 'L0_attn_out_w': _L0_attn_in['out_w'], 'L0_attn_out_b': _L0_attn_in['out_b'], 'L0_attn_norm1_w': _L0_attn_in['norm1_w'], 'L0_attn_norm2_w': _L0_attn_in['norm2_w'], 'L0_attn_mlp_w1': _L0_attn_in['mlp_w1'], 'L0_attn_mlp_b1': _L0_attn_in['mlp_b1'], 'L0_attn_mlp_w2': _L0_attn_in['mlp_w2'], 'L0_attn_mlp_b2': _L0_attn_in['mlp_b2'], 'L0_ffn_W_r': _L0_ffn_in['W_r'], 'L0_ffn_W_k': _L0_ffn_in['W_k'], 'L0_ffn_W_v': _L0_ffn_in['W_v'], 'L0_ffn_mu_r': _L0_ffn_in['mu_r'], 'L0_ffn_mu_k': _L0_ffn_in['mu_k'], 'L1_attn_Wq': _L1_attn_in['Wq'], 'L1_attn_Wkv_down': _L1_attn_in['Wkv_down'], 'L1_attn_Wk_up': _L1_attn_in['Wk_up'], 'L1_attn_Wv_up': _L1_attn_in['Wv_up'], 'L1_attn_Wout': _L1_attn_in['Wout'], 'L1_ffn_router_w0': _L1_ffn_in['router_w0'], 'L1_ffn_wg0': _L1_ffn_in['wg0'], 'L1_ffn_wu0': _L1_ffn_in['wu0'], 'L1_ffn_wd0': _L1_ffn_in['wd0'], 'L1_ffn_router_w1': _L1_ffn_in['router_w1'], 'L1_ffn_wg1': _L1_ffn_in['wg1'], 'L1_ffn_wu1': _L1_ffn_in['wu1'], 'L1_ffn_wd1': _L1_ffn_in['wd1'], 'L2_attn_Wq': _L2_attn_in['Wq'], 'L2_attn_bq': _L2_attn_in['bq'], 'L2_attn_Wk': _L2_attn_in['Wk'], 'L2_attn_bk': _L2_attn_in['bk'], 'L2_attn_Wv': _L2_attn_in['Wv'], 'L2_attn_bv': _L2_attn_in['bv'], 'L2_attn_Wo': _L2_attn_in['Wo'], 'L2_attn_bo': _L2_attn_in['bo'], 'L2_ffn_router_w': _L2_ffn_in['router_w'], 'L2_ffn_expert_weights': _L2_ffn_in['expert_weights'], 'L3_attn_norm_w': _L3_attn_in['norm_w'], 'L3_attn_in_proj_w': _L3_attn_in['in_proj_w'], 'L3_attn_conv_w': _L3_attn_in['conv_w'], 'L3_attn_conv_b': _L3_attn_in['conv_b'], 'L3_attn_dt_bias': _L3_attn_in['dt_bias'], 'L3_attn_A_log': _L3_attn_in['A_log'], 'L3_attn_D_param': _L3_attn_in['D_param'], 'L3_attn_gate_w': _L3_attn_in['gate_w'], 'L3_attn_out_proj_w': _L3_attn_in['out_proj_w'], 'L3_ffn_gamma1': _L3_ffn_in['gamma1'], 'L3_ffn_Wq': _L3_ffn_in['Wq'], 'L3_ffn_bq': _L3_ffn_in['bq'], 'L3_ffn_Wdown': _L3_ffn_in['Wdown'], 'L3_ffn_bdown': _L3_ffn_in['bdown'], 'L3_ffn_Wup': _L3_ffn_in['Wup'], 'L3_ffn_bup': _L3_ffn_in['bup'], 'L3_ffn_Wo': _L3_ffn_in['Wo'], 'L3_ffn_bo': _L3_ffn_in['bo'], 'L3_ffn_gamma2': _L3_ffn_in['gamma2'], 'L3_ffn_Wg': _L3_ffn_in['Wg'], 'L3_ffn_bg': _L3_ffn_in['bg'], 'L3_ffn_We': _L3_ffn_in['We']}
    _x0 = _d['L0_attn_x']
    _d['L0_attn_x'] = jax.random.normal(jax.random.fold_in(jax.random.key(seed), 1), (16, 512, 128), dtype=_x0.dtype)
    del _x0
    return _d

def reference(L0_attn_x, L0_attn_qkv_w, L0_attn_qkv_b, L0_attn_out_w, L0_attn_out_b, L0_attn_norm1_w, L0_attn_norm2_w, L0_attn_mlp_w1, L0_attn_mlp_b1, L0_attn_mlp_w2, L0_attn_mlp_b2, L0_ffn_W_r, L0_ffn_W_k, L0_ffn_W_v, L0_ffn_mu_r, L0_ffn_mu_k, L1_attn_Wq, L1_attn_Wkv_down, L1_attn_Wk_up, L1_attn_Wv_up, L1_attn_Wout, L1_ffn_router_w0, L1_ffn_wg0, L1_ffn_wu0, L1_ffn_wd0, L1_ffn_router_w1, L1_ffn_wg1, L1_ffn_wu1, L1_ffn_wd1, L2_attn_Wq, L2_attn_bq, L2_attn_Wk, L2_attn_bk, L2_attn_Wv, L2_attn_bv, L2_attn_Wo, L2_attn_bo, L2_ffn_router_w, L2_ffn_expert_weights, L3_attn_norm_w, L3_attn_in_proj_w, L3_attn_conv_w, L3_attn_conv_b, L3_attn_dt_bias, L3_attn_A_log, L3_attn_D_param, L3_attn_gate_w, L3_attn_out_proj_w, L3_ffn_gamma1, L3_ffn_Wq, L3_ffn_bq, L3_ffn_Wdown, L3_ffn_bdown, L3_ffn_Wup, L3_ffn_bup, L3_ffn_Wo, L3_ffn_bo, L3_ffn_gamma2, L3_ffn_Wg, L3_ffn_bg, L3_ffn_We):

    def _L0_attn_ref(x, qkv_w, qkv_b, out_w, out_b, norm1_w, norm2_w, mlp_w1, mlp_b1, mlp_w2, mlp_b2):
        import jax, jax.numpy as jnp
        import numpy as np
        B, L, E, H = (2, 128, 128, 16)
        D = E // H
        EPS = 1e-06

        def rmsnorm(x, w, eps=1e-06):
            var = jnp.mean(jnp.square(x), axis=-1, keepdims=True)
            return x * jax.lax.rsqrt(var + eps) * w

        def cosformer_attn(x, qkv_w, qkv_b, out_w, out_b):
            b, l, e = x.shape
            qkv = x @ qkv_w + qkv_b
            q, k, v = jnp.split(qkv, 3, axis=-1)
            q = q.reshape(b, l, H, D).transpose(0, 2, 1, 3)
            k = k.reshape(b, l, H, D).transpose(0, 2, 1, 3)
            v = v.reshape(b, l, H, D).transpose(0, 2, 1, 3)
            positions = jnp.arange(l, dtype=jnp.float32).reshape(1, 1, l, 1)
            cos_w = jnp.cos(jnp.pi / 2 * positions / l)
            sin_w = jnp.sin(jnp.pi / 2 * positions / l)
            q_prime = jax.nn.relu(q)
            k_prime = jax.nn.relu(k)
            q_cos, q_sin = (q_prime * cos_w, q_prime * sin_w)
            k_cos, k_sin = (k_prime * cos_w, k_prime * sin_w)
            kv_cos_cumsum = jnp.cumsum(jnp.einsum('bhld,bhle->bhlde', k_cos, v), axis=2)
            context_cos = jnp.einsum('bhld,bhlde->bhle', q_cos, kv_cos_cumsum)
            kv_sin_cumsum = jnp.cumsum(jnp.einsum('bhld,bhle->bhlde', k_sin, v), axis=2)
            context_sin = jnp.einsum('bhld,bhlde->bhle', q_sin, kv_sin_cumsum)
            context = context_cos + context_sin
            k_cos_cumsum = jnp.cumsum(k_cos, axis=2)
            k_sin_cumsum = jnp.cumsum(k_sin, axis=2)
            norm = jnp.einsum('bhld,bhld->bhl', q_cos, k_cos_cumsum) + jnp.einsum('bhld,bhld->bhl', q_sin, k_sin_cumsum)
            output = context / (norm[..., None] + EPS)
            output = output.transpose(0, 2, 1, 3).reshape(b, l, e)
            return output @ out_w + out_b
        h = x + cosformer_attn(rmsnorm(x, norm1_w), qkv_w, qkv_b, out_w, out_b)
        m = rmsnorm(h, norm2_w)
        m = jax.nn.gelu(m @ mlp_w1 + mlp_b1) @ mlp_w2 + mlp_b2
        return h + m

    def _L0_ffn_ref(x, W_r, W_k, W_v, mu_r, mu_k):
        import jax, jax.numpy as jnp
        import numpy as np
        DIM = 128

        def _reference_tuple_inner(x, W_r, W_k, W_v, mu_r, mu_k):
            B, T, C = x.shape
            x_prev = jnp.concatenate([jnp.zeros((B, 1, C), x.dtype), x[:, :-1, :]], axis=1)
            xr = mu_r * x + (1.0 - mu_r) * x_prev
            xk = mu_k * x + (1.0 - mu_k) * x_prev
            r = jax.nn.sigmoid(jnp.einsum('btc,dc->btd', xr, W_r))
            k = jnp.einsum('btc,dc->btd', xk, W_k)
            k_act = jnp.square(jax.nn.relu(k))
            out = r * jnp.einsum('btc,dc->btd', k_act, W_v)
            new_state = x[:, -1, :]
            return (out, new_state)
        return _reference_tuple_inner(x, W_r, W_k, W_v, mu_r, mu_k)[0]

    def _L1_attn_ref(x_bld, Wq, Wkv_down, Wk_up, Wv_up, Wout):
        import jax, jax.numpy as jnp
        import numpy as np
        B, L, D = (2, 256, 128)
        H, HD = (16, 64)
        LD = 32
        q_blhd = jnp.einsum('bld,dhk->blhk', x_bld, Wq)
        latent_bll = jnp.einsum('bld,dc->blc', x_bld, Wkv_down)
        k_blhd = jnp.einsum('blc,chk->blhk', latent_bll, Wk_up)
        v_blhd = jnp.einsum('blc,chk->blhk', latent_bll, Wv_up)
        attn = jnp.einsum('bqhd,bkhd->bhqk', q_blhd, k_blhd) / jnp.sqrt(jnp.asarray(HD, dtype=x_bld.dtype))
        l = x_bld.shape[1]
        mask = (jnp.arange(l)[None, :] <= jnp.arange(l)[:, None])[None, None]
        neg_inf = jnp.finfo(attn.dtype).min
        attn = jax.nn.softmax(jnp.where(mask, attn, neg_inf), axis=-1)
        y_blhd = jnp.einsum('bhqk,bkhd->bqhd', attn, v_blhd)
        return jnp.einsum('bqhd,hdo->bqo', y_blhd, Wout)

    def _L1_ffn_ref(x, router_w0, wg0, wu0, wd0, router_w1, wg1, wu1, wd1):
        import jax, jax.numpy as jnp
        from jax import lax
        import numpy as np
        D_MODEL = 128
        HIDDEN = 64
        N_EXPERTS = 32
        TOP_K = 2
        B, S = (1, 512)

        def _moe_group(x2, router_w, wg, wu, wd, top_k):
            T = x2.shape[0]
            n_experts = router_w.shape[1]
            logits = x2 @ router_w
            scores = jax.nn.softmax(logits, axis=-1)
            expert_weights, expert_indices = lax.top_k(scores, top_k)
            flat_e = expert_indices.reshape(-1)
            flat_w = expert_weights.reshape(-1)
            flat_t = jnp.repeat(jnp.arange(T), top_k)
            order = jnp.argsort(flat_e)
            tok = flat_t[order]
            xs = x2[tok]
            group_sizes = jnp.bincount(flat_e, length=n_experts).astype(jnp.int32)
            gate = lax.ragged_dot(xs, wg, group_sizes)
            up = lax.ragged_dot(xs, wu, group_sizes)
            ys = lax.ragged_dot(jax.nn.silu(gate) * up, wd, group_sizes)
            ys = ys * flat_w[order][:, None]
            return jnp.zeros_like(x2).at[tok].add(ys)
        b, s, d = x.shape
        x2 = x.reshape(-1, d)
        out0 = _moe_group(x2, router_w0, wg0, wu0, wd0, TOP_K)
        out1 = _moe_group(x2, router_w1, wg1, wu1, wd1, TOP_K)
        out = (out0 * TOP_K + out1 * TOP_K) / (TOP_K + TOP_K)
        return out.reshape(b, s, d)

    def _L2_attn_ref(x, Wq, bq, Wk, bk, Wv, bv, Wo, bo):
        import jax, jax.numpy as jnp
        import numpy as np
        N_HEAD = 16
        ROPE_BASE = 10000.0

        def _rope(Y, d_param):
            b, h, t, dh = Y.shape
            mid = d_param // 2
            Y1 = Y[:, :mid]
            Y2 = Y[:, mid:]
            Ym1 = jnp.concatenate([Y1, Y2], axis=1)
            Ym2 = jnp.concatenate([-Y2, Y1], axis=1)
            j = jnp.arange(t, dtype=Y.dtype)[:, None]
            i = jnp.arange(dh // 2, dtype=Y.dtype)[None, :]
            theta = j * jnp.power(jnp.asarray(ROPE_BASE, Y.dtype), -2.0 * i / dh)
            cos = jnp.cos(theta)
            sin = jnp.sin(theta)
            theta1 = jnp.concatenate([cos, cos], axis=1)
            theta2 = jnp.concatenate([sin, sin], axis=1)
            return Ym1 * theta1 + Ym2 * theta2
        b, t, e = x.shape
        h = N_HEAD
        dh = e // h

        def proj(W, bias):
            y = jnp.einsum('bte,fe->btf', x, W) + bias
            return y.reshape(b, t, h, dh).transpose(0, 2, 1, 3)
        q = _rope(proj(Wq, bq), e)
        k = _rope(proj(Wk, bk), e)
        v = proj(Wv, bv)
        scale = jnp.sqrt(jnp.asarray(dh, x.dtype))
        att = jnp.einsum('bhqd,bhkd->bhqk', q, k) / scale
        causal = jnp.tril(jnp.ones((t, t), dtype=bool))
        att = jnp.where(causal[None, None], att, -jnp.inf)
        att = jax.nn.softmax(att, axis=-1)
        y = jnp.einsum('bhqk,bhkd->bhqd', att, v)
        y = y.transpose(0, 2, 1, 3).reshape(b, t, e)
        return jnp.einsum('bte,fe->btf', y, Wo) + bo

    def _L2_ffn_ref(hidden_states, router_w, expert_weights):
        import jax, jax.numpy as jnp
        import numpy as np
        K_TOP = 2
        B, S, H = hidden_states.shape
        x = hidden_states.reshape(-1, H)
        logits = x @ router_w.T
        probs = jax.nn.softmax(logits, axis=-1)
        topk_vals, topk_idx = jax.lax.top_k(probs, K_TOP)
        topk_w = topk_vals / (topk_vals.sum(-1, keepdims=True) + 1e-06)
        expert_out = jnp.einsum('nh,eho->eno', x, expert_weights)
        combined = jnp.take_along_axis(expert_out.transpose(1, 0, 2), topk_idx[:, :, None], axis=1)
        combined = combined.transpose(1, 0, 2)
        remap_bias = jnp.take_along_axis(probs, topk_idx, axis=1).T[:, :, None]
        weights = topk_w.T[:, :, None]
        out = ((combined + remap_bias) * weights).sum(axis=0)
        return out.reshape(B, S, H)

    def _L3_attn_ref(x, norm_w, in_proj_w, conv_w, conv_b, dt_bias, A_log, D_param, gate_w, out_proj_w):
        import jax, jax.numpy as jnp
        import numpy as np
        D_MODEL = 128
        D_STATE = 128
        D_CONV = 4
        EXPAND = 2
        HEADDIM = 64
        D_INNER = EXPAND * D_MODEL
        NHEADS = D_INNER // HEADDIM
        NGROUPS = 1
        CONV_DIM = D_INNER + 2 * NGROUPS * D_STATE
        D_IN_PROJ = 2 * D_INNER + 2 * NGROUPS * D_STATE + NHEADS
        EPS = 1e-05

        def rmsnorm(x, w):
            var = jnp.mean(jnp.square(x), axis=-1, keepdims=True)
            return x * jax.lax.rsqrt(var + EPS) * w

        def causal_dwconv(x, w, b):
            B, S, C = x.shape
            K = w.shape[1]
            xt = jnp.transpose(x, (0, 2, 1))
            xt = jnp.pad(xt, ((0, 0), (0, 0), (K - 1, 0)))
            out = jax.lax.conv_general_dilated(xt, w[:, None, :], window_strides=(1,), padding='VALID', feature_group_count=C)
            return jnp.transpose(out + b[:, None], (0, 2, 1))

        def ssd_scan(dt, xh, Bm, Cm, A):
            B, S, H = dt.shape
            P = xh.shape[-1]
            N = Bm.shape[-1]

            def step(h, inp):
                dt_t, x_t, B_t, C_t = inp
                decay = jnp.exp(dt_t * A)
                upd = dt_t[:, :, None, None] * x_t[:, :, :, None] * B_t[:, None, None, :]
                h = h * decay[:, :, None, None] + upd
                y_t = jnp.einsum('bhpn,bn->bhp', h, C_t)
                return (h, y_t)
            h0 = jnp.zeros((B, H, P, N), dtype=xh.dtype)
            xs = (jnp.moveaxis(dt, 1, 0), jnp.moveaxis(xh, 1, 0), jnp.moveaxis(Bm, 1, 0), jnp.moveaxis(Cm, 1, 0))
            _, ys = jax.lax.scan(step, h0, xs)
            return jnp.moveaxis(ys, 0, 1)
        B, S, _ = x.shape
        residual = x
        xn = rmsnorm(x, norm_w)
        zxbcdt = jnp.einsum('bsd,ed->bse', xn, in_proj_w)
        z = zxbcdt[..., :D_INNER]
        xBC = zxbcdt[..., D_INNER:D_INNER + CONV_DIM]
        dt_raw = zxbcdt[..., D_INNER + CONV_DIM:]
        xBC = jax.nn.silu(causal_dwconv(xBC, conv_w, conv_b))
        xh = xBC[..., :D_INNER].reshape(B, S, NHEADS, HEADDIM)
        Bm = xBC[..., D_INNER:D_INNER + D_STATE]
        Cm = xBC[..., D_INNER + D_STATE:]
        dt = jax.nn.softplus(dt_raw + dt_bias)
        A = -jnp.exp(A_log)
        y = ssd_scan(dt, xh, Bm, Cm, A)
        y = y + D_param[None, None, :, None] * xh
        y = y.reshape(B, S, D_INNER)
        y = y * jax.nn.silu(z)
        y = rmsnorm(y, gate_w)
        out = jnp.einsum('bsi,di->bsd', y, out_proj_w)
        return residual + out

    def _L3_ffn_ref(x, gamma1, Wq, bq, Wdown, bdown, Wup, bup, Wo, bo, gamma2, Wg, bg, We):
        import jax, jax.numpy as jnp
        import numpy as np
        D = 128
        H = 16
        HD = D // H
        L = 64
        E = 8
        B, T = (4, 256)
        EPS = 1e-06

        def _glorot(k, shape):
            fan_in, fan_out = (shape[-2], shape[-1])
            lim = np.sqrt(6.0 / (fan_in + fan_out)).astype(np.float32)
            return jax.random.uniform(k, shape, jnp.float32, -lim, lim)

        def _rmsnorm(x, gamma):
            return gamma * x * jax.lax.rsqrt(jnp.mean(x * x, axis=-1, keepdims=True) + EPS)
        b, t = (x.shape[0], x.shape[1])
        h = _rmsnorm(x, gamma1)
        q = (h @ Wq + bq).reshape(b, t, H, HD)
        kv = ((h @ Wdown + bdown) @ Wup + bup).reshape(b, t, H, 2 * HD)
        k, v = jnp.split(kv, 2, axis=-1)
        att = jnp.einsum('bthd,btgd->bthg', q, k) / np.sqrt(HD).astype(np.float32)
        att = jax.nn.softmax(att, axis=-1)
        out = jnp.einsum('bthg,btgd->bthd', att, v).reshape(b, t, D)
        x = x + (out @ Wo + bo)
        h2 = _rmsnorm(x, gamma2)
        gate = jax.nn.softmax(h2 @ Wg + bg, axis=-1)
        combined = jnp.einsum('btd,edf,bte->btf', h2, We, gate)
        return x + combined
    x = L0_attn_x
    x = x + _L0_attn_ref(_layernorm(x, axis=-1), L0_attn_qkv_w, L0_attn_qkv_b, L0_attn_out_w, L0_attn_out_b, L0_attn_norm1_w, L0_attn_norm2_w, L0_attn_mlp_w1, L0_attn_mlp_b1, L0_attn_mlp_w2, L0_attn_mlp_b2)
    x = x + _L0_ffn_ref(_layernorm(x, axis=-1), L0_ffn_W_r, L0_ffn_W_k, L0_ffn_W_v, L0_ffn_mu_r, L0_ffn_mu_k)
    x = x + _L1_attn_ref(_layernorm(x, axis=-1), L1_attn_Wq, L1_attn_Wkv_down, L1_attn_Wk_up, L1_attn_Wv_up, L1_attn_Wout)
    x = x + _L1_ffn_ref(_layernorm(x, axis=-1), L1_ffn_router_w0, L1_ffn_wg0, L1_ffn_wu0, L1_ffn_wd0, L1_ffn_router_w1, L1_ffn_wg1, L1_ffn_wu1, L1_ffn_wd1)
    x = x + _L2_attn_ref(_layernorm(x, axis=-1), L2_attn_Wq, L2_attn_bq, L2_attn_Wk, L2_attn_bk, L2_attn_Wv, L2_attn_bv, L2_attn_Wo, L2_attn_bo)
    x = x + _L2_ffn_ref(_layernorm(x, axis=-1), L2_ffn_router_w, L2_ffn_expert_weights)
    x = x + _L3_attn_ref(_layernorm(x, axis=-1), L3_attn_norm_w, L3_attn_in_proj_w, L3_attn_conv_w, L3_attn_conv_b, L3_attn_dt_bias, L3_attn_A_log, L3_attn_D_param, L3_attn_gate_w, L3_attn_out_proj_w)
    x = x + _L3_ffn_ref(_layernorm(x, axis=-1), L3_ffn_gamma1, L3_ffn_Wq, L3_ffn_bq, L3_ffn_Wdown, L3_ffn_bdown, L3_ffn_Wup, L3_ffn_bup, L3_ffn_Wo, L3_ffn_bo, L3_ffn_gamma2, L3_ffn_Wg, L3_ffn_bg, L3_ffn_We)
    return x

_drawn_inputs = setup_inputs


def setup_inputs(seed=0):
    import zlib

    import numpy as np

    out = dict(_drawn_inputs(seed))
    spreads = {'L0_attn_qkv_b': (0.0, 0.1),
     'L0_attn_out_b': (0.0, 0.1),
     'L0_attn_norm1_w': (1.0, 0.2),
     'L0_attn_norm2_w': (1.0, 0.2),
     'L0_attn_mlp_b1': (0.0, 0.1),
     'L0_attn_mlp_b2': (0.0, 0.1),
     'L3_attn_norm_w': (1.0, 0.2),
     'L3_attn_conv_b': (0.0, 0.1),
     'L3_attn_D_param': (1.0, 0.2),
     'L3_attn_gate_w': (1.0, 0.2),
     'L3_ffn_gamma1': (1.0, 0.6),
     'L3_ffn_bq': (0.0, 0.8),
     'L3_ffn_bdown': (0.0, 0.8),
     'L3_ffn_bup': (0.0, 0.593),
     'L3_ffn_bo': (0.0, 0.271),
     'L3_ffn_gamma2': (1.0, 0.2),
     'L3_ffn_bg': (0.0, 0.72)}
    factors = {'L0_ffn_W_r': 4.871,
     'L0_ffn_mu_r': 8.0,
     'L1_ffn_router_w0': 8.0,
     'L1_ffn_wg0': 8.0,
     'L1_ffn_wu0': 8.0,
     'L1_ffn_wd0': 8.0,
     'L1_ffn_router_w1': 8.0,
     'L1_ffn_wg1': 8.0,
     'L1_ffn_wu1': 8.0,
     'L1_ffn_wd1': 8.0,
     'L2_attn_bq': 46.955,
     'L2_attn_bk': 59.198,
     'L2_attn_bv': 8.0,
     'L2_attn_bo': 7.94}
    for name, (base, spread) in spreads.items():
        noise = np.random.default_rng([zlib.crc32(name.encode()), seed]).standard_normal(out[name].shape)
        drawn = base * np.exp(spread * noise) if base else spread * noise
        out[name] = jnp.asarray(drawn.astype(out[name].dtype))
    for name, factor in factors.items():
        out[name] = (out[name] * factor).astype(out[name].dtype)
    return out
```

```python
from contextlib import ExitStack

import numpy as np

import concourse.bass as bass
from concourse import mybir

ALU = mybir.AluOpType
ACT = mybir.ActivationFunctionType
AX = mybir.AxisListType.X
F32 = mybir.dt.float32
BF16 = mybir.dt.bfloat16
U32 = mybir.dt.uint32

SEQS, T, D = 16, 512, 128
P = 128
NT = T // P
PAIR = (0, 1)
H = 16
DH = D // H
HG = 4
LAT = 32
HD1 = 64
NE1, HID = 32, 64
NE2 = 8
DI, NH3, HP3, NS3 = 256, 4, 64, 128
NEG = -1e30
LAYERS = 8
PARTS = ((0, 4), (4, 8))


def program(nc, dram, x_in, out):
    with ExitStack() as ctx:
        def sb(name, shape, dt=F32):
            return ctx.enter_context(nc.sbuf_tensor(name, shape, dt))

        def pair_sb(name, shape, dt=F32):
            return [sb(f"{name}{q}", shape, dt) for q in PAIR]

        resident = [name for name in dram if name not in SETUP_ONLY]
        W = {name: sb("w_" + name, list(dram[name].shape), dram[name].dtype)[:] for name in resident}
        absorbed_q = sb("absorbed_q", [P, HG, P])
        absorbed_o = sb("absorbed_o", [P, HG, P])
        neg_a = sb("neg_a", [P, NH3])
        one_minus_mu = sb("one_minus_mu", [P, 2])
        minus_half = sb("minus_half", [P, NT])

        X = pair_sb("x", [P, NT, D])
        A = pair_sb("a", [P, NT, D])
        B = pair_sb("b", [P, NT, D])
        HR = pair_sb("hres", [P, NT, D])
        F = pair_sb("f", [P, 1 + T])
        VA = pair_sb("va", [P, NT, H, DH + 1])
        MV = pair_sb("mv", [P, NT, 2])
        BS = pair_sb("bs", [P, NT, 6])
        SSQ = pair_sb("ssq", [P, NT])
        RS = pair_sb("rs", [P, NT])
        VE = pair_sb("ve", [P, NT])
        arena = pair_sb("arena", [P, 7168])
        NMAX = [sb(f"nmax{i}", [P, HG]) for i in range(4)]
        PR = [sb(f"prob{i}", [P, T]) for i in range(3)]
        PT = [sb(f"probt{i}", [P, NT, P]) for i in range(3)]

        def cut(q, at, *shape):
            n = int(np.prod(shape))
            assert at + n <= 7168
            v = arena[q][:, at:at + n]
            names = " ".join("abc"[:len(shape)])
            kw = {k: s for k, s in zip("abc", shape)}
            return v.rearrange(f"p ({names}) -> p {names}", **kw) if len(shape) > 1 else v

        bank = [ctx.enter_context(nc.psum_tensor(f"bank{i}", [P, 512], F32)) for i in range(8)]

        def pb(q, b):
            return bank[4 * q + b][:]

        def pb3(q, b, n=4):
            return bank[4 * q + b][:].rearrange("p (t d) -> p t d", t=n)

        at = 0
        for name in SETUP_ONLY:
            n = int(np.prod(dram[name].shape[1:]))
            W[name] = cut(0, at, *dram[name].shape[1:])
            at += n

        pool_of_signals = []

        class Signals(dict):
            def __missing__(self, name):
                if len(self) == len(pool_of_signals):
                    pool_of_signals.append(ctx.enter_context(nc.semaphore(f"signal{len(self)}")))
                self[name] = pool_of_signals[len(self)]
                return self[name]

        setup = {name: ctx.enter_context(nc.semaphore(name)) for name in ("weights_loaded", "absorbed", "exp_a")}
        with nc.Block() as block:
            @block.sync
            def _(sp):
                for name, ap in dram.items():
                    sp.dma_start(W[name], ap).then_inc(setup["weights_loaded"], 16)
                sp.wait_ge(setup["weights_loaded"], 16 * len(dram))

            @block.gpsimd
            def _(pool):
                pool.memset(minus_half[:], -0.5)
                for q in PAIR:
                    pool.memset(VA[q][:], 1.0)
                    pool.memset(F[q][:], 0.0)

            @block.tensor
            def _(pe):
                pe.wait_ge(setup["weights_loaded"], 16 * len(dram))
                for h in range(H):
                    o, c = HD1 * (h % 2), h // 2
                    last = pe.matmul(bank[h % 2][:, (h // 2) * LAT:(h // 2 + 1) * LAT], W["l1_wq_t"][o:o + HD1, c],
                                     W["l1_wk_t"][o:o + HD1, c], start=True, stop=True)
                for h in range(H):
                    o, c, g, j = HD1 * (h % 2), h // 2, h // HG, h % HG
                    last = pe.matmul(bank[2 + h % 2][LAT * g:LAT * (g + 1), j * P:(j + 1) * P],
                                     W["l1_wv_t"][o:o + HD1, c], W["l1_wout"][o:o + HD1, c],
                                     start=True, stop=True)
                last.then_inc(setup["absorbed"], 1)

            @block.vector
            def _(dve):
                dve.wait_ge(setup["absorbed"], 1)
                aq = absorbed_q[:].rearrange("p g (k two c) -> p two (g k) c", k=2, two=2)
                for par in range(2):
                    dve.tensor_copy(aq[:, par], bank[par][:, 0:8 * LAT].rearrange("p (h c) -> p h c", c=LAT))
                for j in range(HG):
                    dve.tensor_copy(absorbed_o[:, j], bank[2 + j % 2][:, j * P:(j + 1) * P])
                dve.tensor_scalar(one_minus_mu[:], W["l0f_mu"], -1.0, 1.0, ALU.mult, ALU.add)
                dve.wait_ge(setup["exp_a"], 1)
                dve.tensor_scalar(neg_a[:], neg_a[:], -1.0, None, ALU.mult)

            @block.scalar
            def _(act):
                act.wait_ge(setup["weights_loaded"], 16 * len(dram))
                act.activation(neg_a[:], W["l3_alog"], ACT.Exp).then_inc(setup["exp_a"], 1)

        l0_qp = [cut(q, 0, HG, T) for q in PAIR]
        l0_kp = [cut(q, 2048, HG, T) for q in PAIR]
        l0_kcs = [cut(q, 4096, NT, 2, P) for q in PAIR]
        l0_qcs = [cut(q, 5120, 2, T) for q in PAIR]
        l0_st = [cut(q, 6144, 2, H * (DH + 1)) for q in PAIR]
        l0_tmp = [cut(q, 6432, 2, H * (DH + 1)) for q in PAIR]
        l0_rec = [cut(q, 6720, H) for q in PAIR]
        l0_gelu = [cut(q, 0, 4, T) for q in PAIR]
        at_q = [cut(q, 0, HG, T) for q in PAIR]
        at_k = [cut(q, 2048, HG, T) for q in PAIR]
        at_yt = [cut(q, 4096, HG, T) for q in PAIR]
        at_lv = [cut(q, 6144, 2 * NT, P) for q in PAIR]
        at_va = [cut(q, 4096, NT * H, 32) for q in PAIR]
        at_o = [[A[q][:].rearrange("p t d -> p (t d)"), B[q][:].rearrange("p t d -> p (t d)"),
                 HR[q][:].rearrange("p t d -> p (t d)"), cut(q, 6656, T)] for q in PAIR]
        at_rec = [cut(q, 2560, T) for q in PAIR]
        at_lt = [cut(q, 2048, T) for q in PAIR]
        mo_lg = [cut(q, 0, 8, NE1) for q in PAIR]
        mo_ex = [cut(q, 256, 8, NE1) for q in PAIR]
        mo_m8 = [cut(q, 512, 8, 8) for q in PAIR]
        mo_i8 = [cut(q, 576, 8, 8) for q in PAIR]
        mo_if = [cut(q, 640, 8, 8) for q in PAIR]
        mo_w = [cut(q, 704, 4, 8) for q in PAIR]
        mo_c = [cut(q, 736, 8, NE1) for q in PAIR]
        mo_t = [cut(q, 992, 8, NE1) for q in PAIR]
        mo_c3 = [cut(q, 1248, 8 * 48) for q in PAIR]
        mo_ct = [cut(q, 1632, 512) for q in PAIR]
        mo_acc = [cut(q, 2144, T) for q in PAIR]
        mo_silu = [cut(0, 2656 + T * i, T) for i in range(3)]
        mo_h = [cut(0, 4192 + T * i, T) for i in range(3)]
        mo_b = [cut(0, 5728 + T * i, T) for i in range(2)]
        mo_fb = [cut(q, 2656, 2, T) for q in PAIR]
        ma_xc = [cut(q, 0, 4, T) for q in PAIR]
        ma_xt = [cut(q, 2048, NT, DI) for q in PAIR]
        ma_bt = [cut(q, 3072, NT, P) for q in PAIR]
        ma_xd = [cut(q, 3584, NT, DI) for q in PAIR]
        XB = [cut(q, 2048, 4, 3 + T) for q in PAIR]
        ma_z = [cut(q, 4608, NT, DI) for q in PAIR]
        ma_y = [cut(q, 5632, NT, DI) for q in PAIR]
        ma_sm = [cut(q, 6656, 16, 16) for q in PAIR]
        ma_tmp = [cut(q, 6912, DI) for q in PAIR]
        ht_q = [cut(q, 0, NT, D) for q in PAIR]
        ht_pr = [cut(q, 512, 2048) for q in PAIR]
        ht_sc = [cut(q, 2560, NT, H, H) for q in PAIR]
        ht_o = [cut(q, 3584, NT, D) for q in PAIR]
        ht_sm = [cut(q, 4096, 2, NT * H) for q in PAIR]
        ht_dt = [cut(q, 4224, T) for q in PAIR]
        ht_v = [cut(q, 4736, NT, D) for q in PAIR]

        ident, ident_b = W["ident"], W["ident_b"]
        sg = Signals()
        fresh = {}

        LN = ("ln", 1e-5)
        norms_of_layer = [[LN, ("rms", 1e-6, D), ("rms", 1e-6, D)], [LN], [LN], [LN], [LN], [LN],
                          [LN, ("rms", 1e-5, D), ("rms", 1e-5, DI)], [LN, ("rms", 1e-6, D), ("rms", 1e-6, D)]]

        with nc.Fori(0, SEQS // 2) as pair:
            for first, last in PARTS:
                sg = Signals()
                with nc.Block(no_gpsimd_drain=True) as block:

                    @block.sync
                    def _(sp):
                        for q in PAIR if first == 0 else ():
                            src = x_in[bass.ds(pair, 1), q].rearrange("b (t p) d -> p (b t) d", p=P)
                            sp.dma_start(X[q][:], src).then_inc(sg[f"x_loaded{q}"], 16)
                        for q in PAIR if last == LAYERS else ():
                            dst = out[bass.ds(pair, 1), q].rearrange("b (t p) d -> p (b t) d", p=P)
                            sp.wait_ge(sg["layers_done"], q + 1)
                            sp.dma_start(dst, X[q][:]).then_inc(sg["x_stored"], 16)
                        if last == LAYERS:
                            sp.wait_ge(sg["x_stored"], 32)

                    @block.gpsimd
                    def _(pool):
                        n = 0
                        for kind in [k for layer in norms_of_layer[first:last] for k in layer]:
                            for q in PAIR:
                                pool.wait_ge(sg["stats_ready"], n + 1)
                                if kind[0] == "ln":
                                    pool.tensor_scalar(VE[q][:], MV[q][:, :, 1], 1.0, kind[1], ALU.mult,
                                                       ALU.add).then_inc(sg["var_eps"], 1)
                                else:
                                    pool.tensor_scalar(VE[q][:], SSQ[q][:], 1.0 / kind[2], kind[1], ALU.mult,
                                                       ALU.add).then_inc(sg["var_eps"], 1)
                                pool.wait_ge(sg["var_eps"], n + 1)
                                pool.tensor_tensor(RS[q][:], VE[q][:], minus_half[:],
                                                   ALU.pow).then_inc(sg["rstd_ready"], 1)
                                n += 1

                    @block.vector
                    def _(dve):
                        chain = [0]
                        norm = [0]
                        counts = {}

                        def done(ins):
                            chain[0] += 1
                            ins.then_inc(sg["dve_order"], 1)
                            dve.wait_ge(sg["dve_order"], chain[0])

                        def rstd():
                            norm[0] += 1
                            dve.wait_ge(sg["rstd_ready"], norm[0])

                        def layernorm_stats(q):
                            for t in range(NT):
                                i = dve.bn_stats(BS[q][:, t], X[q][:, t])
                            done(i)
                            for t in range(NT):
                                i = dve.bn_aggr(MV[q][:, t], BS[q][:, t])
                            i.then_inc(sg["stats_ready"], 1)

                        def layernorm_apply(q, ready):
                            rstd()
                            for t in range(NT):
                                i = dve.tensor_scalar(A[q][:, t], X[q][:, t], MV[q][:, t, 0:1], RS[q][:, t:t + 1],
                                                      ALU.subtract, ALU.mult)
                            if ready:
                                i.then_inc(sg[ready], 1)
                            else:
                                done(i)

                        def rms_stats(q, src, sq):
                            done(dve.tensor_tensor(sq, src, src, ALU.mult))
                            dve.tensor_reduce(SSQ[q][:], sq, AX, ALU.add).then_inc(sg["stats_ready"], 1)

                        def rms_apply(q, src, dst, ready):
                            rstd()
                            for t in range(NT):
                                i = dve.tensor_scalar(dst[:, t], src[:, t], RS[q][:, t:t + 1], None, ALU.mult)
                            i.then_inc(sg[ready], 1)

                        def attention(q, unit_of, tag, pairs, output):
                            units = unit_of
                            for n in range(len(units) + 3):
                                if n < len(units):
                                    i, heads = units[n]
                                    k = q * len(units) + n
                                    dve.wait_ge(sg[tag + "_scores"], k + 1)
                                    if k >= 4:
                                        dve.wait_ge(sg[tag + "_exp"], k - 3)
                                    s = bank[k % 3][:, 0:P * (i + 1) * len(heads)]
                                    dve.tensor_reduce(NMAX[k % 4][:, 0:len(heads)],
                                                      s.rearrange("p (h c) -> p h c", h=len(heads)), AX, ALU.max,
                                                      negate=True).then_inc(sg[tag + "_max"], 1)
                                if n >= 2 and n - 2 < len(units) and not on_act(n - 2):
                                    i, heads = units[n - 2]
                                    k = q * len(units) + n - 2
                                    dve.wait_ge(sg[tag + "_turned"], k + 1)
                                    if k >= 3:
                                        dve.wait_ge(sg[tag + "_av"], k - 2)
                                    w = P * (i + 1) * len(heads)
                                    dve.tensor_copy(PT[k % 3][:].rearrange("p t d -> p (t d)")[:, 0:w],
                                                    bank[3 + k % 3][:, 0:w]).then_inc(sg[tag + "_probt_dve"], 1)
                                if n >= 3 and (n - 2) % (PER_PAIR * pairs) == 0:
                                    k = q * len(units) + n - 3
                                    dve.wait_ge(sg[tag + "_av"], k + 1)
                                    output(q, (n - 3) // (PER_PAIR * pairs), bank[6 + k // (PER_PAIR * pairs) % 2])

                        def l0_attention():
                            for q in PAIR:
                                dve.wait_ge(sg[f"x_loaded{q}"], 16)
                                layernorm_stats(q)
                            for q in PAIR:
                                layernorm_apply(q, None)
                                rms_stats(q, A[q][:], B[q][:])
                            for q in PAIR:
                                rms_apply(q, A[q], B[q], "l0_b")
                            for q in PAIR:
                                for g in range(HG):
                                    dve.wait_ge(sg["l0_kp_mm"], q * HG + g + 1)
                                    dve.tensor_scalar(l0_kp[q][:, g], pb(q, 2 + g % 2), W["l0_bkp"][:, g:g + 1], 0.0,
                                                      ALU.add, ALU.max).then_inc(sg["l0_kp"], 1)
                            for q in PAIR:
                                for half in range(2):
                                    dve.wait_ge(sg["l0_kv_mm"], 2 * q + half + 1)
                                    kv = pb3(q, half, 2)
                                    for u in range(2):
                                        t = 2 * half + u
                                        dve.tensor_tensor(B[q][:, t], kv[:, u, 0:D], W["l0_bkv"][:, 0:D], ALU.add)
                                        i = dve.tensor_tensor(VA[q][:, t, :, 0:DH],
                                                              kv[:, u, D:2 * D].rearrange("p (h c) -> p h c", h=H),
                                                              W["l0_bkv"][:, D:2 * D].rearrange("p (h c) -> p h c", h=H),
                                                              ALU.add)
                                    done(i)
                                for t in range(NT):
                                    for s in range(2):
                                        i = dve.tensor_scalar(l0_kcs[q][:, t, s], B[q][:, t], 0.0,
                                                              W["l0_cs_tok"][:, s, t:t + 1], ALU.max, ALU.mult)
                                i.then_inc(sg["l0_kcs"], 1)
                                dve.wait_ge(sg["l0_q"], q + 1)
                                for s in range(2):
                                    i = dve.tensor_tensor(l0_qcs[q][:, s], F[q][:, 1:], W["l0_cs_feat"][:, s], ALU.mult)
                                i.then_inc(sg["l0_qcs"], 1)
                            n = 0
                            for c in range(NT):
                                for q in PAIR:
                                    for j in range(HG):
                                        k = n * HG + j
                                        dve.wait_ge(sg["l0_scores"], k + 1)
                                        if k >= 3:
                                            dve.wait_ge(sg["l0_av"], k - 2)
                                        dve.tensor_tensor(PT[k % 3][:], pb3(q, j % 2),
                                                          W["l0_mask"].unsqueeze(1).broadcast_to([P, HG, P]),
                                                          ALU.mult).then_inc(sg["l0_probt"], 1)
                                    dve.wait_ge(sg["l0_av"], HG * (n + 1))
                                    o = pb(q, 2)[:, 0:H * (DH + 1)].rearrange("p (h c) -> p h c", h=H)
                                    done(dve.tensor_scalar(l0_rec[q], o[:, :, DH], 1e-6, None, ALU.add))
                                    done(dve.reciprocal(l0_rec[q], l0_rec[q]))
                                    dve.tensor_tensor(B[q][:, c].rearrange("p (h c) -> p h c", h=H), o[:, :, 0:DH],
                                                      l0_rec[q].unsqueeze(2).broadcast_to([P, H, DH]),
                                                      ALU.mult).then_inc(sg["l0_ctx"], 1)
                                    if c < NT - 1:
                                        dve.wait_ge(sg["l0_state_mm"], n + 1)
                                        s_ps = pb(q, 3)[:, 0:2 * H * (DH + 1)].rearrange("p (s c) -> p s c", s=2)
                                        bd = W["l0_diag"].unsqueeze(1).broadcast_to([P, 2, H * (DH + 1)])
                                        if c == 0:
                                            dve.tensor_tensor(l0_st[q], s_ps, bd, ALU.mult).then_inc(sg["l0_state"], 1)
                                        else:
                                            done(dve.tensor_tensor(l0_tmp[q], s_ps, bd, ALU.mult))
                                            dve.tensor_tensor(l0_st[q], l0_st[q], l0_tmp[q],
                                                              ALU.add).then_inc(sg["l0_state"], 1)
                                    n += 1
                            for q in PAIR:
                                done(dve.tensor_tensor(HR[q][:], A[q][:],
                                                       W["l0_bo"].unsqueeze(1).broadcast_to([P, NT, D]), ALU.add))
                                dve.wait_ge(sg["l0_out_mm"], q + 1)
                                done(dve.tensor_tensor(HR[q][:], HR[q][:], pb3(q, 1), ALU.add))
                                rms_stats(q, HR[q][:], B[q][:])
                            for q in PAIR:
                                rms_apply(q, HR[q], B[q], "l0_b2")
                                done(dve.tensor_tensor(X[q][:], X[q][:], HR[q][:], ALU.add))
                                done(dve.tensor_tensor(X[q][:], X[q][:],
                                                       W["l0_b2"].unsqueeze(1).broadcast_to([P, NT, D]), ALU.add))
                            for q in PAIR:
                                dve.wait_ge(sg["l0_mlp_mm"], q + 1)
                                done(dve.tensor_tensor(X[q][:], X[q][:], pb3(q, 1), ALU.add))

                        def l0_channel_mix():
                            for q in PAIR:
                                layernorm_stats(q)
                            for q in PAIR:
                                layernorm_apply(q, "c_a")
                            for q in PAIR:
                                dve.wait_ge(sg["c_f"], q + 1)
                                for s in range(2):
                                    done(dve.tensor_scalar(l0_qcs[q][:, s], F[q][:, 0:T], one_minus_mu[:, s:s + 1], None,
                                                           ALU.mult))
                                    dve.scalar_tensor_tensor(l0_qcs[q][:, s], F[q][:, 1:], W["l0f_mu"][:, s:s + 1],
                                                             l0_qcs[q][:, s], ALU.mult, ALU.add).then_inc(sg["c_x"], 1)
                            for q in PAIR:
                                dve.wait_ge(sg["c_relu"], q + 1)
                                dve.tensor_tensor(l0_gelu[q][:, 0], l0_gelu[q][:, 0], l0_gelu[q][:, 0],
                                                  ALU.mult).then_inc(sg["c_k"], 1)
                            for q in PAIR:
                                dve.wait_ge(sg["c_tanh"], q + 1)
                                dve.wait_ge(sg["c_v_mm"], q + 1)
                                done(dve.scalar_tensor_tensor(B[q][:], B[q][:], 1.0, pb3(q, 1), ALU.add, ALU.mult))
                                done(dve.scalar_tensor_tensor(X[q][:], B[q][:], 0.5, X[q][:], ALU.mult, ALU.add))

                        def l1_attention():
                            for q in PAIR:
                                layernorm_stats(q)
                            for q in PAIR:
                                layernorm_apply(q, "l1_a")
                            for q in PAIR:
                                dve.wait_ge(sg["l1_lat_mm"], q + 1)
                                dve.tensor_copy(at_lt[q], pb(q, 2)).then_inc(sg["l1_lat"], 1)
                                done(dve.memset(at_lv[q], 0.0))
                                for s in range(2):
                                    c = slice(LAT * s, LAT * (s + 1))
                                    lv = at_lv[q].rearrange("p (s t) c -> p s t c", s=2)[:, s]
                                    dve.memset(lv[:, :, 64 + LAT * s:64 + LAT * (s + 1)], 1.0)
                                    i = dve.tensor_copy(lv[:, :, c], pb(q, 3)[:, 0:NT * LAT].rearrange(
                                        "p (t c) -> p t c", t=NT))
                                i.then_inc(sg["l1_lat"], 1)
                            for q in PAIR:
                                def output(q, p, o):
                                    done(dve.reciprocal(at_rec[q][0:64], o[64:128]))
                                    r = 64 * (p % 2)
                                    dve.tensor_tensor(at_yt[q][r:r + 64, p // 2], o[0:64], at_rec[q][0:64],
                                                      ALU.mult).then_inc(sg["l1_y"], 1)
                                    dve.wait_ge(sg["l1_y"], len(PAIRS) * q + p + 1)
                                attention(q, UNITS, "l1", 1, output)
                            for q in PAIR:
                                dve.wait_ge(sg["l1_out_mm"], q + 1)
                                done(dve.tensor_tensor(X[q][:], X[q][:], pb3(q, 2), ALU.add))

                        def top2(q, lg, n_e, groups, renorm):
                            m8, i8, idx, w = mo_m8[q], mo_i8[q].bitcast(U32), mo_if[q], mo_w[q]
                            for r in range(groups):
                                i = dve.max(m8[:, r], lg[:, r])
                            done(i)
                            for r in range(groups):
                                i = dve.max_index(i8[:, r], m8[:, r], lg[:, r])
                            done(i)
                            g = groups
                            ex = mo_ex[q][:, 0:g, 0:n_e]
                            dve.tensor_tensor(ex, lg, m8[:, 0:g, 0:1].broadcast_to([P, g, n_e]), ALU.subtract)
                            dve.tensor_tensor(w[:, 3, 0:g], m8[:, 0:g, 1], m8[:, 0:g, 0],
                                              ALU.subtract).then_inc(sg["top_shift"], 1)
                            done(dve.tensor_copy(idx[:, 0:g], i8[:, 0:g]))
                            counts["top"] = counts.get("top", 0) + 1
                            dve.wait_ge(sg["top_exp"], counts["top"])
                            done(dve.tensor_reduce(w[:, 0, 0:g], ex, AX, ALU.add))
                            done(dve.reciprocal(w[:, 0, 0:g], w[:, 0, 0:g]))
                            done(dve.tensor_tensor(w[:, 1, 0:g], w[:, 0, 0:g], w[:, 3, 0:g], ALU.mult))
                            return idx, w

                        def onehots(q, c, tmp, idx, w0, w1, n_e, g):
                            iota = W["iota"][:, 0:n_e].unsqueeze(1).broadcast_to([P, g, n_e])
                            dve.tensor_tensor(c, iota, idx[:, 0:g, 0:1].broadcast_to([P, g, n_e]), ALU.is_equal)
                            done(dve.tensor_tensor(tmp, iota, idx[:, 0:g, 1:2].broadcast_to([P, g, n_e]), ALU.is_equal))
                            dve.tensor_tensor(c, c, w0.unsqueeze(2).broadcast_to([P, g, n_e]), ALU.mult)
                            done(dve.tensor_tensor(tmp, tmp, w1.unsqueeze(2).broadcast_to([P, g, n_e]), ALU.mult))
                            done(dve.tensor_tensor(c, c, tmp, ALU.add))

                        def thirds(c, c3, ready):
                            done(dve.tensor_copy(c3[:, :, 0], c))
                            done(dve.tensor_tensor(c, c, c3[:, :, 0], ALU.subtract))
                            done(dve.tensor_copy(c3[:, :, 1], c))
                            done(dve.tensor_tensor(c, c, c3[:, :, 1], ALU.subtract))
                            dve.tensor_copy(c3[:, :, 2], c).then_inc(sg[ready], 1)

                        def l1_moe():
                            for q in PAIR:
                                layernorm_stats(q)
                            for q in PAIR:
                                layernorm_apply(q, "m_a")
                            for q in PAIR:
                                dve.wait_ge(sg["m_logits_mm"], q + 1)
                                done(dve.tensor_copy(mo_lg[q], pb(q, 1)[:, 0:8 * NE1].rearrange("p (g e) -> p g e", g=8)))
                                idx, w = top2(q, mo_lg[q], NE1, 8, False)
                                done(dve.tensor_scalar(w[:, 0:2], w[:, 0:2], 0.5, None, ALU.mult))
                                onehots(q, mo_c[q], mo_t[q], idx, w[:, 0], w[:, 1], NE1, 8)
                                thirds(mo_c[q], mo_c3[q].bitcast(BF16).rearrange("p (g s e) -> p g s e", s=3, e=NE1),
                                       "m_c3")
                            for q in PAIR:
                                for n in range(NE1):
                                    k = q * NE1 + n
                                    if k >= 3:
                                        dve.wait_ge(sg["m_down"], k - 2)
                                    dve.wait_ge(sg["m_silu"], k + 1)
                                    dve.wait_ge(sg["m_up"], k + 1)
                                    done(dve.tensor_tensor(mo_h[k % 3], mo_silu[k % 3], bank[2 + k % 2][:], ALU.mult))
                                    dve.wait_ge(sg["m_b"], k + 1)
                                    dve.tensor_tensor(mo_h[k % 3], mo_h[k % 3], bank[4 + k % 2][:],
                                                      ALU.mult).then_inc(sg["m_h"], 1)
                            for q in PAIR:
                                dve.wait_ge(sg["m_back_mm"], q + 1)
                                done(dve.tensor_tensor(X[q][:], X[q][:], pb3(q, 0), ALU.add))

                        def l2_attention():
                            for q in PAIR:
                                layernorm_stats(q)
                            for q in PAIR:
                                layernorm_apply(q, "l2_a")
                            for q in PAIR:
                                for g in range(HG):
                                    for s, (dst, bias, table) in enumerate(((at_q, "l2_bqp", "l2_rope_q"),
                                                                            (at_k, "l2_bkp", "l2_rope_k"))):
                                        dve.wait_ge(sg["l2_qk_mm"], 2 * (q * HG + g) + s + 1)
                                        dve.scalar_tensor_tensor(dst[q][:, g], pb(q, s), W[bias][:, g:g + 1], W[table],
                                                                 ALU.add, ALU.mult).then_inc(sg["l2_qk"], 1)
                                dve.wait_ge(sg["l2_v_mm"], q + 1)
                                done(dve.memset(at_va[q], 0.0))
                                dve.memset(at_va[q][:, :, DH:2 * DH], 1.0)
                                for t in range(NT):
                                    i = dve.tensor_tensor(at_va[q][:, H * t:H * (t + 1), 0:DH],
                                                          pb3(q, 2)[:, t].rearrange("p (h c) -> p h c", h=H),
                                                          W["l2_bv"].rearrange("p (h c) -> p h c", h=H), ALU.add)
                                i.then_inc(sg["l2_v"], 1)
                            for q in PAIR:
                                def output(q, j, o):
                                    dve.tensor_copy(at_o[q][j], o[:]).then_inc(sg["l2_y"], 1)
                                attention(q, UNITS, "l2", 2, output)
                            for q in PAIR:
                                for j in range(HG):
                                    dve.wait_ge(sg["l2_sums_mm"], q * HG + j + 1)
                                    done(dve.reciprocal(at_rec[q], pb(q, j % 2)))
                                    dve.tensor_tensor(at_o[q][j], at_o[q][j], at_rec[q],
                                                      ALU.mult).then_inc(sg["l2_yn"], 1)
                                    dve.wait_ge(sg["l2_yn"], HG * q + j + 1)
                            for q in PAIR:
                                done(dve.tensor_tensor(X[q][:], X[q][:],
                                                       W["l2_bo"].unsqueeze(1).broadcast_to([P, NT, D]), ALU.add))
                                dve.wait_ge(sg["l2_out_mm"], q + 1)
                                done(dve.tensor_tensor(X[q][:], X[q][:], pb3(q, 1), ALU.add))

                        def dense_moe(q, tag, c):
                            for e in range(NE2):
                                k = q * NE2 + e
                                dve.wait_ge(sg[tag + "_weights"], k + 1)
                                if e >= 2:
                                    dve.wait_ge(sg[tag + "_up"], k - 1)
                                dve.tensor_tensor(mo_fb[q][:, e % 2], F[q][:, 1:], pb(q, 1 + e % 2),
                                                  ALU.mult).then_inc(sg[tag + "_fb"], 1)

                        def l2_moe():
                            for q in PAIR:
                                layernorm_stats(q)
                            for q in PAIR:
                                layernorm_apply(q, "n_a")
                            for q in PAIR:
                                lg = mo_lg[q][:, 0:NT, 0:NE2]
                                dve.wait_ge(sg["n_logits_mm"], q + 1)
                                done(dve.tensor_copy(lg, pb(q, 1)[:, 0:NT * NE2].rearrange("p (t e) -> p t e", t=NT)))
                                idx, w = top2(q, lg, NE2, NT, True)
                                p0, p1, t2 = w[:, 0, 0:NT], w[:, 1, 0:NT], w[:, 2, 0:NT]
                                t3 = w[:, 3, 0:NT]
                                done(dve.tensor_tensor(t2, p0, p1, ALU.add))
                                done(dve.tensor_scalar(t2, t2, 1e-6, None, ALU.add))
                                done(dve.reciprocal(t2, t2))
                                w0, w1 = w[:, 0, 4:8], w[:, 1, 4:8]
                                dve.tensor_tensor(w0, p0, t2, ALU.mult)
                                done(dve.tensor_tensor(w1, p1, t2, ALU.mult))
                                dve.tensor_tensor(p0, p0, w0, ALU.mult)
                                done(dve.tensor_tensor(p1, p1, w1, ALU.mult))
                                done(dve.tensor_tensor(t3, p0, p1, ALU.add))
                                done(dve.tensor_tensor(X[q][:], X[q][:], t3.unsqueeze(2).broadcast_to([P, NT, D]),
                                                       ALU.add))
                                c = mo_c[q][:, 0:NT, 0:NE2]
                                onehots(q, c, mo_t[q][:, 0:NT, 0:NE2], idx, w0, w1, NE2, NT)
                                thirds(c, mo_c3[q][:, 0:NT * 12].bitcast(BF16).rearrange("p (g s e) -> p g s e", s=3, e=NE2),
                                       "n_c3")
                            for q in PAIR:
                                dense_moe(q, "n", None)
                            for q in PAIR:
                                dve.wait_ge(sg["n_up"], NE2 * (q + 1))
                                done(dve.tensor_tensor(X[q][:], X[q][:], pb3(q, 3), ALU.add))

                        def l3_mamba():
                            for q in PAIR:
                                layernorm_stats(q)
                                dve.memset(XB[q][:, :, 0:3], 0.0)
                            for q in PAIR:
                                layernorm_apply(q, None)
                                rms_stats(q, A[q][:], B[q][:])
                            for q in PAIR:
                                rms_apply(q, A[q], B[q], "l3_b")
                            for q in PAIR:
                                sm = ma_sm[q]
                                dtr, neg, dt = (sm[:, i].rearrange("p (t h) -> p t h", t=NT) for i in range(3))
                                dve.wait_ge(sg["l3_dt_mm"], q + 1)
                                done(dve.tensor_tensor(dtr, pb(q, 3)[:, 0:NT * NH3].rearrange("p (t h) -> p t h", t=NT),
                                                       W["l3_dtb"].unsqueeze(1).broadcast_to([P, NT, NH3]), ALU.add))
                                done(dve.tensor_scalar(neg, dtr, -1.0, None, ALU.mult))
                                dve.tensor_tensor(neg, neg, dtr, ALU.min).then_inc(sg["l3_absdt"], 1)
                            for q in PAIR:
                                for c in range(4):
                                    acc = ma_y[q].rearrange("p t d -> p (t d)")[:, T * (c % 2):T * (c % 2 + 1)]
                                    dve.wait_ge(sg["l3_xb"], 4 * q + c + 1)
                                    if c >= 2:
                                        dve.wait_ge(sg["l3_xc"], 4 * q + c - 1)
                                    done(dve.tensor_scalar(acc, XB[q][:, c, 0:T], W["l3_cw"][:, c, 0:1], None, ALU.mult))
                                    for k in range(1, 4):
                                        i = dve.scalar_tensor_tensor(acc, XB[q][:, c, k:k + T], W["l3_cw"][:, c, k:k + 1],
                                                                     acc, ALU.mult, ALU.add)
                                        if k < 3:
                                            done(i)
                                    i.then_inc(sg["l3_conv"], 1)
                            for q in PAIR:
                                sm = ma_sm[q]
                                dtr, neg, dt, da = (sm[:, i].rearrange("p (t h) -> p t h", t=NT) for i in range(4))
                                dve.wait_ge(sg["l3_ln"], q + 1)
                                done(dve.scalar_tensor_tensor(dt, dtr, 0.0, neg, ALU.max, ALU.add))
                                dve.tensor_tensor(da, dt, neg_a[:].unsqueeze(1).broadcast_to([P, NT, NH3]),
                                                  ALU.mult).then_inc(sg["l3_da"], 1)
                                dve.wait_ge(sg["l3_cum_mm"], q + 1)
                                dve.tensor_copy(sm[:, 4:6], pb(q, 3)[:, 16:48].rearrange("p (a b) -> p a b", a=2)
                                                ).then_inc(sg["l3_cum"], 1)
                                dve.wait_ge(sg["l3_cum"], q + 1)
                                dve.tensor_tensor(sm[:, 6], sm[:, 5], sm[:, 4], ALU.subtract).then_inc(sg["l3_dif"], 1)
                                for t in range(NT):
                                    dve.wait_ge(sg["l3_turn"], NT * q + t + 1)
                                    dve.tensor_copy(ma_xt[q][:, t], pb(q, t % 2)[:, 0:DI])
                                    dve.tensor_copy(ma_bt[q][:, t], pb(q, t % 2)[:, DI:DI + P]).then_inc(sg["l3_xt"], 1)
                                dve.wait_ge(sg["l3_xt"], NT * (q + 1))
                                for t in range(NT):
                                    xh = ma_xt[q][:, t].rearrange("p (h c) -> p h c", h=NH3)
                                    dve.tensor_tensor(ma_y[q][:, t], ma_xt[q][:, t], W["l3_d"], ALU.mult)
                                    dve.tensor_tensor(ma_xd[q][:, t].rearrange("p (h c) -> p h c", h=NH3), xh,
                                                      sm[:, 2, 4 * t:4 * t + 4].unsqueeze(2).broadcast_to([P, NH3, HP3]),
                                                      ALU.mult).then_inc(sg["l3_xd"], 1)
                                dve.wait_ge(sg["l3_xd"], NT * (q + 1))
                                dve.wait_ge(sg["l3_edec"], q + 1)
                                for t in range(NT):
                                    i = dve.tensor_tensor(ma_xt[q][:, t].rearrange("p (h c) -> p h c", h=NH3),
                                                          ma_xd[q][:, t].rearrange("p (h c) -> p h c", h=NH3),
                                                          sm[:, 9, 4 * t:4 * t + 4].unsqueeze(2).broadcast_to([P, NH3, HP3]),
                                                          ALU.mult)
                                i.then_inc(sg["l3_xw"], 1)
                            n = 0
                            for t in range(NT):
                                for q in PAIR:
                                    sm = ma_sm[q]
                                    dve.wait_ge(sg["l3_decay"], n + 1)
                                    dve.wait_ge(sg["l3_g_mm"], n + 1)
                                    dve.tensor_tensor(PT[q][:], PR[q][:].rearrange("p (h t) -> p h t", h=NH3),
                                                      pb(q, 1)[:, 0:P].unsqueeze(1).broadcast_to([P, NH3, P]),
                                                      ALU.mult).then_inc(sg["l3_w"], 1)
                                    if t > 0:
                                        ec = sm[:, 7, 4 * t:4 * t + 4].unsqueeze(2).broadcast_to([P, NH3, HP3])
                                        done(dve.tensor_tensor(ma_tmp[q].rearrange("p (h c) -> p h c", h=NH3),
                                                               pb(q, 1)[:, P:P + DI].rearrange("p (h c) -> p h c", h=NH3),
                                                               ec, ALU.mult))
                                        done(dve.tensor_tensor(ma_y[q][:, t], ma_y[q][:, t], ma_tmp[q], ALU.add))
                                    dve.wait_ge(sg["l3_intra"], n + 1)
                                    y = dve.tensor_tensor(ma_y[q][:, t], ma_y[q][:, t], pb(q, 2)[:, 0:DI], ALU.add)
                                    y.then_inc(sg["l3_yread"], 1)
                                    dve.wait_ge(sg["l3_yread"], n + 1)
                                    if t < NT - 1:
                                        dve.wait_ge(sg["l3_state_mm"], n + 1)
                                        st = HR[q][:].rearrange("p t d -> p (t d)")[:, 0:DI]
                                        s_ps = pb(q, 3)[:, 64:64 + DI]
                                        if t == 0:
                                            dve.tensor_copy(st, s_ps).then_inc(sg["l3_state"], 1)
                                        else:
                                            et = sm[:, 8, 4 * t:4 * t + 4].unsqueeze(2).broadcast_to([P, NH3, HP3])
                                            sth = st.rearrange("p (h c) -> p h c", h=NH3)
                                            done(dve.tensor_tensor(sth, sth, et, ALU.mult))
                                            dve.tensor_tensor(st, st, s_ps, ALU.add).then_inc(sg["l3_state"], 1)
                                    n += 1
                            for q in PAIR:
                                done(dve.tensor_tensor(ma_y[q], ma_y[q], ma_z[q], ALU.mult))
                                done(dve.tensor_tensor(ma_xd[q], ma_y[q], ma_y[q], ALU.mult))
                                dve.tensor_reduce(SSQ[q][:], ma_xd[q], AX, ALU.add).then_inc(sg["stats_ready"], 1)
                                done(dve.tensor_tensor(X[q][:], X[q][:], A[q][:], ALU.add))
                            for q in PAIR:
                                rms_apply(q, ma_y[q], ma_y[q], "l3_y")
                            for q in PAIR:
                                dve.wait_ge(sg["l3_out_mm"], q + 1)
                                done(dve.tensor_tensor(X[q][:], X[q][:], pb3(q, 2), ALU.add))

                        def l3_ffn():
                            for q in PAIR:
                                layernorm_stats(q)
                            for q in PAIR:
                                layernorm_apply(q, None)
                                rms_stats(q, A[q][:], B[q][:])
                            for q in PAIR:
                                rms_apply(q, A[q], B[q], "f_b")
                                done(dve.tensor_tensor(HR[q][:], A[q][:],
                                                       W["l3f_bo"].unsqueeze(1).broadcast_to([P, NT, D]), ALU.add))
                            for q in PAIR:
                                dve.wait_ge(sg["f_q_mm"], q + 1)
                                done(dve.tensor_tensor(ht_q[q], pb3(q, 1),
                                                       W["l3f_bq"].unsqueeze(1).broadcast_to([P, NT, D]), ALU.add))
                                for t in range(NT):
                                    dve.wait_ge(sg["f_kv_mm"], NT * q + 2 * (t // 2) + 2)
                                    pr = ht_pr[q].rearrange("p (h g d) -> p h g d", h=H, g=H)
                                    qb = ht_q[q][:, t].rearrange("p (h d) -> p h d", h=H).unsqueeze(2)
                                    kb = pb3(q, 2 + t // 2, 2)[:, t % 2, 0:D].rearrange("p (g d) -> p g d", g=H).unsqueeze(1)
                                    done(dve.tensor_tensor(pr, qb.broadcast_to([P, H, H, DH]), kb.broadcast_to([P, H, H, DH]),
                                                           ALU.mult))
                                    done(dve.tensor_reduce(ht_sc[q][:, t], pr, AX, ALU.add))
                                sc = ht_sc[q].rearrange("p t h g -> p (t h) g")
                                red = ht_sm[q][:, 0]
                                done(dve.tensor_reduce(red, sc, AX, ALU.max))
                                dve.tensor_tensor(sc, sc, red.unsqueeze(2).broadcast_to([P, NT * H, H]),
                                                  ALU.subtract).then_inc(sg["f_sc"], 1)
                            for q in PAIR:
                                sc = ht_sc[q].rearrange("p t h g -> p (t h) g")
                                red = ht_sm[q][:, 1]
                                dve.wait_ge(sg["f_exp"], q + 1)
                                done(dve.tensor_reduce(red, sc, AX, ALU.add))
                                done(dve.reciprocal(red, red))
                                for t in range(NT):
                                    pr = ht_pr[q].rearrange("p (h d g) -> p h d g", h=H, d=DH)
                                    ab = ht_sc[q][:, t].unsqueeze(2)
                                    vb = pb3(q, 2 + t // 2, 2)[:, t % 2, D:2 * D].rearrange("p (g d) -> p d g", g=H).unsqueeze(1)
                                    done(dve.tensor_tensor(pr, ab.broadcast_to([P, H, DH, H]), vb.broadcast_to([P, H, DH, H]),
                                                           ALU.mult))
                                    done(dve.tensor_reduce(ht_o[q][:, t].rearrange("p (h d) -> p h d", h=H), pr, AX, ALU.add))
                                o = ht_o[q].rearrange("p t (h d) -> p (t h) d", h=H)
                                dve.tensor_tensor(o, o, red.unsqueeze(2).broadcast_to([P, NT * H, DH]),
                                                  ALU.mult).then_inc(sg["f_o"], 1)
                            for q in PAIR:
                                dve.wait_ge(sg["f_out_mm"], q + 1)
                                done(dve.tensor_tensor(HR[q][:], HR[q][:], pb3(q, 1), ALU.add))
                                rms_stats(q, HR[q][:], B[q][:])
                                done(dve.tensor_tensor(X[q][:], X[q][:], HR[q][:], ALU.add))
                            for q in PAIR:
                                rms_apply(q, HR[q], B[q], "f_b2")
                            for q in PAIR:
                                lg = mo_lg[q][:, 0:NT, 0:NE2]
                                red = mo_w[q][:, 0, 0:NT]
                                dve.wait_ge(sg["f_gate_mm"], q + 1)
                                done(dve.tensor_tensor(lg, pb(q, 1)[:, 0:NT * NE2].rearrange("p (t e) -> p t e", t=NT),
                                                       W["l3f_bg"].unsqueeze(1).broadcast_to([P, NT, NE2]), ALU.add))
                                done(dve.tensor_reduce(red, lg, AX, ALU.max))
                                dve.tensor_tensor(lg, lg, red.unsqueeze(2).broadcast_to([P, NT, NE2]),
                                                  ALU.subtract).then_inc(sg["f_gate"], 1)
                                dve.wait_ge(sg["f_gexp"], q + 1)
                                done(dve.tensor_reduce(red, lg, AX, ALU.add))
                                done(dve.reciprocal(red, red))
                                done(dve.tensor_tensor(lg, lg, red.unsqueeze(2).broadcast_to([P, NT, NE2]), ALU.mult))
                                thirds(lg, mo_c3[q][:, 0:NT * 12].bitcast(BF16).rearrange("p (g s e) -> p g s e", s=3, e=NE2),
                                       "f_c3")
                            for q in PAIR:
                                dense_moe(q, "f", None)
                            for q in PAIR:
                                dve.wait_ge(sg["f_up"], NE2 * (q + 1))
                                done(dve.tensor_tensor(X[q][:], X[q][:], pb3(q, 3), ALU.add))

                        for layer in (l0_attention, l0_channel_mix, l1_attention, l1_moe, l2_attention, l2_moe,
                                      l3_mamba, l3_ffn)[first:last]:
                            layer()
                        if last == LAYERS:
                            dve.engine_nop().then_inc(sg["layers_done"], 2)

                    @block.scalar
                    def _(act):
                        top = [0]

                        def to_f(q, wait, n, ready, scale=1.0, b=0):
                            act.wait_ge(sg[wait], n)
                            act.activation(F[q][:, 1:], pb(q, b), ACT.Copy, scale=scale).then_inc(sg[ready], 1)

                        def attention_exp(q, units, tag):
                            for n in range(len(units) + 2):
                                if n < len(units):
                                    i, heads = units[n]
                                    k = q * len(units) + n
                                    act.wait_ge(sg[tag + "_max"], k + 1)
                                    if k >= 3:
                                        act.wait_ge(sg[tag + "_turned"], k - 2)
                                    w = P * (i + 1)
                                    for u, h in enumerate(heads):
                                        e = act.activation(PR[k % 3][:, u * w:(u + 1) * w], bank[k % 3][:, u * w:(u + 1) * w],
                                                           ACT.Exp, bias=NMAX[k % 4][:, u:u + 1])
                                    e.then_inc(sg[tag + "_exp"], 1)
                                if n >= 2 and on_act(n - 2):
                                    i, heads = units[n - 2]
                                    k = q * len(units) + n - 2
                                    act.wait_ge(sg[tag + "_turned"], k + 1)
                                    if k >= 3:
                                        act.wait_ge(sg[tag + "_av"], k - 2)
                                    w = P * (i + 1) * len(heads)
                                    act.activation(PT[k % 3][:].rearrange("p t d -> p (t d)")[:, 0:w],
                                                   bank[3 + k % 3][:, 0:w], ACT.Copy).then_inc(sg[tag + "_probt_act"], 1)

                        def top2_exp(q, ex, w):
                            top[0] += 1
                            act.wait_ge(sg["top_shift"], top[0])
                            act.activation(ex, ex, ACT.Exp)
                            act.activation(w, w, ACT.Exp).then_inc(sg["top_exp"], 1)

                        def l0_attention():
                            for q in PAIR:
                                to_f(q, "l0_turn", q + 1, "l0_f", W["l0_n1"][:, 0:1])
                            for q in PAIR:
                                for g in range(HG):
                                    act.wait_ge(sg["l0_qp_mm"], q * HG + g + 1)
                                    act.activation(l0_qp[q][:, g], pb(q, g % 2), ACT.Relu,
                                                   bias=W["l0_bqp"][:, g:g + 1]).then_inc(sg["l0_qp"], 1)
                            for q in PAIR:
                                act.wait_ge(sg["l0_q_mm"], q + 1)
                                act.activation(F[q][:, 1:], pb(q, 2), ACT.Relu, bias=W["l0_bq"][:, 0:1]
                                               ).then_inc(sg["l0_q"], 1)
                            for q in PAIR:
                                to_f(q, "l0_turn2", q + 1, "l0_f2")
                            for q in PAIR:
                                to_f(q, "l0_turn3", q + 1, "l0_f3", W["l0_n2"][:, 0:1])
                            for q in PAIR:
                                for m in range(4):
                                    act.wait_ge(sg["l0_up_mm"], 4 * q + m + 1)
                                    act.activation(l0_gelu[q][:, m], pb(q, 2 + m % 2), ACT.Gelu_apprx_tanh,
                                                   bias=W["l0_b1"][:, m:m + 1]).then_inc(sg["l0_gelu"], 1)

                        def l0_channel_mix():
                            for q in PAIR:
                                to_f(q, "c_turn", q + 1, "c_f")
                            for q in PAIR:
                                act.wait_ge(sg["c_k_mm"], q + 1)
                                act.activation(l0_gelu[q][:, 0], pb(q, 2), ACT.Relu).then_inc(sg["c_relu"], 1)
                            for q in PAIR:
                                act.wait_ge(sg["c_r_mm"], q + 1)
                                act.activation(B[q][:], pb3(q, 3), ACT.Tanh, scale=0.5).then_inc(sg["c_tanh"], 1)

                        def l1_attention():
                            for q in PAIR:
                                to_f(q, "l1_turn", q + 1, "l1_f")
                            for q in PAIR:
                                for g in range(HG):
                                    act.wait_ge(sg["l1_q_mm"], q * HG + g + 1)
                                    act.activation(at_q[q][:, g], pb(q, g % 2), ACT.Copy,
                                                   scale=HD1 ** -0.5).then_inc(sg["l1_q"], 1)
                            for q in PAIR:
                                attention_exp(q, UNITS, "l1")

                        def l1_moe():
                            for q in PAIR:
                                to_f(q, "m_turn", q + 1, "m_f")
                            for q in PAIR:
                                top2_exp(q, mo_ex[q], mo_w[q][:, 3])
                            for q in PAIR:
                                for g in range(2):
                                    act.wait_ge(sg["m_ct_mm"], 2 * q + g + 1)
                                    act.activation(mo_ct[q].bitcast(BF16)[0:96, g * T:(g + 1) * T],
                                                   pb(q, 2 + g).bitcast(BF16)[0:96, 0:T], ACT.Copy).then_inc(sg["m_ct"], 1)
                            for q in PAIR:
                                for n in range(NE1):
                                    k = q * NE1 + n
                                    act.wait_ge(sg["m_gate"], k + 1)
                                    if k >= 3:
                                        act.wait_ge(sg["m_h"], k - 2)
                                    act.activation(mo_silu[k % 3], bank[k % 2][:], ACT.Silu).then_inc(sg["m_silu"], 1)
                            for q in PAIR:
                                act.wait_ge(sg["m_down"], NE1 * (q + 1))
                                act.activation(mo_acc[q], bank[6 + q][:], ACT.Copy).then_inc(sg["m_acc"], 1)

                        def l2_attention():
                            for q in PAIR:
                                to_f(q, "l2_turn", q + 1, "l2_f", b=3)
                            for q in PAIR:
                                attention_exp(q, UNITS, "l2")

                        def small_ct(q, tag):
                            act.wait_ge(sg[tag + "_ct_mm"], q + 1)
                            act.activation(mo_ct[q].bitcast(BF16)[0:24, 0:T], pb(q, 2).bitcast(BF16)[0:24, 0:T],
                                           ACT.Copy).then_inc(sg[tag + "_ct"], 1)

                        def l2_moe():
                            for q in PAIR:
                                to_f(q, "n_turn", q + 1, "n_f")
                            for q in PAIR:
                                top2_exp(q, mo_ex[q][:, 0:NT, 0:NE2], mo_w[q][:, 3, 0:NT])
                            for q in PAIR:
                                small_ct(q, "n")

                        def l3_mamba():
                            for q in PAIR:
                                to_f(q, "l3_turn_b", q + 1, "l3_f", W["l3_nw"][:, 0:1])
                            for q in PAIR:
                                for c in range(4):
                                    act.wait_ge(sg["l3_xb_mm"], 4 * q + c + 1)
                                    act.activation(XB[q][:, c, 3:], pb(q, c % 2), ACT.Copy).then_inc(sg["l3_xb"], 1)
                            for q in PAIR:
                                act.wait_ge(sg["l3_absdt"], q + 1)
                                act.activation(ma_sm[q][:, 10], ma_sm[q][:, 1], ACT.Exp).then_inc(sg["l3_expdt"], 1)
                                act.wait_ge(sg["l3_expdt"], q + 1)
                                act.activation(ma_sm[q][:, 1], ma_sm[q][:, 10], ACT.Ln, bias=1.0).then_inc(sg["l3_ln"], 1)
                            for q in PAIR:
                                for half in range(2):
                                    act.wait_ge(sg["l3_z_mm"], 2 * q + half + 1)
                                    act.activation(ma_z[q][:, 2 * half:2 * half + 2], pb3(q, 2, 2),
                                                   ACT.Silu).then_inc(sg["l3_z"], 1)
                            for q in PAIR:
                                for c in range(4):
                                    acc = ma_y[q].rearrange("p t d -> p (t d)")[:, T * (c % 2):T * (c % 2 + 1)]
                                    act.wait_ge(sg["l3_conv"], 4 * q + c + 1)
                                    act.activation(ma_xc[q][:, c], acc, ACT.Silu,
                                                   bias=W["l3_cb"][:, c:c + 1]).then_inc(sg["l3_xc"], 1)
                            for q in PAIR:
                                sm = ma_sm[q]
                                act.wait_ge(sg["l3_cum"], q + 1)
                                act.activation(sm[:, 7:9], sm[:, 4:6], ACT.Exp)
                                act.wait_ge(sg["l3_dif"], q + 1)
                                act.activation(sm[:, 9], sm[:, 6], ACT.Exp).then_inc(sg["l3_edec"], 1)
                            n = 0
                            for t in range(NT):
                                for q in PAIR:
                                    act.wait_ge(sg["l3_decay_mm"], n + 1)
                                    if n >= 2:
                                        act.wait_ge(sg["l3_w"], n - 1)
                                    act.activation(PR[q][:], pb(q, 0), ACT.Exp).then_inc(sg["l3_decay"], 1)
                                    n += 1
                            for q in PAIR:
                                for c in range(2):
                                    act.wait_ge(sg["l3_yt_mm"], 2 * q + c + 1)
                                    act.activation(ma_xc[q][:, c], pb(q, c), ACT.Copy,
                                                   scale=W["l3_gw"][:, c:c + 1]).then_inc(sg["l3_yt"], 1)

                        def l3_ffn():
                            for q in PAIR:
                                to_f(q, "f_turn", q + 1, "f_f", W["l3f_g1"][:, 0:1])
                            for q in PAIR:
                                act.wait_ge(sg["f_down_mm"], q + 1)
                                act.activation(ht_dt[q][0:64], pb(q, 0)[0:64], ACT.Identity,
                                               bias=W["l3f_bd"][0:64, 0:1]).then_inc(sg["f_dt"], 1)
                            for q in PAIR:
                                act.wait_ge(sg["f_sc"], q + 1)
                                act.activation(ht_sc[q], ht_sc[q], ACT.Exp, scale=DH ** -0.5).then_inc(sg["f_exp"], 1)
                            for q in PAIR:
                                to_f(q, "f_turn2", q + 1, "f_f2")
                            for q in PAIR:
                                to_f(q, "f_turn3", q + 1, "f_f3", W["l3f_g2"][:, 0:1])
                            for q in PAIR:
                                act.wait_ge(sg["f_gate"], q + 1)
                                act.activation(mo_lg[q][:, 0:NT, 0:NE2], mo_lg[q][:, 0:NT, 0:NE2],
                                               ACT.Exp).then_inc(sg["f_gexp"], 1)
                            for q in PAIR:
                                small_ct(q, "f")

                        for layer in (l0_attention, l0_channel_mix, l1_attention, l1_moe, l2_attention, l2_moe,
                                      l3_mamba, l3_ffn)[first:last]:
                            layer()

                    @block.tensor
                    def _(pe):
                        def turn(q, src, wait, n, ready, b=0):
                            pe.wait_ge(sg[wait], n)
                            for t in range(NT):
                                i = pe.transpose(pb(q, b)[:, t * P:(t + 1) * P], src[:, t], ident)
                            i.then_inc(sg[ready], 1)

                        def tokens_by(q, b, w, width, at=0, k=P, last=True):
                            for t in range(NT):
                                i = pe.matmul(pb(q, b)[:, t * width:(t + 1) * width],
                                              F[q][:, 1 + t * P:1 + (t + 1) * P], w, start=True, stop=True)
                            return i

                        def probt_ready(tag, k):
                            n = sum(on_act(m % len(UNITS)) for m in range(k + 1))
                            if on_act(k % len(UNITS)):
                                pe.wait_ge(sg[tag + "_probt_act"], n)
                            else:
                                pe.wait_ge(sg[tag + "_probt_dve"], k + 1 - n)

                        def attention(q, units, tag, pairs, scores, values):
                            for n in range(len(units) + 3):
                                if n < len(units):
                                    i, heads = units[n]
                                    k = q * len(units) + n
                                    w = P * (i + 1)
                                    if k >= 3:
                                        pe.wait_ge(sg[tag + "_exp"], k - 2)
                                    for u, h in enumerate(heads):
                                        lhs, rhs = scores(q, i, h)
                                        pe.matmul(bank[k % 3][:, u * w:(u + 1) * w], lhs, rhs, start=(u == 0),
                                                  stop=False, skip_group_check=True)
                                    s = bank[k % 3][:, 0:w * len(heads)].rearrange("p (h c) -> p h c", h=len(heads))
                                    pe.matmul(s[:, :, P * i:], ident_b,
                                              W["mask_b"].unsqueeze(1).broadcast_to([P, len(heads), P]), start=False,
                                              stop=True, skip_group_check=True).then_inc(sg[tag + "_scores"], 1)
                                if n >= 2 and n - 2 < len(units):
                                    i, heads = units[n - 2]
                                    k = q * len(units) + n - 2
                                    pe.wait_ge(sg[tag + "_exp"], k + 1)
                                    if k >= 3:
                                        probt_ready(tag, k - 3)
                                    for m in range((i + 1) * len(heads)):
                                        ins = pe.transpose(bank[3 + k % 3][:, m * P:(m + 1) * P],
                                                           PR[k % 3][:, m * P:(m + 1) * P], ident)
                                    ins.then_inc(sg[tag + "_turned"], 1)
                                if n >= 3:
                                    i, heads = units[n - 3]
                                    k = q * len(units) + n - 3
                                    probt_ready(tag, k)
                                    done_groups = k // (PER_PAIR * pairs)
                                    if k % (PER_PAIR * pairs) == 0 and done_groups >= 2:
                                        pe.wait_ge(sg[tag + "_y"], done_groups - 1)
                                    for u, h in enumerate(heads):
                                        rows, start = values(q, 0, h)[1:]
                                        o = bank[6 + done_groups % 2][rows, P * i:P * (i + 1)]
                                        for m in range(i + 1):
                                            ins = pe.matmul(o, values(q, m, h)[0], PT[k % 3][:, u * (i + 1) + m],
                                                            start=(start and i == NT - 1 and m == 0), stop=(m == i),
                                                            skip_group_check=True)
                                    ins.then_inc(sg[tag + "_av"], 1)

                        def l0_attention():
                            for q in PAIR:
                                turn(q, B[q], "l0_b", q + 1, "l0_turn")
                            for q in PAIR:
                                pe.wait_ge(sg["l0_f"], q + 1)
                                for g in range(HG):
                                    if g >= 2:
                                        pe.wait_ge(sg["l0_qp"], q * HG + g - 1)
                                        pe.wait_ge(sg["l0_kp"], q * HG + g - 1)
                                    pe.matmul(pb(q, g % 2), W["l0_wqp"][:, g * P:(g + 1) * P], F[q][:, 1:], start=True,
                                              stop=True).then_inc(sg["l0_qp_mm"], 1)
                                    pe.matmul(pb(q, 2 + g % 2), W["l0_wkp"][:, g * P:(g + 1) * P], F[q][:, 1:], start=True,
                                              stop=True).then_inc(sg["l0_kp_mm"], 1)
                            for q in PAIR:
                                pe.wait_ge(sg["l0_qp"], HG * (q + 1))
                                for half in range(2):
                                    for u in range(2):
                                        t = 2 * half + u
                                        i = pe.matmul(pb(q, half)[:, u * 2 * D:(u + 1) * 2 * D],
                                                      F[q][:, 1 + t * P:1 + (t + 1) * P], W["l0_wqkv"][:, D:3 * D],
                                                      start=True, stop=True)
                                    i.then_inc(sg["l0_kv_mm"], 1)
                                pe.wait_ge(sg["l0_kp"], HG * (q + 1))
                                pe.matmul(pb(q, 2), W["l0_wqkv"][:, 0:D], F[q][:, 1:], start=True,
                                          stop=True).then_inc(sg["l0_q_mm"], 1)
                            n = 0
                            for c in range(NT):
                                tok = slice(c * P, (c + 1) * P)
                                for q in PAIR:
                                    if c == 0:
                                        pe.wait_ge(sg["l0_kcs"], q + 1)
                                        pe.wait_ge(sg["l0_q"], q + 1)
                                        pe.wait_ge(sg["l0_qcs"], q + 1)
                                    for j in range(HG):
                                        k = n * HG + j
                                        if j >= 2:
                                            pe.wait_ge(sg["l0_probt"], k - 1)
                                        elif c >= 1:
                                            pe.wait_ge(sg["l0_probt"], HG * (n - 1) - 2 + j + 1)
                                        rows = slice(32 * j, 32 * (j + 1))
                                        for g in range(HG):
                                            i = pe.matmul(pb(q, j % 2)[:, g * P:(g + 1) * P], l0_kp[q][rows, g, tok],
                                                          l0_qp[q][rows, g, tok], start=True, stop=True)
                                        i.then_inc(sg["l0_scores"], 1)
                                    if c < NT - 1:
                                        if c > 0:
                                            pe.wait_ge(sg["l0_state"], n - 1)
                                        for s in range(2):
                                            i = pe.matmul(pb(q, 3)[:, s * H * (DH + 1):(s + 1) * H * (DH + 1)],
                                                          l0_kcs[q][:, c, s], VA[q][:, c].rearrange("p h c -> p (h c)"),
                                                          start=True, stop=True)
                                        i.then_inc(sg["l0_state_mm"], 1)
                                    o = pb(q, 2)[:, 0:H * (DH + 1)]
                                    if c > 0:
                                        pe.wait_ge(sg["l0_ctx"], n - 1)
                                        pe.wait_ge(sg["l0_state"], n - 1)
                                        for s in range(2):
                                            pe.matmul(o, l0_qcs[q][:, s, tok], l0_st[q][:, s], start=(s == 0), stop=False,
                                                      skip_group_check=True)
                                    for j in range(HG):
                                        k = n * HG + j
                                        pe.wait_ge(sg["l0_probt"], k + 1)
                                        for g in range(HG):
                                            h = HG * g + j
                                            i = pe.matmul(o[:, h * (DH + 1):(h + 1) * (DH + 1)], PT[k % 3][:, g],
                                                          VA[q][:, c, h], start=(c == 0 and j == 0 and g == 0), stop=True,
                                                          skip_group_check=True)
                                        i.then_inc(sg["l0_av"], 1)
                                    n += 1
                            for q in PAIR:
                                pe.wait_ge(sg["l0_qcs"], q + 1)
                                turn(q, B[q], "l0_ctx", 2 * NT - 1 + q, "l0_turn2")
                            for q in PAIR:
                                pe.wait_ge(sg["l0_f2"], q + 1)
                                tokens_by(q, 1, W["l0_wo"], D).then_inc(sg["l0_out_mm"], 1)
                            for q in PAIR:
                                turn(q, B[q], "l0_b2", q + 1, "l0_turn3")
                            for q in PAIR:
                                pe.wait_ge(sg["l0_f3"], q + 1)
                                for m in range(4):
                                    if m >= 2:
                                        pe.wait_ge(sg["l0_gelu"], 4 * q + m - 1)
                                    pe.matmul(pb(q, 2 + m % 2), W["l0_w1"][:, m * P:(m + 1) * P], F[q][:, 1:], start=True,
                                              stop=True).then_inc(sg["l0_up_mm"], 1)
                            for q in PAIR:
                                pe.wait_ge(sg["l0_gelu"], 4 * (q + 1))
                                for t in range(NT):
                                    for m in range(4):
                                        i = pe.matmul(pb3(q, 1)[:, t], l0_gelu[q][:, m, t * P:(t + 1) * P],
                                                      W["l0_w2"][:, m], start=(m == 0), stop=(m == 3),
                                                      skip_group_check=True)
                                i.then_inc(sg["l0_mlp_mm"], 1)

                        def l0_channel_mix():
                            for q in PAIR:
                                turn(q, A[q], "c_a", q + 1, "c_turn")
                            for q in PAIR:
                                pe.wait_ge(sg["c_x"], 2 * q + 2)
                                pe.matmul(pb(q, 2), W["l0f_wk"], l0_qcs[q][:, 1], start=True,
                                          stop=True).then_inc(sg["c_k_mm"], 1)
                                for t in range(NT):
                                    i = pe.matmul(pb3(q, 3)[:, t], l0_qcs[q][:, 0, t * P:(t + 1) * P], W["l0f_wr"],
                                                  start=True, stop=True)
                                i.then_inc(sg["c_r_mm"], 1)
                            for q in PAIR:
                                pe.wait_ge(sg["c_k"], q + 1)
                                for t in range(NT):
                                    i = pe.matmul(pb3(q, 1)[:, t], l0_gelu[q][:, 0, t * P:(t + 1) * P], W["l0f_wv"],
                                                  start=True, stop=True)
                                i.then_inc(sg["c_v_mm"], 1)

                        def l1_attention():
                            for q in PAIR:
                                turn(q, A[q], "l1_a", q + 1, "l1_turn")
                            for q in PAIR:
                                pe.wait_ge(sg["l1_f"], q + 1)
                                pe.matmul(pb(q, 2), W["l1_wd4"], F[q][:, 1:], start=True, stop=True)
                                tokens_by(q, 3, W["l1_wd4"][:, 0:LAT], LAT).then_inc(sg["l1_lat_mm"], 1)
                                for g in range(HG):
                                    if g >= 2:
                                        pe.wait_ge(sg["l1_q"], q * HG + g - 1)
                                    pe.matmul(pb(q, g % 2), absorbed_q[:, g], F[q][:, 1:], start=True,
                                              stop=True).then_inc(sg["l1_q_mm"], 1)
                            pe.wait_ge(sg["l1_q"], 2 * HG)
                            pe.wait_ge(sg["l1_lat"], 4)
                            for q in PAIR:
                                def scores(q, i, h):
                                    rows = slice(32 * (h % HG), 32 * (h % HG + 1))
                                    return at_q[q][rows, h // HG, P * i:P * (i + 1)], at_lt[q][rows, 0:P * (i + 1)]
                                def values(q, m, h):
                                    s = h // HG % 2
                                    return at_lv[q][:, NT * s + m], slice(0, P), s == 0
                                attention(q, UNITS, "l1", 1, scores, values)
                            for q in PAIR:
                                pe.wait_ge(sg["l1_y"], len(PAIRS) * (q + 1))
                                pe.wait_ge(sg["l1_exp"], 2 * len(UNITS))
                                for t in range(NT):
                                    for c in range(HG):
                                        i = pe.matmul(pb3(q, 2)[:, t], at_yt[q][:, c, t * P:(t + 1) * P],
                                                      absorbed_o[:, c], start=(c == 0), stop=(c == HG - 1),
                                                      skip_group_check=True)
                                i.then_inc(sg["l1_out_mm"], 1)

                        def l1_moe():
                            for q in PAIR:
                                turn(q, A[q], "m_a", q + 1, "m_turn")
                            for q in PAIR:
                                pe.wait_ge(sg["m_f"], q + 1)
                                tokens_by(q, 1, W["mo_router"], 2 * NE1).then_inc(sg["m_logits_mm"], 1)
                            for q in PAIR:
                                pe.wait_ge(sg["m_c3"], q + 1)
                                c3 = mo_c3[q].bitcast(BF16).rearrange("p (g e) -> p g e", e=96)
                                for g in range(2):
                                    for t in range(NT):
                                        i = pe.transpose(pb(q, 2 + g).bitcast(BF16)[0:96, t * P:(t + 1) * P],
                                                         c3[:, 2 * t + g], ident_b)
                                    i.then_inc(sg["m_ct_mm"], 1)
                            pe.wait_ge(sg["m_ct"], 4)
                            for q in PAIR:
                                for n in range(NE1 + 2):
                                    if n < NE1:
                                        k = q * NE1 + n
                                        if k >= 2:
                                            pe.wait_ge(sg["m_silu"], k - 1)
                                        pe.matmul(bank[k % 2][:], W["mo_wg"][:, n * P:(n + 1) * P], F[q][:, 1:], start=True,
                                                  stop=True).then_inc(sg["m_gate"], 1)
                                        if k >= 2:
                                            pe.wait_ge(sg["m_h"], k - 1)
                                        pe.matmul(bank[2 + k % 2][:], W["mo_wu"][:, n * P:(n + 1) * P], F[q][:, 1:],
                                                  start=True, stop=True).then_inc(sg["m_up"], 1)
                                        g, p = n // (NE1 // 2), n % (NE1 // 2)
                                        pe.matmul(bank[4 + k % 2][:], W["sel32"][:, p * P:(p + 1) * P],
                                                  mo_ct[q].bitcast(BF16)[0:96, g * T:(g + 1) * T], start=True,
                                                  stop=True).then_inc(sg["m_b"], 1)
                                    if n >= 2:
                                        k = q * NE1 + n - 2
                                        pe.wait_ge(sg["m_h"], k + 1)
                                        pe.matmul(bank[6 + q][:], W["mo_wd"][:, (n - 2) * P:(n - 1) * P], mo_h[k % 3],
                                                  start=(n == 2), stop=(n == NE1 + 1),
                                                  skip_group_check=True).then_inc(sg["m_down"], 1)
                            for q in PAIR:
                                pe.wait_ge(sg["m_acc"], 2)
                                for t in range(NT):
                                    i = pe.transpose(pb3(q, 0)[:, t], mo_acc[q][:, t * P:(t + 1) * P], ident)
                                i.then_inc(sg["m_back_mm"], 1)

                        def l2_attention():
                            for q in PAIR:
                                turn(q, A[q], "l2_a", q + 1, "l2_turn", b=3)
                            for q in PAIR:
                                pe.wait_ge(sg["l2_f"], q + 1)
                                for g in range(HG):
                                    for s, w in enumerate(("l2_wqp", "l2_wkp")):
                                        if g >= 1:
                                            pe.wait_ge(sg["l2_qk"], 2 * (q * HG + g - 1) + s + 1)
                                        pe.matmul(pb(q, s), W[w][:, g * P:(g + 1) * P], F[q][:, 1:], start=True,
                                                  stop=True).then_inc(sg["l2_qk_mm"], 1)
                                tokens_by(q, 2, W["l2_wv"], D).then_inc(sg["l2_v_mm"], 1)
                            pe.wait_ge(sg["l2_v"], 2)
                            for q in PAIR:
                                def scores(q, i, h):
                                    rows = slice(32 * (h % HG), 32 * (h % HG + 1))
                                    return (at_q[q][rows, h // HG, P * i:P * (i + 1)],
                                            at_k[q][rows, h // HG, 0:P * (i + 1)])
                                def values(q, m, h):
                                    g = h // HG
                                    return at_va[q][:, H * m + h], slice(32 * g, 32 * (g + 1)), True
                                attention(q, UNITS, "l2", 2, scores, values)
                            for q in PAIR:
                                pe.wait_ge(sg["l2_y"], 2 * HG)
                                pe.wait_ge(sg["l2_exp"], 2 * len(UNITS))
                                probt_ready("l2", 2 * len(UNITS) - 1)
                                for j in range(HG):
                                    if j >= 2:
                                        pe.wait_ge(sg["l2_yn"], q * HG + j - 1)
                                    pe.matmul(pb(q, j % 2), W["sel_sums"], at_o[q][j], start=True,
                                              stop=True).then_inc(sg["l2_sums_mm"], 1)
                            for q in PAIR:
                                pe.wait_ge(sg["l2_yn"], HG * (q + 1))
                                for t in range(NT):
                                    for j in range(HG):
                                        i = pe.matmul(pb3(q, 1)[:, t], at_o[q][j][:, t * P:(t + 1) * P],
                                                      W["l2_wo4"][:, j], start=(j == 0), stop=(j == HG - 1),
                                                      skip_group_check=True)
                                i.then_inc(sg["l2_out_mm"], 1)

                        def gated_experts(q, tag, weights):
                            acc = pb3(q, 3)
                            for e in range(NE2 + 1):
                                if e < NE2:
                                    k = q * NE2 + e
                                    if e >= 2:
                                        pe.wait_ge(sg[tag + "_fb"], k - 1)
                                    pe.matmul(pb(q, 1 + e % 2), W["sel8"][:, e * P:(e + 1) * P],
                                              mo_ct[q].bitcast(BF16)[0:24, 0:T], start=True,
                                              stop=True).then_inc(sg[tag + "_weights"], 1)
                                if e >= 1:
                                    k = q * NE2 + e - 1
                                    pe.wait_ge(sg[tag + "_fb"], k + 1)
                                    for t in range(NT):
                                        i = pe.matmul(acc[:, t], mo_fb[q][:, (e - 1) % 2, t * P:(t + 1) * P],
                                                      weights[:, (e - 1) * P:e * P], start=(e == 1 and t == 0),
                                                      stop=(e == NE2), skip_group_check=True)
                                    i.then_inc(sg[tag + "_up"], 1)

                        def small_turn(q, tag):
                            pe.wait_ge(sg[tag + "_c3"], q + 1)
                            c3 = mo_c3[q][:, 0:NT * 12].bitcast(BF16).rearrange("p (g e) -> p g e", e=24)
                            for t in range(NT):
                                i = pe.transpose(pb(q, 2).bitcast(BF16)[0:24, t * P:(t + 1) * P], c3[:, t], ident_b)
                            i.then_inc(sg[tag + "_ct_mm"], 1)

                        def l2_moe():
                            for q in PAIR:
                                turn(q, A[q], "n_a", q + 1, "n_turn")
                            for q in PAIR:
                                pe.wait_ge(sg["n_f"], q + 1)
                                tokens_by(q, 1, W["l2f_router"], NE2).then_inc(sg["n_logits_mm"], 1)
                            for q in PAIR:
                                small_turn(q, "n")
                            for q in PAIR:
                                pe.wait_ge(sg["n_ct"], q + 1)
                                gated_experts(q, "n", W["l2f_we"])

                        def l3_mamba():
                            for q in PAIR:
                                turn(q, B[q], "l3_b", q + 1, "l3_turn_b")
                            for q in PAIR:
                                pe.wait_ge(sg["l3_f"], q + 1)
                                tokens_by(q, 3, W["l3_win"][:, 768:772], NH3).then_inc(sg["l3_dt_mm"], 1)
                                for c in range(4):
                                    if c >= 2:
                                        pe.wait_ge(sg["l3_xb"], 4 * q + c - 1)
                                    pe.matmul(pb(q, c % 2), W["l3_win"][:, DI + c * P:DI + (c + 1) * P], F[q][:, 1:],
                                              start=True, stop=True).then_inc(sg["l3_xb_mm"], 1)
                            for q in PAIR:
                                for half in range(2):
                                    if half:
                                        pe.wait_ge(sg["l3_z"], 2 * q + 1)
                                    for u in range(2):
                                        t = 2 * half + u
                                        i = pe.matmul(pb(q, 2)[:, u * DI:(u + 1) * DI], F[q][:, 1 + t * P:1 + (t + 1) * P],
                                                      W["l3_win"][:, 0:DI], start=True, stop=True)
                                    i.then_inc(sg["l3_z_mm"], 1)
                            for q in PAIR:
                                pe.wait_ge(sg["l3_da"], q + 1)
                                da = ma_sm[q][:, 3]
                                pe.matmul(pb(q, 3)[:, 16:32], W["tri"], da, start=True, stop=True)
                                pe.matmul(pb(q, 3)[:, 32:48], W["ones"], da, start=True, stop=True
                                          ).then_inc(sg["l3_cum_mm"], 1)
                                pe.wait_ge(sg["l3_xb"], 4 * (q + 1))
                                pe.wait_ge(sg["l3_xc"], 4 * q + 3)
                                for t in range(NT):
                                    if t >= 2:
                                        pe.wait_ge(sg["l3_xt"], NT * q + t - 1)
                                    for c in range(3):
                                        i = pe.transpose(pb(q, t % 2)[:, c * P:(c + 1) * P],
                                                         ma_xc[q][:, c, t * P:(t + 1) * P], ident)
                                    i.then_inc(sg["l3_turn"], 1)
                            n = 0
                            for t in range(NT):
                                tok = slice(t * P, (t + 1) * P)
                                for q in PAIR:
                                    sm = ma_sm[q]
                                    if t == 0:
                                        pe.wait_ge(sg["l3_xt"], NT * (q + 1))
                                    else:
                                        pe.wait_ge(sg["l3_decay"], n - 1)
                                    for h in range(NH3):
                                        pe.matmul(pb3(q, 0)[:, h],
                                                  sm[:, 3, NH3 * t + h:NH3 * t + h + 1].broadcast_to([P, P]), W["tri"],
                                                  start=(h == 0), stop=False, skip_group_check=True)
                                    pe.matmul(pb(q, 0), W["neg_tri"],
                                              sm[:, 3, NH3 * t:NH3 * (t + 1)].unsqueeze(2).broadcast_to([P, NH3, P]),
                                              start=False, stop=False, skip_group_check=True)
                                    pe.matmul(pb(q, 0), ident_b, W["mask_tb"].unsqueeze(1).broadcast_to([P, NH3, P]),
                                              start=False, stop=True,
                                              skip_group_check=True).then_inc(sg["l3_decay_mm"], 1)
                                    if t == 0:
                                        pe.wait_ge(sg["l3_xc"], 4 * (q + 1))
                                    else:
                                        pe.wait_ge(sg["l3_w"], n - 1)
                                        pe.wait_ge(sg["l3_yread"], n - 1)
                                    i = pe.matmul(pb(q, 1)[:, 0:P], ma_xc[q][:, 2, tok], ma_xc[q][:, 3, tok],
                                                  start=True, stop=True)
                                    st = HR[q][:].rearrange("p t d -> p (t d)")[:, 0:DI]
                                    if t == 0:
                                        pe.wait_ge(sg["l3_z"], 2 * (q + 1))
                                        pe.wait_ge(sg["l3_xw"], q + 1)
                                    else:
                                        pe.wait_ge(sg["l3_state"], n - 1)
                                        i = pe.matmul(pb(q, 1)[:, P:P + DI], ma_xc[q][:, 3, tok], st, start=True,
                                                      stop=True)
                                    i.then_inc(sg["l3_g_mm"], 1)
                                    if t < NT - 1:
                                        pe.matmul(pb(q, 3)[:, 64:64 + DI], ma_bt[q][:, t], ma_xt[q][:, t], start=True,
                                                  stop=True).then_inc(sg["l3_state_mm"], 1)
                                    pe.wait_ge(sg["l3_w"], n + 1)
                                    for h in range(NH3):
                                        i = pe.matmul(pb(q, 2)[:, h * HP3:(h + 1) * HP3], PT[q][:, h],
                                                      ma_xd[q][:, t, h * HP3:(h + 1) * HP3], start=True, stop=True)
                                    i.then_inc(sg["l3_intra"], 1)
                                    n += 1
                            for q in PAIR:
                                pe.wait_ge(sg["l3_y"], q + 1)
                                for c in range(2):
                                    for t in range(NT):
                                        i = pe.transpose(pb3(q, c)[:, t], ma_y[q][:, t, c * P:(c + 1) * P], ident)
                                    i.then_inc(sg["l3_yt_mm"], 1)
                            for q in PAIR:
                                pe.wait_ge(sg["l3_yt"], 2 * (q + 1))
                                for t in range(NT):
                                    for c in range(2):
                                        i = pe.matmul(pb3(q, 2)[:, t], ma_xc[q][:, c, t * P:(t + 1) * P], W["l3_wout"][:, c],
                                                      start=(c == 0), stop=(c == 1), skip_group_check=True)
                                i.then_inc(sg["l3_out_mm"], 1)

                        def l3_ffn():
                            for q in PAIR:
                                turn(q, B[q], "f_b", q + 1, "f_turn")
                            for q in PAIR:
                                pe.wait_ge(sg["f_f"], q + 1)
                                pe.matmul(pb(q, 0)[0:64], W["l3f_wd"], F[q][:, 1:], start=True,
                                          stop=True).then_inc(sg["f_down_mm"], 1)
                                tokens_by(q, 1, W["l3f_wq"], D).then_inc(sg["f_q_mm"], 1)
                                pe.wait_ge(sg["f_dt"], q + 1)
                                for t in range(NT):
                                    o = pb3(q, 2 + t // 2, 2)[:, t % 2]
                                    pe.matmul(o, ht_dt[q][0:64, t * P:(t + 1) * P], W["l3f_wup"], start=True, stop=False,
                                              skip_group_check=True)
                                    pe.matmul(o, W["ones"][0:1, :], W["l3f_bup"], start=False, stop=True,
                                              skip_group_check=True).then_inc(sg["f_kv_mm"], 1)
                            for q in PAIR:
                                turn(q, ht_o[q], "f_o", q + 1, "f_turn2")
                            for q in PAIR:
                                pe.wait_ge(sg["f_f2"], q + 1)
                                tokens_by(q, 1, W["l3f_wo"], D).then_inc(sg["f_out_mm"], 1)
                            for q in PAIR:
                                turn(q, B[q], "f_b2", q + 1, "f_turn3")
                            for q in PAIR:
                                pe.wait_ge(sg["f_f3"], q + 1)
                                tokens_by(q, 1, W["l3f_wg"], NE2).then_inc(sg["f_gate_mm"], 1)
                            for q in PAIR:
                                small_turn(q, "f")
                            for q in PAIR:
                                pe.wait_ge(sg["f_ct"], q + 1)
                                gated_experts(q, "f", W["l3f_we"])

                        for layer in (l0_attention, l0_channel_mix, l1_attention, l1_moe, l2_attention, l2_moe,
                                      l3_mamba, l3_ffn)[first:last]:
                            layer()

                numbers = sorted(s.num for s in pool_of_signals)
                assert numbers == list(range(numbers[0], numbers[-1] + 1)), numbers
                nc.vector.sem_clear(range(numbers[0], numbers[-1] + 1))
                nc.all_engine_barrier()


PAIRS = [(HG * g0 + j, HG * (g0 + 1) + j) for j in range(HG) for g0 in (0, 2)]
UNITS = [u for a, b in PAIRS for u in ((3, [a]), (3, [b]), (2, [a]), (2, [b]), (1, [a, b]), (0, [a, b]))]
PER_PAIR = len(UNITS) // len(PAIRS)
SETUP_ONLY = ("l1_wq_t", "l1_wk_t", "l1_wv_t", "l1_wout")


def on_act(n):
    return UNITS[n][0] == 2


def tables():
    f4 = np.float32
    bf = mybir.dt.np(BF16)
    pos = np.arange(T, dtype=np.float64)
    cs = np.stack([np.cos(np.pi / 2 * pos / T), np.sin(np.pi / 2 * pos / T)])
    c = {"ident": np.eye(P, dtype=f4), "ident_b": np.eye(P).astype(bf)}
    c["l0_cs_tok"] = cs.reshape(2, NT, P).transpose(2, 0, 1).astype(f4)
    c["l0_cs_feat"] = np.broadcast_to(cs, (P, 2, T)).astype(f4)
    i = np.arange(P)
    lag = i[None, :] - i[:, None]
    c["l0_mask"] = np.where(lag >= 0, np.cos(np.pi / 2 * lag / T), 0).astype(f4)
    c["l0_diag"] = (i[:, None] // DH == np.arange(H * (DH + 1))[None, :] // (DH + 1)).astype(f4)
    c["mask_b"] = np.where(i[None, :] > i[:, None], NEG, 0).astype(bf)
    c["mask_tb"] = np.where(i[None, :] < i[:, None], NEG, 0).astype(bf)
    c["tri"] = (i[:, None] <= i[None, :]).astype(f4)
    c["neg_tri"] = -c["tri"]
    c["ones"] = np.ones((P, P), f4)
    sums = np.zeros((P, P), f4)
    for m in range(P):
        sums[32 * (m // 32) + DH, m] = 1
    c["sel_sums"] = sums
    c["iota"] = np.broadcast_to(np.arange(NE1), (P, NE1)).astype(f4)
    theta = (np.arange(T, dtype=f4)[:, None] * np.power(f4(10000.0), f4(-2.0) * np.arange(DH // 2, dtype=f4) / f4(DH)))
    rope = (np.cos(theta.astype(np.float64)) + np.sin(theta.astype(np.float64)))
    rows = np.zeros((P, T))
    for j in range(HG):
        for d in range(DH):
            rows[32 * j + d] = rope[:, d % (DH // 2)]
    c["l2_rope_k"] = rows.astype(f4)
    c["l2_rope_q"] = (rows / np.sqrt(DH)).astype(f4)
    sel32 = np.zeros((3, NE1, NE1 // 2, P))
    for p in range(NE1 // 2):
        for m in range(P):
            sel32[:, 2 * p + m // HID, p, m] = 1
    c["sel32"] = sel32.reshape(96, -1).astype(bf)
    sel8 = np.zeros((3, NE2, NE2, P))
    for e in range(NE2):
        sel8[:, e, e] = 1
    c["sel8"] = sel8.reshape(24, -1).astype(bf)
    return c


def kernel(**inputs):
    import concourse.bacc as bacc
    from concourse.bass_utils import run_bass_kernel_spmd as run

    g = {k: np.asarray(v) for k, v in inputs.items()}

    def padded(w):
        o = np.zeros((w.shape[0], HG, HG, 32), w.dtype)
        o[..., :DH] = w.reshape(w.shape[0], HG, HG, DH)
        return o.reshape(w.shape[0], HG * P)

    def rows(v):
        return np.broadcast_to(v.reshape(1, -1), (P, v.size))

    def col(v):
        return v.reshape(-1, P).T

    a = dict(tables())
    w = g["L0_attn_qkv_w"]
    b = g["L0_attn_qkv_b"]
    a["l0_wqkv"] = w
    a["l0_wqp"], a["l0_wkp"] = padded(w[:, 0:D]), padded(w[:, D:2 * D])
    a["l0_bqp"], a["l0_bkp"] = (col(padded(b[None, s * D:(s + 1) * D])) for s in range(2))
    a["l0_bq"] = col(b[0:D])
    a["l0_bkv"] = rows(b[D:])
    a["l0_wo"], a["l0_bo"] = g["L0_attn_out_w"], rows(g["L0_attn_out_b"])
    a["l0_n1"], a["l0_n2"] = col(g["L0_attn_norm1_w"]), col(g["L0_attn_norm2_w"])
    a["l0_w1"], a["l0_b1"] = g["L0_attn_mlp_w1"], col(g["L0_attn_mlp_b1"])
    a["l0_w2"] = g["L0_attn_mlp_w2"].reshape(4, P, D).transpose(1, 0, 2)
    a["l0_b2"] = rows(g["L0_attn_mlp_b2"])
    a["l0f_wr"], a["l0f_wk"], a["l0f_wv"] = (g["L0_ffn_W_" + s].T for s in "rkv")
    a["l0f_mu"] = np.stack([g["L0_ffn_mu_r"], g["L0_ffn_mu_k"]], 1)
    a["l1_wq_t"] = g["L1_attn_Wq"].transpose(1, 2, 0).reshape(H // 2, P, D).transpose(1, 0, 2)
    a["l1_wk_t"] = g["L1_attn_Wk_up"].transpose(1, 2, 0).reshape(H // 2, P, LAT).transpose(1, 0, 2)
    a["l1_wv_t"] = g["L1_attn_Wv_up"].transpose(1, 2, 0).reshape(H // 2, P, LAT).transpose(1, 0, 2)
    a["l1_wout"] = g["L1_attn_Wout"].reshape(H // 2, P, D).transpose(1, 0, 2)
    a["l1_wd4"] = np.tile(g["L1_attn_Wkv_down"], (1, 4))
    a["mo_router"] = np.concatenate([g["L1_ffn_router_w0"], g["L1_ffn_router_w1"]], 1)
    for s in "gu":
        a["mo_w" + s] = np.concatenate([g[f"L1_ffn_w{s}{i}"].transpose(1, 0, 2).reshape(D, -1) for i in range(2)], 1)
    a["mo_wd"] = np.concatenate([g[f"L1_ffn_wd{i}"].reshape(NE1 // 2, P, D).transpose(1, 0, 2).reshape(P, -1)
                                 for i in range(2)], 1)
    a["l2_wqp"], a["l2_wkp"] = padded(g["L2_attn_Wq"].T), padded(g["L2_attn_Wk"].T)
    a["l2_bqp"], a["l2_bkp"] = col(padded(g["L2_attn_bq"][None])), col(padded(g["L2_attn_bk"][None]))
    a["l2_wv"] = g["L2_attn_Wv"].T
    wo = g["L2_attn_Wo"].T.reshape(HG, HG, DH, D)
    a["l2_wo4"] = np.zeros((HG, 32, HG, D), wo.dtype)
    a["l2_wo4"][:, 0:DH] = wo.transpose(0, 2, 1, 3)
    a["l2_wo4"] = a["l2_wo4"].reshape(P, HG, D)
    a["l2_bv"], a["l2_bo"] = rows(g["L2_attn_bv"]), rows(g["L2_attn_bo"])
    a["l2f_router"] = g["L2_ffn_router_w"].T
    a["l2f_we"] = g["L2_ffn_expert_weights"].transpose(1, 0, 2).reshape(D, -1)
    a["l3_nw"] = col(g["L3_attn_norm_w"])
    a["l3_win"] = g["L3_attn_in_proj_w"].T
    a["l3_cw"] = g["L3_attn_conv_w"].reshape(4, P, 4).transpose(1, 0, 2)
    a["l3_cb"] = col(g["L3_attn_conv_b"])
    a["l3_dtb"], a["l3_alog"] = rows(g["L3_attn_dt_bias"]), rows(g["L3_attn_A_log"])
    a["l3_d"] = rows(np.repeat(g["L3_attn_D_param"], HP3))
    a["l3_gw"] = col(g["L3_attn_gate_w"])
    a["l3_wout"] = g["L3_attn_out_proj_w"].T.reshape(2, P, D).transpose(1, 0, 2)
    a["l3f_g1"], a["l3f_g2"] = col(g["L3_ffn_gamma1"]), col(g["L3_ffn_gamma2"])
    a["l3f_wq"], a["l3f_bq"] = g["L3_ffn_Wq"], rows(g["L3_ffn_bq"])
    a["l3f_wd"], a["l3f_bd"] = g["L3_ffn_Wdown"], g["L3_ffn_bdown"].reshape(-1, 1)
    a["l3f_wup"] = g["L3_ffn_Wup"].reshape(64, H, 2, DH).transpose(0, 2, 1, 3).reshape(64, 2 * D)
    a["l3f_bup"] = g["L3_ffn_bup"].reshape(H, 2, DH).transpose(1, 0, 2).reshape(1, 2 * D)
    a["l3f_wo"], a["l3f_bo"] = g["L3_ffn_Wo"], rows(g["L3_ffn_bo"])
    a["l3f_wg"], a["l3f_bg"] = g["L3_ffn_Wg"], rows(g["L3_ffn_bg"])
    a["l3f_we"] = g["L3_ffn_We"].transpose(1, 0, 2).reshape(D, -1)
    a = {k: np.ascontiguousarray(v) for k, v in a.items()}

    nc = bacc.Bacc("TRN2", target_bir_lowering=False, num_devices=1)
    dram = {k: nc.dram_tensor(k, v.shape, mybir.dt.from_np(v.dtype), kind="ExternalInput").ap() for k, v in a.items()}
    x = np.ascontiguousarray(g["L0_attn_x"]).reshape(SEQS // 2, 2, T, D)
    x_in = nc.dram_tensor("x_in", x.shape, F32, kind="ExternalInput").ap()
    out = nc.dram_tensor("x_out", x.shape, F32, kind="ExternalOutput").ap()
    program(nc, dram, x_in, out)
    a["x_in"] = x
    return run(nc, [a], core_ids=[0]).results[0]["x_out"].reshape(SEQS, T, D)
```

```python
from contextlib import ExitStack

import numpy as np

import concourse.bass as bass
from concourse import mybir

ALU = mybir.AluOpType
ACT = mybir.ActivationFunctionType
AX = mybir.AxisListType.X
F32 = mybir.dt.float32
BF16 = mybir.dt.bfloat16
U32 = mybir.dt.uint32

SEQS, T, D = 16, 512, 128
P = 128
NT = T // P
PAIR = (0, 1)
H = 16
DH = D // H
HG = 4
LAT = 32
HD1 = 64
NE1, HID = 32, 64
NE2 = 8
DI, NH3, HP3, NS3 = 256, 4, 64, 128
NEG = -1e30
LAYERS = 8
PARTS = ((0, 4), (4, 8))
L2_ATTENTION = 4


def program(nc, dram, x_in, out):
    with ExitStack() as ctx:
        def sb(name, shape, dt=F32):
            return ctx.enter_context(nc.sbuf_tensor(name, shape, dt))

        def pair_sb(name, shape, dt=F32):
            return [sb(f"{name}{q}", shape, dt) for q in PAIR]

        resident = [name for name in dram if name not in SETUP_ONLY]
        W = {name: sb("w_" + name, list(dram[name].shape), dram[name].dtype)[:] for name in resident}
        absorbed_q = sb("absorbed_q", [P, HG, P])
        absorbed_o = sb("absorbed_o", [P, HG, P])
        neg_a = sb("neg_a", [P, NH3])
        one_minus_mu = sb("one_minus_mu", [P, 2])
        minus_half = sb("minus_half", [P, NT])

        X = pair_sb("x", [P, NT, D])
        A = pair_sb("a", [P, NT, D])
        B = pair_sb("b", [P, NT, D])
        HR = pair_sb("hres", [P, NT, D])
        F = pair_sb("f", [P, 1 + T])
        VA = pair_sb("va", [P, NT, H, DH + 1])
        MV = pair_sb("mv", [P, NT, 2])
        BS = pair_sb("bs", [P, NT, 6])
        SSQ = pair_sb("ssq", [P, NT])
        RS = pair_sb("rs", [P, NT])
        VE = pair_sb("ve", [P, NT])
        arena = pair_sb("arena", [P, 7168])
        NMAX = [sb(f"nmax{i}", [P, HG]) for i in range(4)]
        PR = [sb(f"prob{i}", [P, T]) for i in range(3)]
        PT = [sb(f"probt{i}", [P, NT, P]) for i in range(3)]

        def cut(q, at, *shape):
            n = int(np.prod(shape))
            assert at + n <= 7168
            v = arena[q][:, at:at + n]
            names = " ".join("abc"[:len(shape)])
            kw = {k: s for k, s in zip("abc", shape)}
            return v.rearrange(f"p ({names}) -> p {names}", **kw) if len(shape) > 1 else v

        bank = [ctx.enter_context(nc.psum_tensor(f"bank{i}", [P, 512], F32)) for i in range(8)]

        def pb(q, b):
            return bank[4 * q + b][:]

        def pb3(q, b, n=4):
            return bank[4 * q + b][:].rearrange("p (t d) -> p t d", t=n)

        at = 0
        for name in SETUP_ONLY:
            n = int(np.prod(dram[name].shape[1:]))
            W[name] = cut(0, at, *dram[name].shape[1:])
            at += n

        pool_of_signals = []

        class Signals(dict):
            def __missing__(self, name):
                if len(self) == len(pool_of_signals):
                    pool_of_signals.append(ctx.enter_context(nc.semaphore(f"signal{len(self)}")))
                self[name] = pool_of_signals[len(self)]
                return self[name]

        setup = {name: ctx.enter_context(nc.semaphore(name)) for name in ("weights_loaded", "absorbed", "exp_a")}
        with nc.Block() as block:
            @block.sync
            def _(sp):
                for name, ap in dram.items():
                    sp.dma_start(W[name], ap).then_inc(setup["weights_loaded"], 16)
                sp.wait_ge(setup["weights_loaded"], 16 * len(dram))

            @block.gpsimd
            def _(pool):
                pool.memset(minus_half[:], -0.5)
                for q in PAIR:
                    pool.memset(VA[q][:], 1.0)
                    pool.memset(F[q][:], 0.0)

            @block.tensor
            def _(pe):
                pe.wait_ge(setup["weights_loaded"], 16 * len(dram))
                for h in range(H):
                    o, c = HD1 * (h % 2), h // 2
                    last = pe.matmul(bank[h % 2][:, (h // 2) * LAT:(h // 2 + 1) * LAT], W["l1_wq_t"][o:o + HD1, c],
                                     W["l1_wk_t"][o:o + HD1, c], start=True, stop=True)
                for h in range(H):
                    o, c, g, j = HD1 * (h % 2), h // 2, h // HG, h % HG
                    last = pe.matmul(bank[2 + h % 2][LAT * g:LAT * (g + 1), j * P:(j + 1) * P],
                                     W["l1_wv_t"][o:o + HD1, c], W["l1_wout"][o:o + HD1, c],
                                     start=True, stop=True)
                last.then_inc(setup["absorbed"], 1)

            @block.vector
            def _(dve):
                dve.wait_ge(setup["absorbed"], 1)
                aq = absorbed_q[:].rearrange("p g (k two c) -> p two (g k) c", k=2, two=2)
                for par in range(2):
                    dve.tensor_copy(aq[:, par], bank[par][:, 0:8 * LAT].rearrange("p (h c) -> p h c", c=LAT))
                for j in range(HG):
                    dve.tensor_copy(absorbed_o[:, j], bank[2 + j % 2][:, j * P:(j + 1) * P])
                dve.tensor_scalar(one_minus_mu[:], W["l0f_mu"], -1.0, 1.0, ALU.mult, ALU.add)
                dve.wait_ge(setup["exp_a"], 1)
                dve.tensor_scalar(neg_a[:], neg_a[:], -1.0, None, ALU.mult)

            @block.scalar
            def _(act):
                act.wait_ge(setup["weights_loaded"], 16 * len(dram))
                act.activation(neg_a[:], W["l3_alog"], ACT.Exp).then_inc(setup["exp_a"], 1)

        l0_qp = [cut(q, 0, HG, T) for q in PAIR]
        l0_kp = [cut(q, 2048, HG, T) for q in PAIR]
        l0_kcs = [cut(q, 4096, NT, 2, P) for q in PAIR]
        l0_qcs = [cut(q, 5120, 2, T) for q in PAIR]
        l0_st = [cut(q, 6144, 2, H * (DH + 1)) for q in PAIR]
        l0_tmp = [cut(q, 6432, 2, H * (DH + 1)) for q in PAIR]
        l0_rec = [cut(q, 6720, H) for q in PAIR]
        l0_gelu = [cut(q, 0, 4, T) for q in PAIR]
        at_q = [cut(q, 0, HG, T) for q in PAIR]
        at_lm = [cut(q, 2048, HG, T) for q in PAIR]
        at_lv = [cut(q, 4096, NT, LAT) for q in PAIR]
        at_q2, at_k2 = ([cut(q, T * i, T) for q in PAIR] for i in range(2))
        at_va = [cut(q, 1024, NT, D + 24) for q in PAIR]
        at_km = [[cut(c, 1664 + T * g, T) for g in range(HG)] for c in range(2)]
        at_pr = [PR[i][:] for i in range(3)] + [cut(q, 4736 + T * i, T) for q in PAIR for i in range(3)]
        at_sum = cut(0, 6272, 2, NT * HG)
        at_rec = cut(0, 6304, NT * HG)
        at_y = [[t[q][:].rearrange("p t d -> p (t d)") for t in (A, B, HR)] + [cut(q, 6656, T)] for q in PAIR]
        mo_lg = [cut(q, 0, 8, NE1) for q in PAIR]
        mo_ex = [cut(q, 256, 8, NE1) for q in PAIR]
        mo_m8 = [cut(q, 512, 8, 8) for q in PAIR]
        mo_i8 = [cut(q, 576, 8, 8) for q in PAIR]
        mo_if = [cut(q, 640, 8, 8) for q in PAIR]
        mo_w = [cut(q, 704, 4, 8) for q in PAIR]
        mo_c = [cut(q, 736, 8, NE1) for q in PAIR]
        mo_t = [cut(q, 992, 8, NE1) for q in PAIR]
        mo_c3 = [cut(q, 1248, 8 * 48) for q in PAIR]
        mo_ct = [cut(q, 1632, 512) for q in PAIR]
        mo_acc = [cut(q, 2144, T) for q in PAIR]
        mo_silu = [cut(0, 2656 + T * i, T) for i in range(3)]
        mo_h = [cut(0, 4192 + T * i, T) for i in range(3)]
        mo_b = [cut(0, 5728 + T * i, T) for i in range(2)]
        mo_fb = [cut(q, 2656, 2, T) for q in PAIR]
        ma_xc = [cut(q, 0, 4, T) for q in PAIR]
        ma_xt = [cut(q, 2048, NT, DI) for q in PAIR]
        ma_bt = [cut(q, 3072, NT, P) for q in PAIR]
        ma_xd = [cut(q, 3584, NT, DI) for q in PAIR]
        XB = [cut(q, 2048, 4, 3 + T) for q in PAIR]
        ma_z = [cut(q, 4608, NT, DI) for q in PAIR]
        ma_y = [cut(q, 5632, NT, DI) for q in PAIR]
        ma_sm = [cut(q, 6656, 16, 16) for q in PAIR]
        ma_tmp = [cut(q, 6912, DI) for q in PAIR]
        ht_q = [cut(q, 0, NT, D) for q in PAIR]
        ht_pr = [cut(q, 512, 2048) for q in PAIR]
        ht_sc = [cut(q, 2560, NT, H, H) for q in PAIR]
        ht_o = [cut(q, 3584, NT, D) for q in PAIR]
        ht_sm = [cut(q, 4096, 2, NT * H) for q in PAIR]
        ht_dt = [cut(q, 4224, T) for q in PAIR]
        ht_v = [cut(q, 4736, NT, D) for q in PAIR]

        ident, ident_b = W["ident"], W["ident_b"]
        sg = Signals()
        fresh = {}

        LN = ("ln", 1e-5)
        norms_of_layer = [[LN, ("rms", 1e-6, D), ("rms", 1e-6, D)], [LN], [LN], [LN], [LN], [LN],
                          [LN, ("rms", 1e-5, D), ("rms", 1e-5, DI)], [LN, ("rms", 1e-6, D), ("rms", 1e-6, D)]]

        with nc.Fori(0, SEQS // 2) as pair:
            for first, last in PARTS:
                sg = Signals()
                with nc.Block(no_gpsimd_drain=True) as block:

                    @block.sync
                    def _(sp):
                        for q in PAIR if first == 0 else ():
                            src = x_in[bass.ds(pair, 1), q].rearrange("b (t p) d -> p (b t) d", p=P)
                            sp.dma_start(X[q][:], src).then_inc(sg[f"x_loaded{q}"], 16)
                        for q in PAIR if last == LAYERS else ():
                            dst = out[bass.ds(pair, 1), q].rearrange("b (t p) d -> p (b t) d", p=P)
                            sp.wait_ge(sg["layers_done"], q + 1)
                            sp.dma_start(dst, X[q][:]).then_inc(sg["x_stored"], 16)
                        if last == LAYERS:
                            sp.wait_ge(sg["x_stored"], 32)

                    @block.gpsimd
                    def _(pool):
                        n = 0
                        for layer in range(first, last):
                            for kind in norms_of_layer[layer]:
                                for q in PAIR:
                                    pool.wait_ge(sg["stats_ready"], n + 1)
                                    if kind[0] == "ln":
                                        pool.tensor_scalar(VE[q][:], MV[q][:, :, 1], 1.0, kind[1], ALU.mult,
                                                           ALU.add).then_inc(sg["var_eps"], 1)
                                    else:
                                        pool.tensor_scalar(VE[q][:], SSQ[q][:], 1.0 / kind[2], kind[1], ALU.mult,
                                                           ALU.add).then_inc(sg["var_eps"], 1)
                                    pool.wait_ge(sg["var_eps"], n + 1)
                                    pool.tensor_tensor(RS[q][:], VE[q][:], minus_half[:],
                                                       ALU.pow).then_inc(sg["rstd_ready"], 1)
                                    n += 1
                            if layer == L2_ATTENTION:
                                for c in range(QUARTETS):
                                    q, j = divmod(c, HG)
                                    pool.wait_ge(sg["l2_qk"], 2 * q + 1)
                                    if c >= 2:
                                        pool.wait_ge(sg["l2_scores"], len(UNITS) * (c - 1))
                                    for g in range(HG):
                                        h = HG * g + j
                                        pool.tensor_scalar(at_km[c % 2][g], at_k2[q], W["of_head"][:, h:h + 1], None,
                                                           ALU.mult).then_inc(sg["l2_km"], 1)

                    @block.vector
                    def _(dve):
                        chain = [0]
                        norm = [0]
                        counts = {}

                        def done(ins):
                            chain[0] += 1
                            ins.then_inc(sg["dve_order"], 1)
                            dve.wait_ge(sg["dve_order"], chain[0])

                        def rstd():
                            norm[0] += 1
                            dve.wait_ge(sg["rstd_ready"], norm[0])

                        def layernorm_stats(q):
                            for t in range(NT):
                                i = dve.bn_stats(BS[q][:, t], X[q][:, t])
                            done(i)
                            for t in range(NT):
                                i = dve.bn_aggr(MV[q][:, t], BS[q][:, t])
                            i.then_inc(sg["stats_ready"], 1)

                        def layernorm_apply(q, ready):
                            rstd()
                            for t in range(NT):
                                i = dve.tensor_scalar(A[q][:, t], X[q][:, t], MV[q][:, t, 0:1], RS[q][:, t:t + 1],
                                                      ALU.subtract, ALU.mult)
                            if ready:
                                i.then_inc(sg[ready], 1)
                            else:
                                done(i)

                        def rms_stats(q, src, sq):
                            done(dve.tensor_tensor(sq, src, src, ALU.mult))
                            dve.tensor_reduce(SSQ[q][:], sq, AX, ALU.add).then_inc(sg["stats_ready"], 1)

                        def rms_apply(q, src, dst, ready):
                            rstd()
                            for t in range(NT):
                                i = dve.tensor_scalar(dst[:, t], src[:, t], RS[q][:, t:t + 1], None, ALU.mult)
                            i.then_inc(sg[ready], 1)

                        def attention(tag):
                            for n, unit, block, ended in STEPS:
                                if unit is not None:
                                    k, i, heads = unit
                                    dve.wait_ge(sg[tag + "_scores"], k + 1)
                                    if k >= 4:
                                        dve.wait_ge(sg[tag + "_exp"], k - 3)
                                    s = bank[k % 3][:, 0:P * (i + 1) * len(heads)]
                                    dve.tensor_reduce(NMAX[k % 4][:, 0:len(heads)],
                                                      s.rearrange("p (h c) -> p h c", h=len(heads)), AX, ALU.max,
                                                      negate=True).then_inc(sg[tag + "_max"], 1)
                                if block is not None and not on_act(block[0]):
                                    b = block[0]
                                    dve.wait_ge(sg[tag + "_turned"], b + 1)
                                    if b >= 3:
                                        dve.wait_ge(sg[tag + "_av"], b - 2)
                                    dve.tensor_copy(PT[b % 3][:].rearrange("p t d -> p (t d)"),
                                                    bank[3 + b % 2][:]).then_inc(sg[tag + "_probt_dve"], 1)
                                if block is not None and block[1:] == (0, 0):
                                    c = block[0] // len(BLOCKS)
                                    dve.wait_ge(sg[tag + "_exp"], len(UNITS) * (c + 1))
                                    if c >= 1:
                                        dve.wait_ge(sg[tag + "_rec_mm"], c)
                                    dve.reciprocal(at_rec, at_sum[:, c % 2]).then_inc(sg[tag + "_rec"], 1)
                                if ended is not None:
                                    dve.wait_ge(sg[tag + "_av"], len(BLOCKS) * (ended + 1))
                                    dve.wait_ge(sg[tag + "_rec_rows"], ended + 1)
                                    q, j = divmod(ended, HG)
                                    dve.tensor_tensor(at_y[q][j], bank[5 + ended % 2][:], F[q][:, 1:],
                                                      ALU.mult).then_inc(sg[tag + "_y"], 1)

                        def l0_attention():
                            for q in PAIR:
                                dve.wait_ge(sg[f"x_loaded{q}"], 16)
                                layernorm_stats(q)
                            for q in PAIR:
                                layernorm_apply(q, None)
                                rms_stats(q, A[q][:], B[q][:])
                            for q in PAIR:
                                rms_apply(q, A[q], B[q], "l0_b")
                            for q in PAIR:
                                for g in range(HG):
                                    dve.wait_ge(sg["l0_kp_mm"], q * HG + g + 1)
                                    dve.tensor_scalar(l0_kp[q][:, g], pb(q, 2 + g % 2), W["l0_bkp"][:, g:g + 1], 0.0,
                                                      ALU.add, ALU.max).then_inc(sg["l0_kp"], 1)
                            for q in PAIR:
                                for half in range(2):
                                    dve.wait_ge(sg["l0_kv_mm"], 2 * q + half + 1)
                                    kv = pb3(q, half, 2)
                                    for u in range(2):
                                        t = 2 * half + u
                                        dve.tensor_tensor(B[q][:, t], kv[:, u, 0:D], W["l0_bkv"][:, 0:D], ALU.add)
                                        i = dve.tensor_tensor(VA[q][:, t, :, 0:DH],
                                                              kv[:, u, D:2 * D].rearrange("p (h c) -> p h c", h=H),
                                                              W["l0_bkv"][:, D:2 * D].rearrange("p (h c) -> p h c", h=H),
                                                              ALU.add)
                                    done(i)
                                for t in range(NT):
                                    for s in range(2):
                                        i = dve.tensor_scalar(l0_kcs[q][:, t, s], B[q][:, t], 0.0,
                                                              W["l0_cs_tok"][:, s, t:t + 1], ALU.max, ALU.mult)
                                i.then_inc(sg["l0_kcs"], 1)
                                dve.wait_ge(sg["l0_q"], q + 1)
                                for s in range(2):
                                    i = dve.tensor_tensor(l0_qcs[q][:, s], F[q][:, 1:], W["l0_cs_feat"][:, s], ALU.mult)
                                i.then_inc(sg["l0_qcs"], 1)
                            n = 0
                            for c in range(NT):
                                for q in PAIR:
                                    for j in range(HG):
                                        k = n * HG + j
                                        dve.wait_ge(sg["l0_scores"], k + 1)
                                        if k >= 3:
                                            dve.wait_ge(sg["l0_av"], k - 2)
                                        dve.tensor_tensor(PT[k % 3][:], pb3(q, j % 2),
                                                          W["l0_mask"].unsqueeze(1).broadcast_to([P, HG, P]),
                                                          ALU.mult).then_inc(sg["l0_probt"], 1)
                                    dve.wait_ge(sg["l0_av"], HG * (n + 1))
                                    o = pb(q, 2)[:, 0:H * (DH + 1)].rearrange("p (h c) -> p h c", h=H)
                                    done(dve.tensor_scalar(l0_rec[q], o[:, :, DH], 1e-6, None, ALU.add))
                                    done(dve.reciprocal(l0_rec[q], l0_rec[q]))
                                    dve.tensor_tensor(B[q][:, c].rearrange("p (h c) -> p h c", h=H), o[:, :, 0:DH],
                                                      l0_rec[q].unsqueeze(2).broadcast_to([P, H, DH]),
                                                      ALU.mult).then_inc(sg["l0_ctx"], 1)
                                    if c < NT - 1:
                                        dve.wait_ge(sg["l0_state_mm"], n + 1)
                                        s_ps = pb(q, 3)[:, 0:2 * H * (DH + 1)].rearrange("p (s c) -> p s c", s=2)
                                        bd = W["l0_diag"].unsqueeze(1).broadcast_to([P, 2, H * (DH + 1)])
                                        if c == 0:
                                            dve.tensor_tensor(l0_st[q], s_ps, bd, ALU.mult).then_inc(sg["l0_state"], 1)
                                        else:
                                            done(dve.tensor_tensor(l0_tmp[q], s_ps, bd, ALU.mult))
                                            dve.tensor_tensor(l0_st[q], l0_st[q], l0_tmp[q],
                                                              ALU.add).then_inc(sg["l0_state"], 1)
                                    n += 1
                            for q in PAIR:
                                done(dve.tensor_tensor(HR[q][:], A[q][:],
                                                       W["l0_bo"].unsqueeze(1).broadcast_to([P, NT, D]), ALU.add))
                                dve.wait_ge(sg["l0_out_mm"], q + 1)
                                done(dve.tensor_tensor(HR[q][:], HR[q][:], pb3(q, 1), ALU.add))
                                rms_stats(q, HR[q][:], B[q][:])
                            for q in PAIR:
                                rms_apply(q, HR[q], B[q], "l0_b2")
                                done(dve.tensor_tensor(X[q][:], X[q][:], HR[q][:], ALU.add))
                                done(dve.tensor_tensor(X[q][:], X[q][:],
                                                       W["l0_b2"].unsqueeze(1).broadcast_to([P, NT, D]), ALU.add))
                            for q in PAIR:
                                dve.wait_ge(sg["l0_mlp_mm"], q + 1)
                                done(dve.tensor_tensor(X[q][:], X[q][:], pb3(q, 1), ALU.add))

                        def l0_channel_mix():
                            for q in PAIR:
                                layernorm_stats(q)
                            for q in PAIR:
                                layernorm_apply(q, "c_a")
                            for q in PAIR:
                                dve.wait_ge(sg["c_f"], q + 1)
                                for s in range(2):
                                    done(dve.tensor_scalar(l0_qcs[q][:, s], F[q][:, 0:T], one_minus_mu[:, s:s + 1], None,
                                                           ALU.mult))
                                    dve.scalar_tensor_tensor(l0_qcs[q][:, s], F[q][:, 1:], W["l0f_mu"][:, s:s + 1],
                                                             l0_qcs[q][:, s], ALU.mult, ALU.add).then_inc(sg["c_x"], 1)
                            for q in PAIR:
                                dve.wait_ge(sg["c_relu"], q + 1)
                                dve.tensor_tensor(l0_gelu[q][:, 0], l0_gelu[q][:, 0], l0_gelu[q][:, 0],
                                                  ALU.mult).then_inc(sg["c_k"], 1)
                            for q in PAIR:
                                dve.wait_ge(sg["c_tanh"], q + 1)
                                dve.wait_ge(sg["c_v_mm"], q + 1)
                                done(dve.scalar_tensor_tensor(B[q][:], B[q][:], 1.0, pb3(q, 1), ALU.add, ALU.mult))
                                done(dve.scalar_tensor_tensor(X[q][:], B[q][:], 0.5, X[q][:], ALU.mult, ALU.add))

                        def l1_attention():
                            for q in PAIR:
                                layernorm_stats(q)
                            for q in PAIR:
                                layernorm_apply(q, "l1_a")
                            for q in PAIR:
                                dve.wait_ge(sg["l1_lat_mm"], q + 1)
                                for j in range(HG):
                                    dve.tensor_scalar(at_lm[q][:, j], pb(q, 2), W["quarter"][:, j:j + 1], None, ALU.mult)
                                dve.tensor_copy(at_lv[q], pb(q, 3)[:, 0:NT * LAT].rearrange("p (t c) -> p t c", t=NT)
                                                ).then_inc(sg["l1_lat"], 1)
                            attention("l1")
                            for q in PAIR:
                                dve.wait_ge(sg["l1_out_mm"], q + 1)
                                done(dve.tensor_tensor(X[q][:], X[q][:], pb3(q, 2), ALU.add))

                        def top2(q, lg, n_e, groups, renorm):
                            m8, i8, idx, w = mo_m8[q], mo_i8[q].bitcast(U32), mo_if[q], mo_w[q]
                            for r in range(groups):
                                i = dve.max(m8[:, r], lg[:, r])
                            done(i)
                            for r in range(groups):
                                i = dve.max_index(i8[:, r], m8[:, r], lg[:, r])
                            done(i)
                            g = groups
                            ex = mo_ex[q][:, 0:g, 0:n_e]
                            dve.tensor_tensor(ex, lg, m8[:, 0:g, 0:1].broadcast_to([P, g, n_e]), ALU.subtract)
                            dve.tensor_tensor(w[:, 3, 0:g], m8[:, 0:g, 1], m8[:, 0:g, 0],
                                              ALU.subtract).then_inc(sg["top_shift"], 1)
                            done(dve.tensor_copy(idx[:, 0:g], i8[:, 0:g]))
                            counts["top"] = counts.get("top", 0) + 1
                            dve.wait_ge(sg["top_exp"], counts["top"])
                            done(dve.tensor_reduce(w[:, 0, 0:g], ex, AX, ALU.add))
                            done(dve.reciprocal(w[:, 0, 0:g], w[:, 0, 0:g]))
                            done(dve.tensor_tensor(w[:, 1, 0:g], w[:, 0, 0:g], w[:, 3, 0:g], ALU.mult))
                            return idx, w

                        def onehots(q, c, tmp, idx, w0, w1, n_e, g):
                            iota = W["iota"][:, 0:n_e].unsqueeze(1).broadcast_to([P, g, n_e])
                            dve.tensor_tensor(c, iota, idx[:, 0:g, 0:1].broadcast_to([P, g, n_e]), ALU.is_equal)
                            done(dve.tensor_tensor(tmp, iota, idx[:, 0:g, 1:2].broadcast_to([P, g, n_e]), ALU.is_equal))
                            dve.tensor_tensor(c, c, w0.unsqueeze(2).broadcast_to([P, g, n_e]), ALU.mult)
                            done(dve.tensor_tensor(tmp, tmp, w1.unsqueeze(2).broadcast_to([P, g, n_e]), ALU.mult))
                            done(dve.tensor_tensor(c, c, tmp, ALU.add))

                        def thirds(c, c3, ready):
                            done(dve.tensor_copy(c3[:, :, 0], c))
                            done(dve.tensor_tensor(c, c, c3[:, :, 0], ALU.subtract))
                            done(dve.tensor_copy(c3[:, :, 1], c))
                            done(dve.tensor_tensor(c, c, c3[:, :, 1], ALU.subtract))
                            dve.tensor_copy(c3[:, :, 2], c).then_inc(sg[ready], 1)

                        def l1_moe():
                            for q in PAIR:
                                layernorm_stats(q)
                            for q in PAIR:
                                layernorm_apply(q, "m_a")
                            for q in PAIR:
                                dve.wait_ge(sg["m_logits_mm"], q + 1)
                                done(dve.tensor_copy(mo_lg[q], pb(q, 1)[:, 0:8 * NE1].rearrange("p (g e) -> p g e", g=8)))
                                idx, w = top2(q, mo_lg[q], NE1, 8, False)
                                done(dve.tensor_scalar(w[:, 0:2], w[:, 0:2], 0.5, None, ALU.mult))
                                onehots(q, mo_c[q], mo_t[q], idx, w[:, 0], w[:, 1], NE1, 8)
                                thirds(mo_c[q], mo_c3[q].bitcast(BF16).rearrange("p (g s e) -> p g s e", s=3, e=NE1),
                                       "m_c3")
                            for q in PAIR:
                                for n in range(NE1):
                                    k = q * NE1 + n
                                    if k >= 3:
                                        dve.wait_ge(sg["m_down"], k - 2)
                                    dve.wait_ge(sg["m_silu"], k + 1)
                                    dve.wait_ge(sg["m_up"], k + 1)
                                    done(dve.tensor_tensor(mo_h[k % 3], mo_silu[k % 3], bank[2 + k % 2][:], ALU.mult))
                                    dve.wait_ge(sg["m_b"], k + 1)
                                    dve.tensor_tensor(mo_h[k % 3], mo_h[k % 3], bank[4 + k % 2][:],
                                                      ALU.mult).then_inc(sg["m_h"], 1)
                            for q in PAIR:
                                dve.wait_ge(sg["m_back_mm"], q + 1)
                                done(dve.tensor_tensor(X[q][:], X[q][:], pb3(q, 0), ALU.add))

                        def l2_attention():
                            for q in PAIR:
                                layernorm_stats(q)
                            for q in PAIR:
                                layernorm_apply(q, "l2_a")
                            for q in PAIR:
                                for s, (dst, bias, table) in enumerate(((at_k2, "l2_bk", "l2_rope_k"),
                                                                        (at_q2, "l2_bq", "l2_rope_q"))):
                                    dve.wait_ge(sg["l2_qk_mm"], 2 * q + s + 1)
                                    dve.scalar_tensor_tensor(dst[q], pb(q, s), W[bias], W[table],
                                                             ALU.add, ALU.mult).then_inc(sg["l2_qk"], 1)
                                dve.wait_ge(sg["l2_v_mm"], q + 1)
                                dve.memset(at_va[q][:, :, D:], 0.0)
                                dve.tensor_tensor(at_va[q][:, :, 0:D], pb3(q, 2), W["l2_bv"].unsqueeze(1).broadcast_to(
                                    [P, NT, D]), ALU.add).then_inc(sg["l2_v"], 1)
                            attention("l2")
                            for q in PAIR:
                                done(dve.tensor_tensor(X[q][:], X[q][:],
                                                       W["l2_bo"].unsqueeze(1).broadcast_to([P, NT, D]), ALU.add))
                                dve.wait_ge(sg["l2_out_mm"], q + 1)
                                done(dve.tensor_tensor(X[q][:], X[q][:], pb3(q, 1), ALU.add))

                        def dense_moe(q, tag, c):
                            for e in range(NE2):
                                k = q * NE2 + e
                                dve.wait_ge(sg[tag + "_weights"], k + 1)
                                if e >= 2:
                                    dve.wait_ge(sg[tag + "_up"], k - 1)
                                dve.tensor_tensor(mo_fb[q][:, e % 2], F[q][:, 1:], pb(q, 1 + e % 2),
                                                  ALU.mult).then_inc(sg[tag + "_fb"], 1)

                        def l2_moe():
                            for q in PAIR:
                                layernorm_stats(q)
                            for q in PAIR:
                                layernorm_apply(q, "n_a")
                            for q in PAIR:
                                lg = mo_lg[q][:, 0:NT, 0:NE2]
                                dve.wait_ge(sg["n_logits_mm"], q + 1)
                                done(dve.tensor_copy(lg, pb(q, 1)[:, 0:NT * NE2].rearrange("p (t e) -> p t e", t=NT)))
                                idx, w = top2(q, lg, NE2, NT, True)
                                p0, p1, t2 = w[:, 0, 0:NT], w[:, 1, 0:NT], w[:, 2, 0:NT]
                                t3 = w[:, 3, 0:NT]
                                done(dve.tensor_tensor(t2, p0, p1, ALU.add))
                                done(dve.tensor_scalar(t2, t2, 1e-6, None, ALU.add))
                                done(dve.reciprocal(t2, t2))
                                w0, w1 = w[:, 0, 4:8], w[:, 1, 4:8]
                                dve.tensor_tensor(w0, p0, t2, ALU.mult)
                                done(dve.tensor_tensor(w1, p1, t2, ALU.mult))
                                dve.tensor_tensor(p0, p0, w0, ALU.mult)
                                done(dve.tensor_tensor(p1, p1, w1, ALU.mult))
                                done(dve.tensor_tensor(t3, p0, p1, ALU.add))
                                done(dve.tensor_tensor(X[q][:], X[q][:], t3.unsqueeze(2).broadcast_to([P, NT, D]),
                                                       ALU.add))
                                c = mo_c[q][:, 0:NT, 0:NE2]
                                onehots(q, c, mo_t[q][:, 0:NT, 0:NE2], idx, w0, w1, NE2, NT)
                                thirds(c, mo_c3[q][:, 0:NT * 12].bitcast(BF16).rearrange("p (g s e) -> p g s e", s=3, e=NE2),
                                       "n_c3")
                            for q in PAIR:
                                dense_moe(q, "n", None)
                            for q in PAIR:
                                dve.wait_ge(sg["n_up"], NE2 * (q + 1))
                                done(dve.tensor_tensor(X[q][:], X[q][:], pb3(q, 3), ALU.add))

                        def l3_mamba():
                            for q in PAIR:
                                layernorm_stats(q)
                                dve.memset(XB[q][:, :, 0:3], 0.0)
                            for q in PAIR:
                                layernorm_apply(q, None)
                                rms_stats(q, A[q][:], B[q][:])
                            for q in PAIR:
                                rms_apply(q, A[q], B[q], "l3_b")
                            for q in PAIR:
                                sm = ma_sm[q]
                                dtr, neg, dt = (sm[:, i].rearrange("p (t h) -> p t h", t=NT) for i in range(3))
                                dve.wait_ge(sg["l3_dt_mm"], q + 1)
                                done(dve.tensor_tensor(dtr, pb(q, 3)[:, 0:NT * NH3].rearrange("p (t h) -> p t h", t=NT),
                                                       W["l3_dtb"].unsqueeze(1).broadcast_to([P, NT, NH3]), ALU.add))
                                done(dve.tensor_scalar(neg, dtr, -1.0, None, ALU.mult))
                                dve.tensor_tensor(neg, neg, dtr, ALU.min).then_inc(sg["l3_absdt"], 1)
                            for q in PAIR:
                                for c in range(4):
                                    acc = ma_y[q].rearrange("p t d -> p (t d)")[:, T * (c % 2):T * (c % 2 + 1)]
                                    dve.wait_ge(sg["l3_xb"], 4 * q + c + 1)
                                    if c >= 2:
                                        dve.wait_ge(sg["l3_xc"], 4 * q + c - 1)
                                    done(dve.tensor_scalar(acc, XB[q][:, c, 0:T], W["l3_cw"][:, c, 0:1], None, ALU.mult))
                                    for k in range(1, 4):
                                        i = dve.scalar_tensor_tensor(acc, XB[q][:, c, k:k + T], W["l3_cw"][:, c, k:k + 1],
                                                                     acc, ALU.mult, ALU.add)
                                        if k < 3:
                                            done(i)
                                    i.then_inc(sg["l3_conv"], 1)
                            for q in PAIR:
                                sm = ma_sm[q]
                                dtr, neg, dt, da = (sm[:, i].rearrange("p (t h) -> p t h", t=NT) for i in range(4))
                                dve.wait_ge(sg["l3_ln"], q + 1)
                                done(dve.scalar_tensor_tensor(dt, dtr, 0.0, neg, ALU.max, ALU.add))
                                dve.tensor_tensor(da, dt, neg_a[:].unsqueeze(1).broadcast_to([P, NT, NH3]),
                                                  ALU.mult).then_inc(sg["l3_da"], 1)
                                dve.wait_ge(sg["l3_cum_mm"], q + 1)
                                dve.tensor_copy(sm[:, 4:6], pb(q, 3)[:, 16:48].rearrange("p (a b) -> p a b", a=2)
                                                ).then_inc(sg["l3_cum"], 1)
                                dve.wait_ge(sg["l3_cum"], q + 1)
                                dve.tensor_tensor(sm[:, 6], sm[:, 5], sm[:, 4], ALU.subtract).then_inc(sg["l3_dif"], 1)
                                for t in range(NT):
                                    dve.wait_ge(sg["l3_turn"], NT * q + t + 1)
                                    dve.tensor_copy(ma_xt[q][:, t], pb(q, t % 2)[:, 0:DI])
                                    dve.tensor_copy(ma_bt[q][:, t], pb(q, t % 2)[:, DI:DI + P]).then_inc(sg["l3_xt"], 1)
                                dve.wait_ge(sg["l3_xt"], NT * (q + 1))
                                for t in range(NT):
                                    xh = ma_xt[q][:, t].rearrange("p (h c) -> p h c", h=NH3)
                                    dve.tensor_tensor(ma_y[q][:, t], ma_xt[q][:, t], W["l3_d"], ALU.mult)
                                    dve.tensor_tensor(ma_xd[q][:, t].rearrange("p (h c) -> p h c", h=NH3), xh,
                                                      sm[:, 2, 4 * t:4 * t + 4].unsqueeze(2).broadcast_to([P, NH3, HP3]),
                                                      ALU.mult).then_inc(sg["l3_xd"], 1)
                                dve.wait_ge(sg["l3_xd"], NT * (q + 1))
                                dve.wait_ge(sg["l3_edec"], q + 1)
                                for t in range(NT):
                                    i = dve.tensor_tensor(ma_xt[q][:, t].rearrange("p (h c) -> p h c", h=NH3),
                                                          ma_xd[q][:, t].rearrange("p (h c) -> p h c", h=NH3),
                                                          sm[:, 9, 4 * t:4 * t + 4].unsqueeze(2).broadcast_to([P, NH3, HP3]),
                                                          ALU.mult)
                                i.then_inc(sg["l3_xw"], 1)
                            n = 0
                            for t in range(NT):
                                for q in PAIR:
                                    sm = ma_sm[q]
                                    dve.wait_ge(sg["l3_decay"], n + 1)
                                    dve.wait_ge(sg["l3_g_mm"], n + 1)
                                    dve.tensor_tensor(PT[q][:], PR[q][:].rearrange("p (h t) -> p h t", h=NH3),
                                                      pb(q, 1)[:, 0:P].unsqueeze(1).broadcast_to([P, NH3, P]),
                                                      ALU.mult).then_inc(sg["l3_w"], 1)
                                    if t > 0:
                                        ec = sm[:, 7, 4 * t:4 * t + 4].unsqueeze(2).broadcast_to([P, NH3, HP3])
                                        done(dve.tensor_tensor(ma_tmp[q].rearrange("p (h c) -> p h c", h=NH3),
                                                               pb(q, 1)[:, P:P + DI].rearrange("p (h c) -> p h c", h=NH3),
                                                               ec, ALU.mult))
                                        done(dve.tensor_tensor(ma_y[q][:, t], ma_y[q][:, t], ma_tmp[q], ALU.add))
                                    dve.wait_ge(sg["l3_intra"], n + 1)
                                    y = dve.tensor_tensor(ma_y[q][:, t], ma_y[q][:, t], pb(q, 2)[:, 0:DI], ALU.add)
                                    y.then_inc(sg["l3_yread"], 1)
                                    dve.wait_ge(sg["l3_yread"], n + 1)
                                    if t < NT - 1:
                                        dve.wait_ge(sg["l3_state_mm"], n + 1)
                                        st = HR[q][:].rearrange("p t d -> p (t d)")[:, 0:DI]
                                        s_ps = pb(q, 3)[:, 64:64 + DI]
                                        if t == 0:
                                            dve.tensor_copy(st, s_ps).then_inc(sg["l3_state"], 1)
                                        else:
                                            et = sm[:, 8, 4 * t:4 * t + 4].unsqueeze(2).broadcast_to([P, NH3, HP3])
                                            sth = st.rearrange("p (h c) -> p h c", h=NH3)
                                            done(dve.tensor_tensor(sth, sth, et, ALU.mult))
                                            dve.tensor_tensor(st, st, s_ps, ALU.add).then_inc(sg["l3_state"], 1)
                                    n += 1
                            for q in PAIR:
                                done(dve.tensor_tensor(ma_y[q], ma_y[q], ma_z[q], ALU.mult))
                                done(dve.tensor_tensor(ma_xd[q], ma_y[q], ma_y[q], ALU.mult))
                                dve.tensor_reduce(SSQ[q][:], ma_xd[q], AX, ALU.add).then_inc(sg["stats_ready"], 1)
                                done(dve.tensor_tensor(X[q][:], X[q][:], A[q][:], ALU.add))
                            for q in PAIR:
                                rms_apply(q, ma_y[q], ma_y[q], "l3_y")
                            for q in PAIR:
                                dve.wait_ge(sg["l3_out_mm"], q + 1)
                                done(dve.tensor_tensor(X[q][:], X[q][:], pb3(q, 2), ALU.add))

                        def l3_ffn():
                            for q in PAIR:
                                layernorm_stats(q)
                            for q in PAIR:
                                layernorm_apply(q, None)
                                rms_stats(q, A[q][:], B[q][:])
                            for q in PAIR:
                                rms_apply(q, A[q], B[q], "f_b")
                                done(dve.tensor_tensor(HR[q][:], A[q][:],
                                                       W["l3f_bo"].unsqueeze(1).broadcast_to([P, NT, D]), ALU.add))
                            for q in PAIR:
                                dve.wait_ge(sg["f_q_mm"], q + 1)
                                done(dve.tensor_tensor(ht_q[q], pb3(q, 1),
                                                       W["l3f_bq"].unsqueeze(1).broadcast_to([P, NT, D]), ALU.add))
                                for t in range(NT):
                                    dve.wait_ge(sg["f_kv_mm"], NT * q + 2 * (t // 2) + 2)
                                    pr = ht_pr[q].rearrange("p (h g d) -> p h g d", h=H, g=H)
                                    qb = ht_q[q][:, t].rearrange("p (h d) -> p h d", h=H).unsqueeze(2)
                                    kb = pb3(q, 2 + t // 2, 2)[:, t % 2, 0:D].rearrange("p (g d) -> p g d", g=H).unsqueeze(1)
                                    done(dve.tensor_tensor(pr, qb.broadcast_to([P, H, H, DH]), kb.broadcast_to([P, H, H, DH]),
                                                           ALU.mult))
                                    done(dve.tensor_reduce(ht_sc[q][:, t], pr, AX, ALU.add))
                                sc = ht_sc[q].rearrange("p t h g -> p (t h) g")
                                red = ht_sm[q][:, 0]
                                done(dve.tensor_reduce(red, sc, AX, ALU.max))
                                dve.tensor_tensor(sc, sc, red.unsqueeze(2).broadcast_to([P, NT * H, H]),
                                                  ALU.subtract).then_inc(sg["f_sc"], 1)
                            for q in PAIR:
                                sc = ht_sc[q].rearrange("p t h g -> p (t h) g")
                                red = ht_sm[q][:, 1]
                                dve.wait_ge(sg["f_exp"], q + 1)
                                done(dve.tensor_reduce(red, sc, AX, ALU.add))
                                done(dve.reciprocal(red, red))
                                for t in range(NT):
                                    pr = ht_pr[q].rearrange("p (h d g) -> p h d g", h=H, d=DH)
                                    ab = ht_sc[q][:, t].unsqueeze(2)
                                    vb = pb3(q, 2 + t // 2, 2)[:, t % 2, D:2 * D].rearrange("p (g d) -> p d g", g=H).unsqueeze(1)
                                    done(dve.tensor_tensor(pr, ab.broadcast_to([P, H, DH, H]), vb.broadcast_to([P, H, DH, H]),
                                                           ALU.mult))
                                    done(dve.tensor_reduce(ht_o[q][:, t].rearrange("p (h d) -> p h d", h=H), pr, AX, ALU.add))
                                o = ht_o[q].rearrange("p t (h d) -> p (t h) d", h=H)
                                dve.tensor_tensor(o, o, red.unsqueeze(2).broadcast_to([P, NT * H, DH]),
                                                  ALU.mult).then_inc(sg["f_o"], 1)
                            for q in PAIR:
                                dve.wait_ge(sg["f_out_mm"], q + 1)
                                done(dve.tensor_tensor(HR[q][:], HR[q][:], pb3(q, 1), ALU.add))
                                rms_stats(q, HR[q][:], B[q][:])
                                done(dve.tensor_tensor(X[q][:], X[q][:], HR[q][:], ALU.add))
                            for q in PAIR:
                                rms_apply(q, HR[q], B[q], "f_b2")
                            for q in PAIR:
                                lg = mo_lg[q][:, 0:NT, 0:NE2]
                                red = mo_w[q][:, 0, 0:NT]
                                dve.wait_ge(sg["f_gate_mm"], q + 1)
                                done(dve.tensor_tensor(lg, pb(q, 1)[:, 0:NT * NE2].rearrange("p (t e) -> p t e", t=NT),
                                                       W["l3f_bg"].unsqueeze(1).broadcast_to([P, NT, NE2]), ALU.add))
                                done(dve.tensor_reduce(red, lg, AX, ALU.max))
                                dve.tensor_tensor(lg, lg, red.unsqueeze(2).broadcast_to([P, NT, NE2]),
                                                  ALU.subtract).then_inc(sg["f_gate"], 1)
                                dve.wait_ge(sg["f_gexp"], q + 1)
                                done(dve.tensor_reduce(red, lg, AX, ALU.add))
                                done(dve.reciprocal(red, red))
                                done(dve.tensor_tensor(lg, lg, red.unsqueeze(2).broadcast_to([P, NT, NE2]), ALU.mult))
                                thirds(lg, mo_c3[q][:, 0:NT * 12].bitcast(BF16).rearrange("p (g s e) -> p g s e", s=3, e=NE2),
                                       "f_c3")
                            for q in PAIR:
                                dense_moe(q, "f", None)
                            for q in PAIR:
                                dve.wait_ge(sg["f_up"], NE2 * (q + 1))
                                done(dve.tensor_tensor(X[q][:], X[q][:], pb3(q, 3), ALU.add))

                        for layer in (l0_attention, l0_channel_mix, l1_attention, l1_moe, l2_attention, l2_moe,
                                      l3_mamba, l3_ffn)[first:last]:
                            layer()
                        if last == LAYERS:
                            dve.engine_nop().then_inc(sg["layers_done"], 2)

                    @block.scalar
                    def _(act):
                        top = [0]

                        def to_f(q, wait, n, ready, scale=1.0, b=0):
                            act.wait_ge(sg[wait], n)
                            act.activation(F[q][:, 1:], pb(q, b), ACT.Copy, scale=scale).then_inc(sg[ready], 1)

                        def attention(tag):
                            for n, unit, block, ended in STEPS:
                                if unit is not None:
                                    k, i, heads = unit
                                    c = k // len(UNITS)
                                    act.wait_ge(sg[tag + "_max"], k + 1)
                                    if k >= len(at_pr):
                                        act.wait_ge(sg[tag + "_turned"], last_block(k - len(at_pr)) + 1)
                                    if k % len(UNITS) == 0 and c >= 2:
                                        act.wait_ge(sg[tag + "_rec"], c - 1)
                                    w = P * (i + 1)
                                    for u, g in enumerate(heads):
                                        e = act.activation(at_pr[k % len(at_pr)][:, u * w:(u + 1) * w],
                                                           bank[k % 3][:, u * w:(u + 1) * w], ACT.Exp,
                                                           bias=NMAX[k % 4][:, u:u + 1],
                                                           accum_out=at_sum[:, c % 2, HG * i + g:HG * i + g + 1])
                                    e.then_inc(sg[tag + "_exp"], 1)
                                if block is not None and on_act(block[0]):
                                    b = block[0]
                                    act.wait_ge(sg[tag + "_turned"], b + 1)
                                    if b >= 3:
                                        act.wait_ge(sg[tag + "_av"], b - 2)
                                    act.activation(PT[b % 3][:].rearrange("p t d -> p (t d)"), bank[3 + b % 2][:],
                                                   ACT.Copy).then_inc(sg[tag + "_probt_act"], 1)
                                if ended is not None:
                                    act.wait_ge(sg[tag + "_rec_mm"], ended + 1)
                                    if ended >= 1:
                                        act.wait_ge(sg[tag + "_y"], ended)
                                    act.activation(F[ended // HG][:, 1:], bank[7][:], ACT.Copy
                                                   ).then_inc(sg[tag + "_rec_rows"], 1)

                        def top2_exp(q, ex, w):
                            top[0] += 1
                            act.wait_ge(sg["top_shift"], top[0])
                            act.activation(ex, ex, ACT.Exp)
                            act.activation(w, w, ACT.Exp).then_inc(sg["top_exp"], 1)

                        def l0_attention():
                            for q in PAIR:
                                to_f(q, "l0_turn", q + 1, "l0_f", W["l0_n1"][:, 0:1])
                            for q in PAIR:
                                for g in range(HG):
                                    act.wait_ge(sg["l0_qp_mm"], q * HG + g + 1)
                                    act.activation(l0_qp[q][:, g], pb(q, g % 2), ACT.Relu,
                                                   bias=W["l0_bqp"][:, g:g + 1]).then_inc(sg["l0_qp"], 1)
                            for q in PAIR:
                                act.wait_ge(sg["l0_q_mm"], q + 1)
                                act.activation(F[q][:, 1:], pb(q, 2), ACT.Relu, bias=W["l0_bq"][:, 0:1]
                                               ).then_inc(sg["l0_q"], 1)
                            for q in PAIR:
                                to_f(q, "l0_turn2", q + 1, "l0_f2")
                            for q in PAIR:
                                to_f(q, "l0_turn3", q + 1, "l0_f3", W["l0_n2"][:, 0:1])
                            for q in PAIR:
                                for m in range(4):
                                    act.wait_ge(sg["l0_up_mm"], 4 * q + m + 1)
                                    act.activation(l0_gelu[q][:, m], pb(q, 2 + m % 2), ACT.Gelu_apprx_tanh,
                                                   bias=W["l0_b1"][:, m:m + 1]).then_inc(sg["l0_gelu"], 1)

                        def l0_channel_mix():
                            for q in PAIR:
                                to_f(q, "c_turn", q + 1, "c_f")
                            for q in PAIR:
                                act.wait_ge(sg["c_k_mm"], q + 1)
                                act.activation(l0_gelu[q][:, 0], pb(q, 2), ACT.Relu).then_inc(sg["c_relu"], 1)
                            for q in PAIR:
                                act.wait_ge(sg["c_r_mm"], q + 1)
                                act.activation(B[q][:], pb3(q, 3), ACT.Tanh, scale=0.5).then_inc(sg["c_tanh"], 1)

                        def l1_attention():
                            for q in PAIR:
                                to_f(q, "l1_turn", q + 1, "l1_f")
                            for q in PAIR:
                                for g in range(HG):
                                    act.wait_ge(sg["l1_q_mm"], q * HG + g + 1)
                                    act.activation(at_q[q][:, g], pb(q, g % 2), ACT.Copy,
                                                   scale=HD1 ** -0.5).then_inc(sg["l1_q"], 1)
                            attention("l1")

                        def l1_moe():
                            for q in PAIR:
                                to_f(q, "m_turn", q + 1, "m_f")
                            for q in PAIR:
                                top2_exp(q, mo_ex[q], mo_w[q][:, 3])
                            for q in PAIR:
                                for g in range(2):
                                    act.wait_ge(sg["m_ct_mm"], 2 * q + g + 1)
                                    act.activation(mo_ct[q].bitcast(BF16)[0:96, g * T:(g + 1) * T],
                                                   pb(q, 2 + g).bitcast(BF16)[0:96, 0:T], ACT.Copy).then_inc(sg["m_ct"], 1)
                            for q in PAIR:
                                for n in range(NE1):
                                    k = q * NE1 + n
                                    act.wait_ge(sg["m_gate"], k + 1)
                                    if k >= 3:
                                        act.wait_ge(sg["m_h"], k - 2)
                                    act.activation(mo_silu[k % 3], bank[k % 2][:], ACT.Silu).then_inc(sg["m_silu"], 1)
                            for q in PAIR:
                                act.wait_ge(sg["m_down"], NE1 * (q + 1))
                                act.activation(mo_acc[q], bank[6 + q][:], ACT.Copy).then_inc(sg["m_acc"], 1)

                        def l2_attention():
                            for q in PAIR:
                                to_f(q, "l2_turn", q + 1, "l2_f", b=3)
                            attention("l2")

                        def small_ct(q, tag):
                            act.wait_ge(sg[tag + "_ct_mm"], q + 1)
                            act.activation(mo_ct[q].bitcast(BF16)[0:24, 0:T], pb(q, 2).bitcast(BF16)[0:24, 0:T],
                                           ACT.Copy).then_inc(sg[tag + "_ct"], 1)

                        def l2_moe():
                            for q in PAIR:
                                to_f(q, "n_turn", q + 1, "n_f")
                            for q in PAIR:
                                top2_exp(q, mo_ex[q][:, 0:NT, 0:NE2], mo_w[q][:, 3, 0:NT])
                            for q in PAIR:
                                small_ct(q, "n")

                        def l3_mamba():
                            for q in PAIR:
                                to_f(q, "l3_turn_b", q + 1, "l3_f", W["l3_nw"][:, 0:1])
                            for q in PAIR:
                                for c in range(4):
                                    act.wait_ge(sg["l3_xb_mm"], 4 * q + c + 1)
                                    act.activation(XB[q][:, c, 3:], pb(q, c % 2), ACT.Copy).then_inc(sg["l3_xb"], 1)
                            for q in PAIR:
                                act.wait_ge(sg["l3_absdt"], q + 1)
                                act.activation(ma_sm[q][:, 10], ma_sm[q][:, 1], ACT.Exp).then_inc(sg["l3_expdt"], 1)
                                act.wait_ge(sg["l3_expdt"], q + 1)
                                act.activation(ma_sm[q][:, 1], ma_sm[q][:, 10], ACT.Ln, bias=1.0).then_inc(sg["l3_ln"], 1)
                            for q in PAIR:
                                for half in range(2):
                                    act.wait_ge(sg["l3_z_mm"], 2 * q + half + 1)
                                    act.activation(ma_z[q][:, 2 * half:2 * half + 2], pb3(q, 2, 2),
                                                   ACT.Silu).then_inc(sg["l3_z"], 1)
                            for q in PAIR:
                                for c in range(4):
                                    acc = ma_y[q].rearrange("p t d -> p (t d)")[:, T * (c % 2):T * (c % 2 + 1)]
                                    act.wait_ge(sg["l3_conv"], 4 * q + c + 1)
                                    act.activation(ma_xc[q][:, c], acc, ACT.Silu,
                                                   bias=W["l3_cb"][:, c:c + 1]).then_inc(sg["l3_xc"], 1)
                            for q in PAIR:
                                sm = ma_sm[q]
                                act.wait_ge(sg["l3_cum"], q + 1)
                                act.activation(sm[:, 7:9], sm[:, 4:6], ACT.Exp)
                                act.wait_ge(sg["l3_dif"], q + 1)
                                act.activation(sm[:, 9], sm[:, 6], ACT.Exp).then_inc(sg["l3_edec"], 1)
                            n = 0
                            for t in range(NT):
                                for q in PAIR:
                                    act.wait_ge(sg["l3_decay_mm"], n + 1)
                                    if n >= 2:
                                        act.wait_ge(sg["l3_w"], n - 1)
                                    act.activation(PR[q][:], pb(q, 0), ACT.Exp).then_inc(sg["l3_decay"], 1)
                                    n += 1
                            for q in PAIR:
                                for c in range(2):
                                    act.wait_ge(sg["l3_yt_mm"], 2 * q + c + 1)
                                    act.activation(ma_xc[q][:, c], pb(q, c), ACT.Copy,
                                                   scale=W["l3_gw"][:, c:c + 1]).then_inc(sg["l3_yt"], 1)

                        def l3_ffn():
                            for q in PAIR:
                                to_f(q, "f_turn", q + 1, "f_f", W["l3f_g1"][:, 0:1])
                            for q in PAIR:
                                act.wait_ge(sg["f_down_mm"], q + 1)
                                act.activation(ht_dt[q][0:64], pb(q, 0)[0:64], ACT.Identity,
                                               bias=W["l3f_bd"][0:64, 0:1]).then_inc(sg["f_dt"], 1)
                            for q in PAIR:
                                act.wait_ge(sg["f_sc"], q + 1)
                                act.activation(ht_sc[q], ht_sc[q], ACT.Exp, scale=DH ** -0.5).then_inc(sg["f_exp"], 1)
                            for q in PAIR:
                                to_f(q, "f_turn2", q + 1, "f_f2")
                            for q in PAIR:
                                to_f(q, "f_turn3", q + 1, "f_f3", W["l3f_g2"][:, 0:1])
                            for q in PAIR:
                                act.wait_ge(sg["f_gate"], q + 1)
                                act.activation(mo_lg[q][:, 0:NT, 0:NE2], mo_lg[q][:, 0:NT, 0:NE2],
                                               ACT.Exp).then_inc(sg["f_gexp"], 1)
                            for q in PAIR:
                                small_ct(q, "f")

                        for layer in (l0_attention, l0_channel_mix, l1_attention, l1_moe, l2_attention, l2_moe,
                                      l3_mamba, l3_ffn)[first:last]:
                            layer()

                    @block.tensor
                    def _(pe):
                        def turn(q, src, wait, n, ready, b=0):
                            pe.wait_ge(sg[wait], n)
                            for t in range(NT):
                                i = pe.transpose(pb(q, b)[:, t * P:(t + 1) * P], src[:, t], ident)
                            i.then_inc(sg[ready], 1)

                        def tokens_by(q, b, w, width, at=0, k=P, last=True):
                            for t in range(NT):
                                i = pe.matmul(pb(q, b)[:, t * width:(t + 1) * width],
                                              F[q][:, 1 + t * P:1 + (t + 1) * P], w, start=True, stop=True)
                            return i

                        def probt_ready(tag, b):
                            n = sum(on_act(m) for m in range(b + 1))
                            if on_act(b):
                                pe.wait_ge(sg[tag + "_probt_act"], n)
                            else:
                                pe.wait_ge(sg[tag + "_probt_dve"], b + 1 - n)

                        def attention(tag, scores, values):
                            last = None
                            for n, unit, block, ended in STEPS:
                                if unit is not None:
                                    k, i, heads = unit
                                    q, j = divmod(k // len(UNITS), HG)
                                    w = P * (i + 1)
                                    if k >= 3:
                                        pe.wait_ge(sg[tag + "_exp"], k - 2)
                                    for u, g in enumerate(heads):
                                        lhs, rhs = scores(q, i, HG * g + j)
                                        pe.matmul(bank[k % 3][:, u * w:(u + 1) * w], lhs, rhs, start=(u == 0),
                                                  stop=False, skip_group_check=True)
                                    s = bank[k % 3][:, 0:w * len(heads)].rearrange("p (h c) -> p h c", h=len(heads))
                                    pe.matmul(s[:, :, P * i:], ident_b,
                                              W["mask_b"].unsqueeze(1).broadcast_to([P, len(heads), P]), start=False,
                                              stop=True, skip_group_check=True).then_inc(sg[tag + "_scores"], 1)
                                if block is not None:
                                    b, i, m = block
                                    c = b // len(BLOCKS)
                                    pe.wait_ge(sg[tag + "_exp"], len(UNITS) * c + last_unit_of(i) + 1)
                                    if b >= 2:
                                        probt_ready(tag, b - 2)
                                    for g in range(HG):
                                        k, u = unit_of(c, i, g)
                                        at = P * (u * (i + 1) + m)
                                        ins = pe.transpose(bank[3 + b % 2][:, g * P:(g + 1) * P],
                                                           at_pr[k % len(at_pr)][:, at:at + P], ident)
                                    ins.then_inc(sg[tag + "_turned"], 1)
                                if last is not None:
                                    b, i, m = last
                                    c = b // len(BLOCKS)
                                    q, j = divmod(c, HG)
                                    probt_ready(tag, b)
                                    if b % len(BLOCKS) == 0 and c >= 2:
                                        pe.wait_ge(sg[tag + "_y"], c - 1)
                                    for g in range(HG):
                                        ins = pe.matmul(bank[5 + c % 2][32 * g:32 * (g + 1), P * i:P * (i + 1)],
                                                        values(q, m, HG * g + j), PT[b % 3][:, g],
                                                        start=(i == NT - 1 and m == 0), stop=(m == i),
                                                        skip_group_check=True)
                                    ins.then_inc(sg[tag + "_av"], 1)
                                last = block
                                if ended is not None:
                                    pe.wait_ge(sg[tag + "_rec"], ended + 1)
                                    if ended >= 1:
                                        pe.wait_ge(sg[tag + "_rec_rows"], ended)
                                    for i in range(NT):
                                        for g in range(HG):
                                            n = HG * i + g
                                            ins = pe.matmul(bank[7][32 * g:32 * (g + 1), P * i:P * (i + 1)],
                                                            at_rec[:, n:n + 1].broadcast_to([P, 32]), ident,
                                                            start=True, stop=True)
                                    ins.then_inc(sg[tag + "_rec_mm"], 1)

                        def l0_attention():
                            for q in PAIR:
                                turn(q, B[q], "l0_b", q + 1, "l0_turn")
                            for q in PAIR:
                                pe.wait_ge(sg["l0_f"], q + 1)
                                for g in range(HG):
                                    if g >= 2:
                                        pe.wait_ge(sg["l0_qp"], q * HG + g - 1)
                                        pe.wait_ge(sg["l0_kp"], q * HG + g - 1)
                                    pe.matmul(pb(q, g % 2), W["l0_wqp"][:, g * P:(g + 1) * P], F[q][:, 1:], start=True,
                                              stop=True).then_inc(sg["l0_qp_mm"], 1)
                                    pe.matmul(pb(q, 2 + g % 2), W["l0_wkp"][:, g * P:(g + 1) * P], F[q][:, 1:], start=True,
                                              stop=True).then_inc(sg["l0_kp_mm"], 1)
                            for q in PAIR:
                                pe.wait_ge(sg["l0_qp"], HG * (q + 1))
                                for half in range(2):
                                    for u in range(2):
                                        t = 2 * half + u
                                        i = pe.matmul(pb(q, half)[:, u * 2 * D:(u + 1) * 2 * D],
                                                      F[q][:, 1 + t * P:1 + (t + 1) * P], W["l0_wqkv"][:, D:3 * D],
                                                      start=True, stop=True)
                                    i.then_inc(sg["l0_kv_mm"], 1)
                                pe.wait_ge(sg["l0_kp"], HG * (q + 1))
                                pe.matmul(pb(q, 2), W["l0_wqkv"][:, 0:D], F[q][:, 1:], start=True,
                                          stop=True).then_inc(sg["l0_q_mm"], 1)
                            n = 0
                            for c in range(NT):
                                tok = slice(c * P, (c + 1) * P)
                                for q in PAIR:
                                    if c == 0:
                                        pe.wait_ge(sg["l0_kcs"], q + 1)
                                        pe.wait_ge(sg["l0_q"], q + 1)
                                        pe.wait_ge(sg["l0_qcs"], q + 1)
                                    for j in range(HG):
                                        k = n * HG + j
                                        if j >= 2:
                                            pe.wait_ge(sg["l0_probt"], k - 1)
                                        elif c >= 1:
                                            pe.wait_ge(sg["l0_probt"], HG * (n - 1) - 2 + j + 1)
                                        rows = slice(32 * j, 32 * (j + 1))
                                        for g in range(HG):
                                            i = pe.matmul(pb(q, j % 2)[:, g * P:(g + 1) * P], l0_kp[q][rows, g, tok],
                                                          l0_qp[q][rows, g, tok], start=True, stop=True)
                                        i.then_inc(sg["l0_scores"], 1)
                                    if c < NT - 1:
                                        if c > 0:
                                            pe.wait_ge(sg["l0_state"], n - 1)
                                        for s in range(2):
                                            i = pe.matmul(pb(q, 3)[:, s * H * (DH + 1):(s + 1) * H * (DH + 1)],
                                                          l0_kcs[q][:, c, s], VA[q][:, c].rearrange("p h c -> p (h c)"),
                                                          start=True, stop=True)
                                        i.then_inc(sg["l0_state_mm"], 1)
                                    o = pb(q, 2)[:, 0:H * (DH + 1)]
                                    if c > 0:
                                        pe.wait_ge(sg["l0_ctx"], n - 1)
                                        pe.wait_ge(sg["l0_state"], n - 1)
                                        for s in range(2):
                                            pe.matmul(o, l0_qcs[q][:, s, tok], l0_st[q][:, s], start=(s == 0), stop=False,
                                                      skip_group_check=True)
                                    for j in range(HG):
                                        k = n * HG + j
                                        pe.wait_ge(sg["l0_probt"], k + 1)
                                        for g in range(HG):
                                            h = HG * g + j
                                            i = pe.matmul(o[:, h * (DH + 1):(h + 1) * (DH + 1)], PT[k % 3][:, g],
                                                          VA[q][:, c, h], start=(c == 0 and j == 0 and g == 0), stop=True,
                                                          skip_group_check=True)
                                        i.then_inc(sg["l0_av"], 1)
                                    n += 1
                            for q in PAIR:
                                pe.wait_ge(sg["l0_qcs"], q + 1)
                                turn(q, B[q], "l0_ctx", 2 * NT - 1 + q, "l0_turn2")
                            for q in PAIR:
                                pe.wait_ge(sg["l0_f2"], q + 1)
                                tokens_by(q, 1, W["l0_wo"], D).then_inc(sg["l0_out_mm"], 1)
                            for q in PAIR:
                                turn(q, B[q], "l0_b2", q + 1, "l0_turn3")
                            for q in PAIR:
                                pe.wait_ge(sg["l0_f3"], q + 1)
                                for m in range(4):
                                    if m >= 2:
                                        pe.wait_ge(sg["l0_gelu"], 4 * q + m - 1)
                                    pe.matmul(pb(q, 2 + m % 2), W["l0_w1"][:, m * P:(m + 1) * P], F[q][:, 1:], start=True,
                                              stop=True).then_inc(sg["l0_up_mm"], 1)
                            for q in PAIR:
                                pe.wait_ge(sg["l0_gelu"], 4 * (q + 1))
                                for t in range(NT):
                                    for m in range(4):
                                        i = pe.matmul(pb3(q, 1)[:, t], l0_gelu[q][:, m, t * P:(t + 1) * P],
                                                      W["l0_w2"][:, m], start=(m == 0), stop=(m == 3),
                                                      skip_group_check=True)
                                i.then_inc(sg["l0_mlp_mm"], 1)

                        def l0_channel_mix():
                            for q in PAIR:
                                turn(q, A[q], "c_a", q + 1, "c_turn")
                            for q in PAIR:
                                pe.wait_ge(sg["c_x"], 2 * q + 2)
                                pe.matmul(pb(q, 2), W["l0f_wk"], l0_qcs[q][:, 1], start=True,
                                          stop=True).then_inc(sg["c_k_mm"], 1)
                                for t in range(NT):
                                    i = pe.matmul(pb3(q, 3)[:, t], l0_qcs[q][:, 0, t * P:(t + 1) * P], W["l0f_wr"],
                                                  start=True, stop=True)
                                i.then_inc(sg["c_r_mm"], 1)
                            for q in PAIR:
                                pe.wait_ge(sg["c_k"], q + 1)
                                for t in range(NT):
                                    i = pe.matmul(pb3(q, 1)[:, t], l0_gelu[q][:, 0, t * P:(t + 1) * P], W["l0f_wv"],
                                                  start=True, stop=True)
                                i.then_inc(sg["c_v_mm"], 1)

                        def l1_attention():
                            for q in PAIR:
                                turn(q, A[q], "l1_a", q + 1, "l1_turn")
                            for q in PAIR:
                                pe.wait_ge(sg["l1_f"], q + 1)
                                pe.matmul(pb(q, 2), W["l1_wd4"], F[q][:, 1:], start=True, stop=True)
                                tokens_by(q, 3, W["l1_wd4"][:, 0:LAT], LAT).then_inc(sg["l1_lat_mm"], 1)
                                for g in range(HG):
                                    if g >= 2:
                                        pe.wait_ge(sg["l1_q"], q * HG + g - 1)
                                    pe.matmul(pb(q, g % 2), absorbed_q[:, g], F[q][:, 1:], start=True,
                                              stop=True).then_inc(sg["l1_q_mm"], 1)
                            pe.wait_ge(sg["l1_q"], 2 * HG)
                            pe.wait_ge(sg["l1_lat"], 2)
                            def scores(q, i, h):
                                return at_q[q][:, h // HG, P * i:P * (i + 1)], at_lm[q][:, h % HG, 0:P * (i + 1)]

                            def values(q, m, h):
                                return at_lv[q][:, m]
                            attention("l1", scores, values)
                            for q in PAIR:
                                pe.wait_ge(sg["l1_y"], 2 * HG)
                                for t in range(NT):
                                    for j in range(HG):
                                        i = pe.matmul(pb3(q, 2)[:, t], at_y[q][j][:, t * P:(t + 1) * P],
                                                      absorbed_o[:, j], start=(j == 0), stop=(j == HG - 1),
                                                      skip_group_check=True)
                                i.then_inc(sg["l1_out_mm"], 1)

                        def l1_moe():
                            for q in PAIR:
                                turn(q, A[q], "m_a", q + 1, "m_turn")
                            for q in PAIR:
                                pe.wait_ge(sg["m_f"], q + 1)
                                tokens_by(q, 1, W["mo_router"], 2 * NE1).then_inc(sg["m_logits_mm"], 1)
                            for q in PAIR:
                                pe.wait_ge(sg["m_c3"], q + 1)
                                c3 = mo_c3[q].bitcast(BF16).rearrange("p (g e) -> p g e", e=96)
                                for g in range(2):
                                    for t in range(NT):
                                        i = pe.transpose(pb(q, 2 + g).bitcast(BF16)[0:96, t * P:(t + 1) * P],
                                                         c3[:, 2 * t + g], ident_b)
                                    i.then_inc(sg["m_ct_mm"], 1)
                            pe.wait_ge(sg["m_ct"], 4)
                            for q in PAIR:
                                for n in range(NE1 + 2):
                                    if n < NE1:
                                        k = q * NE1 + n
                                        if k >= 2:
                                            pe.wait_ge(sg["m_silu"], k - 1)
                                        pe.matmul(bank[k % 2][:], W["mo_wg"][:, n * P:(n + 1) * P], F[q][:, 1:], start=True,
                                                  stop=True).then_inc(sg["m_gate"], 1)
                                        if k >= 2:
                                            pe.wait_ge(sg["m_h"], k - 1)
                                        pe.matmul(bank[2 + k % 2][:], W["mo_wu"][:, n * P:(n + 1) * P], F[q][:, 1:],
                                                  start=True, stop=True).then_inc(sg["m_up"], 1)
                                        g, p = n // (NE1 // 2), n % (NE1 // 2)
                                        pe.matmul(bank[4 + k % 2][:], W["sel32"][:, p * P:(p + 1) * P],
                                                  mo_ct[q].bitcast(BF16)[0:96, g * T:(g + 1) * T], start=True,
                                                  stop=True).then_inc(sg["m_b"], 1)
                                    if n >= 2:
                                        k = q * NE1 + n - 2
                                        pe.wait_ge(sg["m_h"], k + 1)
                                        pe.matmul(bank[6 + q][:], W["mo_wd"][:, (n - 2) * P:(n - 1) * P], mo_h[k % 3],
                                                  start=(n == 2), stop=(n == NE1 + 1),
                                                  skip_group_check=True).then_inc(sg["m_down"], 1)
                            for q in PAIR:
                                pe.wait_ge(sg["m_acc"], 2)
                                for t in range(NT):
                                    i = pe.transpose(pb3(q, 0)[:, t], mo_acc[q][:, t * P:(t + 1) * P], ident)
                                i.then_inc(sg["m_back_mm"], 1)

                        def l2_attention():
                            for q in PAIR:
                                turn(q, A[q], "l2_a", q + 1, "l2_turn", b=3)
                            for q in PAIR:
                                pe.wait_ge(sg["l2_f"], q + 1)
                                for s, w in enumerate(("l2_wk", "l2_wq")):
                                    pe.matmul(pb(q, s), W[w], F[q][:, 1:], start=True,
                                              stop=True).then_inc(sg["l2_qk_mm"], 1)
                                tokens_by(q, 2, W["l2_wv"], D).then_inc(sg["l2_v_mm"], 1)
                            pe.wait_ge(sg["l2_v"], 2)
                            def scores(q, i, h):
                                c, g = HG * q + h % HG, h // HG
                                if i == NT - 1:
                                    pe.wait_ge(sg["l2_km"], HG * c + g + 1)
                                return at_q2[q][:, P * i:P * (i + 1)], at_km[c % 2][g][:, 0:P * (i + 1)]

                            def values(q, m, h):
                                return at_va[q][:, m, DH * h:DH * h + 32]
                            attention("l2", scores, values)
                            for q in PAIR:
                                pe.wait_ge(sg["l2_y"], 2 * HG)
                                for t in range(NT):
                                    for j in range(HG):
                                        i = pe.matmul(pb3(q, 1)[:, t], at_y[q][j][:, t * P:(t + 1) * P],
                                                      W["l2_wo4"][:, j], start=(j == 0), stop=(j == HG - 1),
                                                      skip_group_check=True)
                                i.then_inc(sg["l2_out_mm"], 1)

                        def gated_experts(q, tag, weights):
                            acc = pb3(q, 3)
                            for e in range(NE2 + 1):
                                if e < NE2:
                                    k = q * NE2 + e
                                    if e >= 2:
                                        pe.wait_ge(sg[tag + "_fb"], k - 1)
                                    pe.matmul(pb(q, 1 + e % 2), W["sel8"][:, e * P:(e + 1) * P],
                                              mo_ct[q].bitcast(BF16)[0:24, 0:T], start=True,
                                              stop=True).then_inc(sg[tag + "_weights"], 1)
                                if e >= 1:
                                    k = q * NE2 + e - 1
                                    pe.wait_ge(sg[tag + "_fb"], k + 1)
                                    for t in range(NT):
                                        i = pe.matmul(acc[:, t], mo_fb[q][:, (e - 1) % 2, t * P:(t + 1) * P],
                                                      weights[:, (e - 1) * P:e * P], start=(e == 1 and t == 0),
                                                      stop=(e == NE2), skip_group_check=True)
                                    i.then_inc(sg[tag + "_up"], 1)

                        def small_turn(q, tag):
                            pe.wait_ge(sg[tag + "_c3"], q + 1)
                            c3 = mo_c3[q][:, 0:NT * 12].bitcast(BF16).rearrange("p (g e) -> p g e", e=24)
                            for t in range(NT):
                                i = pe.transpose(pb(q, 2).bitcast(BF16)[0:24, t * P:(t + 1) * P], c3[:, t], ident_b)
                            i.then_inc(sg[tag + "_ct_mm"], 1)

                        def l2_moe():
                            for q in PAIR:
                                turn(q, A[q], "n_a", q + 1, "n_turn")
                            for q in PAIR:
                                pe.wait_ge(sg["n_f"], q + 1)
                                tokens_by(q, 1, W["l2f_router"], NE2).then_inc(sg["n_logits_mm"], 1)
                            for q in PAIR:
                                small_turn(q, "n")
                            for q in PAIR:
                                pe.wait_ge(sg["n_ct"], q + 1)
                                gated_experts(q, "n", W["l2f_we"])

                        def l3_mamba():
                            for q in PAIR:
                                turn(q, B[q], "l3_b", q + 1, "l3_turn_b")
                            for q in PAIR:
                                pe.wait_ge(sg["l3_f"], q + 1)
                                tokens_by(q, 3, W["l3_win"][:, 768:772], NH3).then_inc(sg["l3_dt_mm"], 1)
                                for c in range(4):
                                    if c >= 2:
                                        pe.wait_ge(sg["l3_xb"], 4 * q + c - 1)
                                    pe.matmul(pb(q, c % 2), W["l3_win"][:, DI + c * P:DI + (c + 1) * P], F[q][:, 1:],
                                              start=True, stop=True).then_inc(sg["l3_xb_mm"], 1)
                            for q in PAIR:
                                for half in range(2):
                                    if half:
                                        pe.wait_ge(sg["l3_z"], 2 * q + 1)
                                    for u in range(2):
                                        t = 2 * half + u
                                        i = pe.matmul(pb(q, 2)[:, u * DI:(u + 1) * DI], F[q][:, 1 + t * P:1 + (t + 1) * P],
                                                      W["l3_win"][:, 0:DI], start=True, stop=True)
                                    i.then_inc(sg["l3_z_mm"], 1)
                            for q in PAIR:
                                pe.wait_ge(sg["l3_da"], q + 1)
                                da = ma_sm[q][:, 3]
                                pe.matmul(pb(q, 3)[:, 16:32], W["tri"], da, start=True, stop=True)
                                pe.matmul(pb(q, 3)[:, 32:48], W["ones"], da, start=True, stop=True
                                          ).then_inc(sg["l3_cum_mm"], 1)
                                pe.wait_ge(sg["l3_xb"], 4 * (q + 1))
                                pe.wait_ge(sg["l3_xc"], 4 * q + 3)
                                for t in range(NT):
                                    if t >= 2:
                                        pe.wait_ge(sg["l3_xt"], NT * q + t - 1)
                                    for c in range(3):
                                        i = pe.transpose(pb(q, t % 2)[:, c * P:(c + 1) * P],
                                                         ma_xc[q][:, c, t * P:(t + 1) * P], ident)
                                    i.then_inc(sg["l3_turn"], 1)
                            n = 0
                            for t in range(NT):
                                tok = slice(t * P, (t + 1) * P)
                                for q in PAIR:
                                    sm = ma_sm[q]
                                    if t == 0:
                                        pe.wait_ge(sg["l3_xt"], NT * (q + 1))
                                    else:
                                        pe.wait_ge(sg["l3_decay"], n - 1)
                                    for h in range(NH3):
                                        pe.matmul(pb3(q, 0)[:, h],
                                                  sm[:, 3, NH3 * t + h:NH3 * t + h + 1].broadcast_to([P, P]), W["tri"],
                                                  start=(h == 0), stop=False, skip_group_check=True)
                                    pe.matmul(pb(q, 0), W["neg_tri"],
                                              sm[:, 3, NH3 * t:NH3 * (t + 1)].unsqueeze(2).broadcast_to([P, NH3, P]),
                                              start=False, stop=False, skip_group_check=True)
                                    pe.matmul(pb(q, 0), ident_b, W["mask_tb"].unsqueeze(1).broadcast_to([P, NH3, P]),
                                              start=False, stop=True,
                                              skip_group_check=True).then_inc(sg["l3_decay_mm"], 1)
                                    if t == 0:
                                        pe.wait_ge(sg["l3_xc"], 4 * (q + 1))
                                    else:
                                        pe.wait_ge(sg["l3_w"], n - 1)
                                        pe.wait_ge(sg["l3_yread"], n - 1)
                                    i = pe.matmul(pb(q, 1)[:, 0:P], ma_xc[q][:, 2, tok], ma_xc[q][:, 3, tok],
                                                  start=True, stop=True)
                                    st = HR[q][:].rearrange("p t d -> p (t d)")[:, 0:DI]
                                    if t == 0:
                                        pe.wait_ge(sg["l3_z"], 2 * (q + 1))
                                        pe.wait_ge(sg["l3_xw"], q + 1)
                                    else:
                                        pe.wait_ge(sg["l3_state"], n - 1)
                                        i = pe.matmul(pb(q, 1)[:, P:P + DI], ma_xc[q][:, 3, tok], st, start=True,
                                                      stop=True)
                                    i.then_inc(sg["l3_g_mm"], 1)
                                    if t < NT - 1:
                                        pe.matmul(pb(q, 3)[:, 64:64 + DI], ma_bt[q][:, t], ma_xt[q][:, t], start=True,
                                                  stop=True).then_inc(sg["l3_state_mm"], 1)
                                    pe.wait_ge(sg["l3_w"], n + 1)
                                    for h in range(NH3):
                                        i = pe.matmul(pb(q, 2)[:, h * HP3:(h + 1) * HP3], PT[q][:, h],
                                                      ma_xd[q][:, t, h * HP3:(h + 1) * HP3], start=True, stop=True)
                                    i.then_inc(sg["l3_intra"], 1)
                                    n += 1
                            for q in PAIR:
                                pe.wait_ge(sg["l3_y"], q + 1)
                                for c in range(2):
                                    for t in range(NT):
                                        i = pe.transpose(pb3(q, c)[:, t], ma_y[q][:, t, c * P:(c + 1) * P], ident)
                                    i.then_inc(sg["l3_yt_mm"], 1)
                            for q in PAIR:
                                pe.wait_ge(sg["l3_yt"], 2 * (q + 1))
                                for t in range(NT):
                                    for c in range(2):
                                        i = pe.matmul(pb3(q, 2)[:, t], ma_xc[q][:, c, t * P:(t + 1) * P], W["l3_wout"][:, c],
                                                      start=(c == 0), stop=(c == 1), skip_group_check=True)
                                i.then_inc(sg["l3_out_mm"], 1)

                        def l3_ffn():
                            for q in PAIR:
                                turn(q, B[q], "f_b", q + 1, "f_turn")
                            for q in PAIR:
                                pe.wait_ge(sg["f_f"], q + 1)
                                pe.matmul(pb(q, 0)[0:64], W["l3f_wd"], F[q][:, 1:], start=True,
                                          stop=True).then_inc(sg["f_down_mm"], 1)
                                tokens_by(q, 1, W["l3f_wq"], D).then_inc(sg["f_q_mm"], 1)
                                pe.wait_ge(sg["f_dt"], q + 1)
                                for t in range(NT):
                                    o = pb3(q, 2 + t // 2, 2)[:, t % 2]
                                    pe.matmul(o, ht_dt[q][0:64, t * P:(t + 1) * P], W["l3f_wup"], start=True, stop=False,
                                              skip_group_check=True)
                                    pe.matmul(o, W["ones"][0:1, :], W["l3f_bup"], start=False, stop=True,
                                              skip_group_check=True).then_inc(sg["f_kv_mm"], 1)
                            for q in PAIR:
                                turn(q, ht_o[q], "f_o", q + 1, "f_turn2")
                            for q in PAIR:
                                pe.wait_ge(sg["f_f2"], q + 1)
                                tokens_by(q, 1, W["l3f_wo"], D).then_inc(sg["f_out_mm"], 1)
                            for q in PAIR:
                                turn(q, B[q], "f_b2", q + 1, "f_turn3")
                            for q in PAIR:
                                pe.wait_ge(sg["f_f3"], q + 1)
                                tokens_by(q, 1, W["l3f_wg"], NE2).then_inc(sg["f_gate_mm"], 1)
                            for q in PAIR:
                                small_turn(q, "f")
                            for q in PAIR:
                                pe.wait_ge(sg["f_ct"], q + 1)
                                gated_experts(q, "f", W["l3f_we"])

                        for layer in (l0_attention, l0_channel_mix, l1_attention, l1_moe, l2_attention, l2_moe,
                                      l3_mamba, l3_ffn)[first:last]:
                            layer()

                numbers = sorted(s.num for s in pool_of_signals)
                assert numbers == list(range(numbers[0], numbers[-1] + 1)), numbers
                nc.vector.sem_clear(range(numbers[0], numbers[-1] + 1))
                nc.all_engine_barrier()


UNITS = ([(3, (g,)) for g in range(HG)] + [(2, (g,)) for g in range(HG)] + [(1, (0, 1)), (1, (2, 3)), (0, (0, 1, 2, 3))])
BLOCKS = [(i, m) for i in (3, 2, 1, 0) for m in range(i + 1)]
QUARTETS = len(PAIR) * HG


def last_unit_of(i):
    return max(n for n, unit in enumerate(UNITS) if unit[0] == i)


def unit_of(c, i, g):
    n, heads = next((n, heads) for n, (tile, heads) in enumerate(UNITS) if tile == i and g in heads)
    return len(UNITS) * c + n, heads.index(g)


def last_block(k):
    c, n = divmod(k, len(UNITS))
    return len(BLOCKS) * c + BLOCKS.index((UNITS[n][0], UNITS[n][0]))


def steps():
    out, b, n, ended = [], 0, 0, None
    units, blocks = len(UNITS) * QUARTETS, len(BLOCKS) * QUARTETS
    while b < blocks or ended is not None:
        unit = (n,) + UNITS[n % len(UNITS)] if n < units else None
        i, m = BLOCKS[b % len(BLOCKS)]
        ready = b < blocks and len(UNITS) * (b // len(BLOCKS)) + last_unit_of(i) + 2 <= n
        out.append((n, unit, (b, i, m) if ready else None, ended))
        ended = b // len(BLOCKS) if ready and (i, m) == BLOCKS[-1] else None
        b, n = b + ready, n + 1
    return out


STEPS = steps()
SETUP_ONLY = ("l1_wq_t", "l1_wk_t", "l1_wv_t", "l1_wout")


def on_act(b):
    return b % 5 == 2


def tables():
    f4 = np.float32
    bf = mybir.dt.np(BF16)
    pos = np.arange(T, dtype=np.float64)
    cs = np.stack([np.cos(np.pi / 2 * pos / T), np.sin(np.pi / 2 * pos / T)])
    c = {"ident": np.eye(P, dtype=f4), "ident_b": np.eye(P).astype(bf)}
    c["l0_cs_tok"] = cs.reshape(2, NT, P).transpose(2, 0, 1).astype(f4)
    c["l0_cs_feat"] = np.broadcast_to(cs, (P, 2, T)).astype(f4)
    i = np.arange(P)
    lag = i[None, :] - i[:, None]
    c["l0_mask"] = np.where(lag >= 0, np.cos(np.pi / 2 * lag / T), 0).astype(f4)
    c["l0_diag"] = (i[:, None] // DH == np.arange(H * (DH + 1))[None, :] // (DH + 1)).astype(f4)
    c["mask_b"] = np.where(i[None, :] > i[:, None], NEG, 0).astype(bf)
    c["mask_tb"] = np.where(i[None, :] < i[:, None], NEG, 0).astype(bf)
    c["tri"] = (i[:, None] <= i[None, :]).astype(f4)
    c["neg_tri"] = -c["tri"]
    c["ones"] = np.ones((P, P), f4)
    c["iota"] = np.broadcast_to(np.arange(NE1), (P, NE1)).astype(f4)
    theta = (np.arange(T, dtype=f4)[:, None] * np.power(f4(10000.0), f4(-2.0) * np.arange(DH // 2, dtype=f4) / f4(DH)))
    rope = (np.cos(theta.astype(np.float64)) + np.sin(theta.astype(np.float64)))
    rows = np.stack([rope[:, p % (DH // 2)] for p in range(P)])
    c["quarter"] = (i[:, None] // 32 == np.arange(HG)[None, :]).astype(f4)
    c["of_head"] = (i[:, None] // DH == np.arange(H)[None, :]).astype(f4)
    c["l2_rope_k"] = rows.astype(f4)
    c["l2_rope_q"] = (rows / np.sqrt(DH)).astype(f4)
    sel32 = np.zeros((3, NE1, NE1 // 2, P))
    for p in range(NE1 // 2):
        for m in range(P):
            sel32[:, 2 * p + m // HID, p, m] = 1
    c["sel32"] = sel32.reshape(96, -1).astype(bf)
    sel8 = np.zeros((3, NE2, NE2, P))
    for e in range(NE2):
        sel8[:, e, e] = 1
    c["sel8"] = sel8.reshape(24, -1).astype(bf)
    return c


def kernel(**inputs):
    import concourse.bacc as bacc
    from concourse.bass_utils import run_bass_kernel_spmd as run

    g = {k: np.asarray(v) for k, v in inputs.items()}

    def padded(w):
        o = np.zeros((w.shape[0], HG, HG, 32), w.dtype)
        o[..., :DH] = w.reshape(w.shape[0], HG, HG, DH)
        return o.reshape(w.shape[0], HG * P)

    def rows(v):
        return np.broadcast_to(v.reshape(1, -1), (P, v.size))

    def col(v):
        return v.reshape(-1, P).T

    a = dict(tables())
    w = g["L0_attn_qkv_w"]
    b = g["L0_attn_qkv_b"]
    a["l0_wqkv"] = w
    a["l0_wqp"], a["l0_wkp"] = padded(w[:, 0:D]), padded(w[:, D:2 * D])
    a["l0_bqp"], a["l0_bkp"] = (col(padded(b[None, s * D:(s + 1) * D])) for s in range(2))
    a["l0_bq"] = col(b[0:D])
    a["l0_bkv"] = rows(b[D:])
    a["l0_wo"], a["l0_bo"] = g["L0_attn_out_w"], rows(g["L0_attn_out_b"])
    a["l0_n1"], a["l0_n2"] = col(g["L0_attn_norm1_w"]), col(g["L0_attn_norm2_w"])
    a["l0_w1"], a["l0_b1"] = g["L0_attn_mlp_w1"], col(g["L0_attn_mlp_b1"])
    a["l0_w2"] = g["L0_attn_mlp_w2"].reshape(4, P, D).transpose(1, 0, 2)
    a["l0_b2"] = rows(g["L0_attn_mlp_b2"])
    a["l0f_wr"], a["l0f_wk"], a["l0f_wv"] = (g["L0_ffn_W_" + s].T for s in "rkv")
    a["l0f_mu"] = np.stack([g["L0_ffn_mu_r"], g["L0_ffn_mu_k"]], 1)
    a["l1_wq_t"] = g["L1_attn_Wq"].transpose(1, 2, 0).reshape(H // 2, P, D).transpose(1, 0, 2)
    a["l1_wk_t"] = g["L1_attn_Wk_up"].transpose(1, 2, 0).reshape(H // 2, P, LAT).transpose(1, 0, 2)
    a["l1_wv_t"] = g["L1_attn_Wv_up"].transpose(1, 2, 0).reshape(H // 2, P, LAT).transpose(1, 0, 2)
    a["l1_wout"] = g["L1_attn_Wout"].reshape(H // 2, P, D).transpose(1, 0, 2)
    a["l1_wd4"] = np.tile(g["L1_attn_Wkv_down"], (1, 4))
    a["mo_router"] = np.concatenate([g["L1_ffn_router_w0"], g["L1_ffn_router_w1"]], 1)
    for s in "gu":
        a["mo_w" + s] = np.concatenate([g[f"L1_ffn_w{s}{i}"].transpose(1, 0, 2).reshape(D, -1) for i in range(2)], 1)
    a["mo_wd"] = np.concatenate([g[f"L1_ffn_wd{i}"].reshape(NE1 // 2, P, D).transpose(1, 0, 2).reshape(P, -1)
                                 for i in range(2)], 1)
    a["l2_wq"], a["l2_wk"] = g["L2_attn_Wq"].T, g["L2_attn_Wk"].T
    a["l2_bq"], a["l2_bk"] = col(g["L2_attn_bq"]), col(g["L2_attn_bk"])
    a["l2_wv"] = g["L2_attn_Wv"].T
    wo = g["L2_attn_Wo"].T.reshape(HG, HG, DH, D)
    a["l2_wo4"] = np.zeros((HG, 32, HG, D), wo.dtype)
    a["l2_wo4"][:, 0:DH] = wo.transpose(0, 2, 1, 3)
    a["l2_wo4"] = a["l2_wo4"].reshape(P, HG, D)
    a["l2_bv"], a["l2_bo"] = rows(g["L2_attn_bv"]), rows(g["L2_attn_bo"])
    a["l2f_router"] = g["L2_ffn_router_w"].T
    a["l2f_we"] = g["L2_ffn_expert_weights"].transpose(1, 0, 2).reshape(D, -1)
    a["l3_nw"] = col(g["L3_attn_norm_w"])
    a["l3_win"] = g["L3_attn_in_proj_w"].T
    a["l3_cw"] = g["L3_attn_conv_w"].reshape(4, P, 4).transpose(1, 0, 2)
    a["l3_cb"] = col(g["L3_attn_conv_b"])
    a["l3_dtb"], a["l3_alog"] = rows(g["L3_attn_dt_bias"]), rows(g["L3_attn_A_log"])
    a["l3_d"] = rows(np.repeat(g["L3_attn_D_param"], HP3))
    a["l3_gw"] = col(g["L3_attn_gate_w"])
    a["l3_wout"] = g["L3_attn_out_proj_w"].T.reshape(2, P, D).transpose(1, 0, 2)
    a["l3f_g1"], a["l3f_g2"] = col(g["L3_ffn_gamma1"]), col(g["L3_ffn_gamma2"])
    a["l3f_wq"], a["l3f_bq"] = g["L3_ffn_Wq"], rows(g["L3_ffn_bq"])
    a["l3f_wd"], a["l3f_bd"] = g["L3_ffn_Wdown"], g["L3_ffn_bdown"].reshape(-1, 1)
    a["l3f_wup"] = g["L3_ffn_Wup"].reshape(64, H, 2, DH).transpose(0, 2, 1, 3).reshape(64, 2 * D)
    a["l3f_bup"] = g["L3_ffn_bup"].reshape(H, 2, DH).transpose(1, 0, 2).reshape(1, 2 * D)
    a["l3f_wo"], a["l3f_bo"] = g["L3_ffn_Wo"], rows(g["L3_ffn_bo"])
    a["l3f_wg"], a["l3f_bg"] = g["L3_ffn_Wg"], rows(g["L3_ffn_bg"])
    a["l3f_we"] = g["L3_ffn_We"].transpose(1, 0, 2).reshape(D, -1)
    a = {k: np.ascontiguousarray(v) for k, v in a.items()}

    nc = bacc.Bacc("TRN2", target_bir_lowering=False, num_devices=1)
    dram = {k: nc.dram_tensor(k, v.shape, mybir.dt.from_np(v.dtype), kind="ExternalInput").ap() for k, v in a.items()}
    x = np.ascontiguousarray(g["L0_attn_x"]).reshape(SEQS // 2, 2, T, D)
    x_in = nc.dram_tensor("x_in", x.shape, F32, kind="ExternalInput").ap()
    out = nc.dram_tensor("x_out", x.shape, F32, kind="ExternalOutput").ap()
    program(nc, dram, x_in, out)
    a["x_in"] = x
    return run(nc, [a], core_ids=[0]).results[0]["x_out"].reshape(SEQS, T, D)
```

```python
from contextlib import ExitStack

import numpy as np

import concourse.bass as bass
from concourse import mybir

ALU = mybir.AluOpType
ACT = mybir.ActivationFunctionType
AX = mybir.AxisListType.X
F32 = mybir.dt.float32
BF16 = mybir.dt.bfloat16
U32 = mybir.dt.uint32

SEQS, T, D = 16, 512, 128
TAPS = 4
PAD = TAPS - 1
P = 128
NT = T // P
PAIR = (0, 1)
H = 16
DH = D // H
HG = 4
LAT = 32
HD1 = 64
NE1, HID = 32, 64
NE2 = 8
DI, NH3, HP3 = 256, 4, 64
NEG = -1e30
LAYERS = 8
PARTS = ((0, 4), (4, 8))
L2_ATTENTION = 4


def program(nc, dram, x_in, out, scratch):
    with ExitStack() as ctx:
        def sb(name, shape, dt=F32):
            return ctx.enter_context(nc.sbuf_tensor(name, shape, dt))

        def pair_sb(name, shape, dt=F32):
            return [sb(f"{name}{q}", shape, dt) for q in PAIR]

        resident = [name for name in dram if name not in SETUP_ONLY]
        W = {name: sb("w_" + name, list(dram[name].shape), dram[name].dtype)[:] for name in resident}
        absorbed_q = sb("absorbed_q", [P, HG, P])
        absorbed_o = sb("absorbed_o", [P, HG, P])
        neg_a = sb("neg_a", [P, NH3])
        one_minus_mu = sb("one_minus_mu", [P, 2])
        minus_half = sb("minus_half", [P, NT])
        taps_in = sb("taps_in", [P, TAPS, 4 * P])

        X = pair_sb("x", [P, NT, D])
        A = pair_sb("a", [P, NT, D])
        B = pair_sb("b", [P, NT, D])
        HR = pair_sb("hres", [P, NT, D])
        F = pair_sb("f", [P, PAD + T])
        VA = pair_sb("va", [P, NT * H * (DH + 1) + 24])
        MV = pair_sb("mv", [P, NT, 2])
        BS = pair_sb("bs", [P, NT, 6])
        SSQ = pair_sb("ssq", [P, NT])
        RS = pair_sb("rs", [P, NT])
        VE = pair_sb("ve", [P, NT])
        arena = pair_sb("arena", [P, 7168])
        NMAX = [sb(f"nmax{i}", [P, HG]) for i in range(4)]
        PR = [sb(f"prob{i}", [P, T]) for i in range(3)]
        PT = [sb(f"probt{i}", [P, NT, P]) for i in range(3)]

        def cut(q, at, *shape):
            n = int(np.prod(shape))
            assert at + n <= 7168
            v = arena[q][:, at:at + n]
            names = " ".join("abc"[:len(shape)])
            kw = {k: s for k, s in zip("abc", shape)}
            return v.rearrange(f"p ({names}) -> p {names}", **kw) if len(shape) > 1 else v

        bank = [ctx.enter_context(nc.psum_tensor(f"bank{i}", [P, 512], F32)) for i in range(8)]

        def pb(q, b):
            return bank[4 * q + b][:]

        def pb3(q, b, n=4):
            return bank[4 * q + b][:].rearrange("p (t d) -> p t d", t=n)

        at = 0
        for name in SETUP_ONLY:
            n = int(np.prod(dram[name].shape[1:]))
            W[name] = cut(0, at, *dram[name].shape[1:])
            at += n

        pool_of_signals = []

        class Signals(dict):
            def __missing__(self, name):
                if len(self) == len(pool_of_signals):
                    pool_of_signals.append(ctx.enter_context(nc.semaphore(f"signal{len(self)}")))
                self[name] = pool_of_signals[len(self)]
                return self[name]

        setup = {name: ctx.enter_context(nc.semaphore(name)) for name in ("weights_loaded", "absorbed", "exp_a")}
        with nc.Block() as block:
            @block.sync
            def _(sp):
                for name, ap in dram.items():
                    sp.dma_start(W[name], ap).then_inc(setup["weights_loaded"], 16)
                sp.wait_ge(setup["weights_loaded"], 16 * len(dram))

            @block.gpsimd
            def _(pool):
                pool.memset(minus_half[:], -0.5)
                for q in PAIR:
                    pool.memset(VA[q][:], 1.0)
                    pool.memset(F[q][:], 0.0)

            @block.tensor
            def _(pe):
                pe.wait_ge(setup["weights_loaded"], 16 * len(dram))
                for h in range(H):
                    o, c = HD1 * (h % 2), h // 2
                    last = pe.matmul(bank[h % 2][:, (h // 2) * LAT:(h // 2 + 1) * LAT], W["l1_wq_t"][o:o + HD1, c],
                                     W["l1_wk_t"][o:o + HD1, c], start=True, stop=True)
                for h in range(H):
                    o, c, g, j = HD1 * (h % 2), h // 2, h // HG, h % HG
                    last = pe.matmul(bank[2 + h % 2][LAT * g:LAT * (g + 1), j * P:(j + 1) * P],
                                     W["l1_wv_t"][o:o + HD1, c], W["l1_wout"][o:o + HD1, c],
                                     start=True, stop=True)
                last.then_inc(setup["absorbed"], 1)

            @block.vector
            def _(dve):
                dve.wait_ge(setup["absorbed"], 1)
                aq = absorbed_q[:].rearrange("p g (k two c) -> p two (g k) c", k=2, two=2)
                for par in range(2):
                    dve.tensor_copy(aq[:, par], bank[par][:, 0:8 * LAT].rearrange("p (h c) -> p h c", c=LAT))
                for j in range(HG):
                    dve.tensor_copy(absorbed_o[:, j], bank[2 + j % 2][:, j * P:(j + 1) * P])
                dve.tensor_scalar(one_minus_mu[:], W["l0f_mu"], -1.0, 1.0, ALU.mult, ALU.add)
                dve.tensor_tensor(taps_in[:], W["l3_cw"], W["l3_win"][:, DI:DI + 4 * P].unsqueeze(1).broadcast_to(
                    [P, TAPS, 4 * P]), ALU.mult)
                dve.wait_ge(setup["exp_a"], 1)
                dve.tensor_scalar(neg_a[:], neg_a[:], -1.0, None, ALU.mult)

            @block.scalar
            def _(act):
                act.wait_ge(setup["weights_loaded"], 16 * len(dram))
                act.activation(neg_a[:], W["l3_alog"], ACT.Exp).then_inc(setup["exp_a"], 1)

        l0_q, l0_k = ([cut(q, T * i, T) for q in PAIR] for i in range(2))
        l0_km = [[cut(c, 1664 + T * g, T) for g in range(HG)] for c in range(2)]
        l0_kcs = [cut(q, 3712, NT, 2, P) for q in PAIR]
        l0_qcs = [cut(q, 4736, 2, T) for q in PAIR]
        l0_st = [cut(q, 5760, (NT - 1) * 2 * (H * (DH + 1) + 24)).rearrange("p (c s d) -> p c s d", c=NT - 1, s=2)
                 for q in PAIR]
        l0_tmp = [cut(q, 6768, 2, H * (DH + 1)) for q in PAIR]
        l0_y = [[B[q][:].rearrange("p t d -> p (t d)"), PR[q][:], cut(q, 1024, T), cut(q, 3712, T)] for q in PAIR]
        VAT = [VA[q][:, 0:NT * H * (DH + 1)].rearrange("p (t h c) -> p t h c", t=NT, h=H) for q in PAIR]
        l0_gelu = [cut(q, 0, 4, T) for q in PAIR]
        at_q = [cut(q, 0, HG, T) for q in PAIR]
        at_lm = [cut(q, 2048, HG, T) for q in PAIR]
        at_lv = [cut(q, 4096, NT, LAT) for q in PAIR]
        at_va = [cut(q, 0, NT, D + 24) for q in PAIR]
        at_kq = [(B[q][:].rearrange("p t d -> p (t d)"), HR[q][:].rearrange("p t d -> p (t d)")) for q in PAIR]
        at_parts = [cut(q, 608, 2 * 3 * T // 2).bitcast(BF16).rearrange("p (o r t) -> p o r t", o=2, r=3)
                    for q in PAIR]
        at_stack = [cut(half, 2160, 2 * HG * T // 2).bitcast(BF16).rearrange("p (o g t) -> p o g t", o=2, g=HG)
                    for half in range(2)]
        at_pr = [PR[i][:] for i in range(3)] + [cut(q, 4736 + T * i, T) for q in PAIR for i in range(3)]
        at_sum = cut(0, 6272, 2, NT * HG)
        at_rec = sb("inverse_sums", [P, NT * HG])[:]
        at_y = [[t[q][:].rearrange("p t d -> p (t d)") for t in (A, B, HR)] + [cut(q, 6656, T)] for q in PAIR]
        mo_lg = [cut(q, 0, 8, NE1) for q in PAIR]
        mo_ex = [cut(q, 256, 8, NE1) for q in PAIR]
        mo_m8 = [cut(q, 512, 8, 8) for q in PAIR]
        mo_i8 = [cut(q, 576, 8, 8) for q in PAIR]
        mo_if = [cut(q, 640, 8, 8) for q in PAIR]
        mo_w = [cut(q, 704, 4, 8) for q in PAIR]
        mo_c = [cut(q, 736, 8, NE1) for q in PAIR]
        mo_t = [cut(q, 992, 8, NE1) for q in PAIR]
        mo_c3 = [cut(q, 1248, 8 * 48) for q in PAIR]
        mo_ct = [cut(q, 1632, 512) for q in PAIR]
        mo_acc = [cut(q, 2144, T) for q in PAIR]
        mo_silu = [cut(0, 2656 + T * i, T) for i in range(3)]
        mo_h = [cut(0, 4192 + T * i, T) for i in range(3)]
        mo_fb = [cut(q, 2656, 2, T) for q in PAIR]
        ma_xc = [cut(q, 0, 4, T) for q in PAIR]
        ma_xt = [cut(q, 2048, NT, DI) for q in PAIR]
        ma_bt = [cut(q, 3072, NT, P) for q in PAIR]
        ma_xd = [cut(q, 3584, NT, DI) for q in PAIR]
        ma_z = [cut(q, 4608, NT, DI) for q in PAIR]
        ma_y = [cut(q, 5632, NT, DI) for q in PAIR]
        ma_sm = [cut(q, 6656, 16, 16) for q in PAIR]
        ma_tmp = [cut(q, 6912, DI) for q in PAIR]
        ht_q = [cut(q, 0, NT, D) for q in PAIR]
        ht_pr = [cut(q, 512, 2048) for q in PAIR]
        ht_sc = [cut(q, 2560, NT, H, H) for q in PAIR]
        ht_o = [cut(q, 3584, NT, D) for q in PAIR]
        ht_sm = [cut(q, 4096, 2, NT * H) for q in PAIR]
        ht_dt = [cut(q, 4224, T) for q in PAIR]

        ident, ident_b = W["ident"], W["ident_b"]

        LN = ("ln", 1e-5)
        norms_of_layer = [[LN, ("rms", 1e-6, D), ("rms", 1e-6, D)], [LN], [LN], [LN], [LN], [LN],
                          [LN, ("rms", 1e-5, D), ("rms", 1e-5, DI)], [LN, ("rms", 1e-6, D), ("rms", 1e-6, D)]]

        with nc.Fori(0, SEQS // 2) as pair:
            for first, last in PARTS:
                sg = Signals()
                with nc.Block(no_gpsimd_drain=True) as block:

                    @block.sync
                    def _(sp):
                        for q in PAIR if first == 0 else ():
                            src = x_in[bass.ds(pair, 1), q].rearrange("b (t p) d -> p (b t) d", p=P)
                            sp.dma_start(X[q][:], src).then_inc(sg[f"x_loaded{q}"], 16)
                        for q in PAIR if first <= L2_ATTENTION < last else ():
                            for o in range(2):
                                sp.wait_ge(sg["l2_parts"], 2 * q + o + 1)
                                for r in range(3):
                                    sp.dma_start(scratch[q, o, :, r], at_parts[q][:, o, r]
                                                 ).then_inc(sg[f"l2_written{q}"], 16)
                            sp.wait_ge(sg[f"l2_written{q}"], 6 * 16)
                            for half in range(2):
                                if q == 0:
                                    sp.wait_ge(sg["l2_pads"], 2 * (half + 1))
                                else:
                                    sp.wait_ge(sg["l2_scores"], len(UNITS) * 2 * (half + 1))
                                for r in range(2):
                                    keys, queries = (scratch[q, o].rearrange("(g j) r d t -> j r d g t", j=HG)[
                                        2 * half + r] for o in range(2))
                                    row = 64 * r
                                    for key_part, n in enumerate(PRODUCTS):
                                        rows = slice(row, row + n * DH)
                                        for m in range(n):
                                            sp.dma_start(at_stack[half][row + m * DH:row + (m + 1) * DH, 0],
                                                         keys[key_part]).then_inc(sg[f"l2_stacked{q}{half}{r}"], 16)
                                        sp.dma_start(at_stack[half][rows, 1],
                                                     queries[0:n].rearrange("r d g t -> (r d) g t")
                                                     ).then_inc(sg[f"l2_stacked{q}{half}{r}"], 16)
                                        row += n * DH
                        for q in PAIR if last == LAYERS else ():
                            dst = out[bass.ds(pair, 1), q].rearrange("b (t p) d -> p (b t) d", p=P)
                            sp.wait_ge(sg["layers_done"], q + 1)
                            sp.dma_start(dst, X[q][:]).then_inc(sg["x_stored"], 16)
                        if last == LAYERS:
                            sp.wait_ge(sg["x_stored"], 32)

                    @block.gpsimd
                    def _(pool):
                        n = 0
                        for layer in range(first, last):
                            for kind in norms_of_layer[layer]:
                                for q in PAIR:
                                    pool.wait_ge(sg["stats_ready"], n + 1)
                                    if kind[0] == "ln":
                                        pool.tensor_scalar(VE[q][:], MV[q][:, :, 1], 1.0, kind[1], ALU.mult,
                                                           ALU.add).then_inc(sg["var_eps"], 1)
                                    else:
                                        pool.tensor_scalar(VE[q][:], SSQ[q][:], 1.0 / kind[2], kind[1], ALU.mult,
                                                           ALU.add).then_inc(sg["var_eps"], 1)
                                    pool.wait_ge(sg["var_eps"], n + 1)
                                    pool.tensor_tensor(RS[q][:], VE[q][:], minus_half[:],
                                                       ALU.pow).then_inc(sg["rstd_ready"], 1)
                                    n += 1
                            if layer == L2_ATTENTION:
                                pool.wait_ge(sg["rstd_ready"], n)
                                for m in range(4):
                                    row = 32 + 64 * (m % 2)
                                    pool.memset(at_stack[m // 2][row:row + 32], 0.0).then_inc(sg["l2_pads"], 1)
                                    pool.wait_ge(sg["l2_pads"], m + 1)

                    @block.vector
                    def _(dve):
                        chain = [0]
                        norm = [0]
                        tops = [0]

                        def done(ins):
                            chain[0] += 1
                            ins.then_inc(sg["dve_order"], 1)
                            dve.wait_ge(sg["dve_order"], chain[0])

                        def rstd():
                            norm[0] += 1
                            dve.wait_ge(sg["rstd_ready"], norm[0])

                        def layernorm_stats(q):
                            for t in range(NT):
                                i = dve.bn_stats(BS[q][:, t], X[q][:, t])
                            done(i)
                            for t in range(NT):
                                i = dve.bn_aggr(MV[q][:, t], BS[q][:, t])
                            i.then_inc(sg["stats_ready"], 1)

                        def layernorm_apply(q, ready):
                            rstd()
                            for t in range(NT):
                                i = dve.tensor_scalar(A[q][:, t], X[q][:, t], MV[q][:, t, 0:1], RS[q][:, t:t + 1],
                                                      ALU.subtract, ALU.mult)
                            if ready:
                                i.then_inc(sg[ready], 1)
                            else:
                                done(i)

                        def rms_stats(q, src, sq):
                            done(dve.tensor_tensor(sq, src, src, ALU.mult))
                            dve.tensor_reduce(SSQ[q][:], sq, AX, ALU.add).then_inc(sg["stats_ready"], 1)

                        def rms_apply(q, src, dst, ready):
                            rstd()
                            for t in range(NT):
                                i = dve.tensor_scalar(dst[:, t], src[:, t], RS[q][:, t:t + 1], None, ALU.mult)
                            i.then_inc(sg[ready], 1)

                        def attention(tag):
                            def divide(c):
                                q, j = divmod(c, HG)
                                dve.wait_ge(sg[tag + "_av"], len(BLOCKS) * (c + 1))
                                dve.wait_ge(sg[tag + "_rec_rows"], c + 1)
                                dve.tensor_tensor(at_y[q][j], bank[6][:], F[q][:, PAD:],
                                                  ALU.mult).then_inc(sg[tag + "_y"], 1)

                            to_divide = None
                            for unit, block, used, ended in STEPS:
                                if unit is not None:
                                    k, i, heads = unit
                                    dve.wait_ge(sg[tag + "_scores"], k + 1)
                                    if k >= 4:
                                        dve.wait_ge(sg[tag + "_exp"], k - 3)
                                    s = bank[k % 3][:, 0:P * (i + 1) * len(heads)]
                                    dve.tensor_reduce(NMAX[k % 4][:, 0:len(heads)],
                                                      s.rearrange("p (h c) -> p h c", h=len(heads)), AX, ALU.max,
                                                      negate=True).then_inc(sg[tag + "_max"], 1)
                                if block is not None and not on_act(block[0]):
                                    b = block[0]
                                    dve.wait_ge(sg[tag + "_turned"], b + 1)
                                    if b >= 3:
                                        dve.wait_ge(sg[tag + "_av"], b - 2)
                                    dve.tensor_copy(PT[b % 3][:].rearrange("p t d -> p (t d)"),
                                                    bank[3 + b % 3][:]).then_inc(sg[tag + "_probt_dve"], 1)
                                if block is not None and block[1:] == (0, 0):
                                    c = block[0] // len(BLOCKS)
                                    dve.wait_ge(sg[tag + "_exp"], len(UNITS) * (c + 1))
                                    if c >= 1:
                                        dve.wait_ge(sg[tag + "_rec_mm"], c)
                                    dve.reciprocal(at_rec, at_sum[:, c % 2]).then_inc(sg[tag + "_rec"], 1)
                                if to_divide is not None:
                                    divide(to_divide)
                                to_divide = ended
                            divide(to_divide)

                        def l0_attention():
                            for q in PAIR:
                                dve.wait_ge(sg[f"x_loaded{q}"], 16)
                                layernorm_stats(q)
                            for q in PAIR:
                                layernorm_apply(q, None)
                                rms_stats(q, A[q][:], B[q][:])
                            for q in PAIR:
                                rms_apply(q, A[q], B[q], "l0_b")
                            for q in PAIR:
                                dve.memset(l0_st[q][:, :, :, H * (DH + 1):], 0.0)
                                for half in range(2):
                                    dve.wait_ge(sg["l0_kv_mm"], 2 * q + half + 1)
                                    kv = pb3(q, 2 + half, 2)
                                    bias = W["l0_bkv"].unsqueeze(1)
                                    dve.tensor_tensor(B[q][:, 2 * half:2 * half + 2], kv[:, :, 0:D],
                                                      bias[:, :, 0:D].broadcast_to([P, 2, D]), ALU.add)
                                    for u in range(2):
                                        i = dve.tensor_tensor(VAT[q][:, 2 * half + u, :, 0:DH],
                                                              kv[:, u, D:2 * D].rearrange("p (h c) -> p h c", h=H),
                                                              W["l0_bkv"][:, D:2 * D].rearrange("p (h c) -> p h c", h=H),
                                                              ALU.add)
                                    done(i)
                                for t in range(NT):
                                    for s in range(2):
                                        i = dve.tensor_scalar(l0_kcs[q][:, t, s], B[q][:, t], 0.0,
                                                              W["l0_cs_tok"][:, s, t:t + 1], ALU.max, ALU.mult)
                                i.then_inc(sg["l0_kcs"], 1)
                                dve.wait_ge(sg["l0_q"], q + 1)
                                dve.tensor_tensor(l0_qcs[q], l0_q[q].unsqueeze(1).broadcast_to([P, 2, T]),
                                                  W["l0_cs_feat"], ALU.mult).then_inc(sg["l0_qcs"], 1)
                            for q in PAIR:
                                for c in range(NT - 1):
                                    dve.wait_ge(sg["l0_state_mm"], (NT - 1) * q + c + 1)
                                    s_ps = pb(q, c)[:, 0:2 * H * (DH + 1)].rearrange("p (s c) -> p s c", s=2)
                                    bd = W["l0_diag"].unsqueeze(1).broadcast_to([P, 2, H * (DH + 1)])
                                    st = l0_st[q][:, :, :, 0:H * (DH + 1)]
                                    if c == 0:
                                        done(dve.tensor_tensor(st[:, c], s_ps, bd, ALU.mult))
                                    else:
                                        done(dve.tensor_tensor(l0_tmp[q], s_ps, bd, ALU.mult))
                                        done(dve.tensor_tensor(st[:, c], st[:, c - 1], l0_tmp[q], ALU.add))
                                dve.engine_nop().then_inc(sg["l0_state"], 1)

                            def invert(c):
                                dve.wait_ge(sg["l0_norm_mm"], c + 1)
                                if c >= 1:
                                    dve.wait_ge(sg["l0_rec_mm"], c)
                                done(dve.tensor_scalar(at_rec, bank[4][:, 0:NT * HG], 1e-6, None, ALU.add))
                                dve.reciprocal(at_rec, at_rec).then_inc(sg["l0_rec"], 1)

                            def divide(c):
                                q, j = divmod(c, HG)
                                dve.wait_ge(sg["l0_rec_mm"], c + 1)
                                dve.tensor_tensor(l0_y[q][j], l0_y[q][j], bank[7][:], ALU.mult
                                                  ).then_inc(sg["l0_ctx"], 1)

                            for n in range(NT * QUARTETS):
                                dve.wait_ge(sg["l0_scores"], n + 1)
                                if n >= 3:
                                    dve.wait_ge(sg["l0_av"], n - 2)
                                dve.tensor_tensor(PT[n % 3][:], bank[n % 3][:].rearrange("p (g t) -> p g t", g=HG),
                                                  W["l0_mask"].unsqueeze(1).broadcast_to([P, HG, P]),
                                                  ALU.mult).then_inc(sg["l0_probt"], 1)
                                if n >= NT + 2 and n % NT == 2:
                                    invert(n // NT - 1)
                                if n >= NT + 2 and n % NT == 3:
                                    divide(n // NT - 1)
                            invert(QUARTETS - 1)
                            divide(QUARTETS - 1)
                            for q in PAIR:
                                done(dve.tensor_tensor(HR[q][:], A[q][:],
                                                       W["l0_bo"].unsqueeze(1).broadcast_to([P, NT, D]), ALU.add))
                                dve.wait_ge(sg["l0_out_mm"], q + 1)
                                done(dve.tensor_tensor(HR[q][:], HR[q][:], pb3(q, 1), ALU.add))
                                rms_stats(q, HR[q][:], B[q][:])
                            for q in PAIR:
                                rms_apply(q, HR[q], B[q], "l0_b2")
                                done(dve.tensor_tensor(X[q][:], X[q][:], HR[q][:], ALU.add))
                                done(dve.tensor_tensor(X[q][:], X[q][:],
                                                       W["l0_b2"].unsqueeze(1).broadcast_to([P, NT, D]), ALU.add))
                            for q in PAIR:
                                dve.wait_ge(sg["l0_mlp_mm"], q + 1)
                                done(dve.tensor_tensor(X[q][:], X[q][:], pb3(q, 1), ALU.add))
                                layernorm_stats(q)

                        def l0_channel_mix():
                            for q in PAIR:
                                layernorm_apply(q, "c_a")
                            for q in PAIR:
                                dve.wait_ge(sg["c_f"], q + 1)
                                for s in range(2):
                                    done(dve.tensor_scalar(l0_qcs[q][:, s], F[q][:, PAD - 1:PAD - 1 + T], one_minus_mu[:, s:s + 1], None,
                                                           ALU.mult))
                                    dve.scalar_tensor_tensor(l0_qcs[q][:, s], F[q][:, PAD:], W["l0f_mu"][:, s:s + 1],
                                                             l0_qcs[q][:, s], ALU.mult, ALU.add).then_inc(sg["c_x"], 1)
                            for q in PAIR:
                                dve.wait_ge(sg["c_relu"], q + 1)
                                dve.tensor_tensor(l0_gelu[q][:, 0], l0_gelu[q][:, 0], l0_gelu[q][:, 0],
                                                  ALU.mult).then_inc(sg["c_k"], 1)
                            for q in PAIR:
                                dve.wait_ge(sg["c_tanh"], q + 1)
                                dve.wait_ge(sg["c_v_mm"], q + 1)
                                done(dve.scalar_tensor_tensor(B[q][:], B[q][:], 1.0, pb3(q, 1), ALU.add, ALU.mult))
                                done(dve.scalar_tensor_tensor(X[q][:], B[q][:], 0.5, X[q][:], ALU.mult, ALU.add))
                                layernorm_stats(q)

                        def l1_attention():
                            for q in PAIR:
                                layernorm_apply(q, "l1_a")
                            for q in PAIR:
                                dve.wait_ge(sg["l1_lat_mm"], q + 1)
                                for j in range(HG):
                                    dve.tensor_scalar(at_lm[q][:, j], pb(q, 2), W["quarter"][:, j:j + 1], None, ALU.mult)
                                dve.tensor_copy(at_lv[q], pb(q, 3)[:, 0:NT * LAT].rearrange("p (t c) -> p t c", t=NT)
                                                ).then_inc(sg["l1_lat"], 1)
                            attention("l1")
                            for q in PAIR:
                                dve.wait_ge(sg["l1_out_mm"], q + 1)
                                done(dve.tensor_tensor(X[q][:], X[q][:], pb3(q, 2), ALU.add))
                                layernorm_stats(q)

                        def top2(q, lg, groups):
                            m8, i8 = mo_m8[q], mo_i8[q].bitcast(U32)
                            for r in range(groups):
                                i = dve.max(m8[:, r], lg[:, r])
                            done(i)
                            for r in range(groups):
                                i = dve.max_index(i8[:, r], m8[:, r], lg[:, r])
                            done(i)

                        def top2_weights(q, lg, n_e, g):
                            m8, i8, idx, w = mo_m8[q], mo_i8[q].bitcast(U32), mo_if[q], mo_w[q]
                            ex = mo_ex[q][:, 0:g, 0:n_e]
                            dve.tensor_tensor(ex, lg, m8[:, 0:g, 0:1].broadcast_to([P, g, n_e]), ALU.subtract)
                            dve.tensor_tensor(w[:, 3, 0:g], m8[:, 0:g, 1], m8[:, 0:g, 0],
                                              ALU.subtract).then_inc(sg["top_shift"], 1)
                            done(dve.tensor_copy(idx[:, 0:g], i8[:, 0:g]))
                            tops[0] += 1
                            dve.wait_ge(sg["top_exp"], tops[0])
                            done(dve.tensor_reduce(w[:, 0, 0:g], ex, AX, ALU.add))
                            done(dve.reciprocal(w[:, 0, 0:g], w[:, 0, 0:g]))
                            done(dve.tensor_tensor(w[:, 1, 0:g], w[:, 0, 0:g], w[:, 3, 0:g], ALU.mult))
                            return w

                        def onehots(q, c, tmp, idx, w0, w1, n_e, g):
                            iota = W["iota"][:, 0:n_e].unsqueeze(1).broadcast_to([P, g, n_e])
                            dve.tensor_tensor(c, iota, idx[:, 0:g, 0:1].broadcast_to([P, g, n_e]), ALU.is_equal)
                            done(dve.tensor_tensor(tmp, iota, idx[:, 0:g, 1:2].broadcast_to([P, g, n_e]), ALU.is_equal))
                            dve.tensor_tensor(c, c, w0.unsqueeze(2).broadcast_to([P, g, n_e]), ALU.mult)
                            done(dve.tensor_tensor(tmp, tmp, w1.unsqueeze(2).broadcast_to([P, g, n_e]), ALU.mult))
                            done(dve.tensor_tensor(c, c, tmp, ALU.add))

                        def thirds(c, c3, ready):
                            done(dve.tensor_copy(c3[:, :, 0], c))
                            done(dve.tensor_tensor(c, c, c3[:, :, 0], ALU.subtract))
                            done(dve.tensor_copy(c3[:, :, 1], c))
                            done(dve.tensor_tensor(c, c, c3[:, :, 1], ALU.subtract))
                            dve.tensor_copy(c3[:, :, 2], c).then_inc(sg[ready], 1)

                        def l1_moe():
                            for q in PAIR:
                                layernorm_apply(q, "m_a")
                            for q in PAIR:
                                dve.wait_ge(sg["m_logits_mm"], q + 1)
                                done(dve.tensor_copy(mo_lg[q], pb(q, 1)[:, 0:8 * NE1].rearrange("p (g e) -> p g e", g=8)))

                            def find(q):
                                top2(q, mo_lg[q], 8)

                            def weigh(q):
                                w = top2_weights(q, mo_lg[q], NE1, 8)
                                done(dve.tensor_scalar(w[:, 0:2], w[:, 0:2], 0.5, None, ALU.mult))

                            def place(q):
                                onehots(q, mo_c[q], mo_t[q], mo_if[q], mo_w[q][:, 0], mo_w[q][:, 1], NE1, 8)
                                thirds(mo_c[q], mo_c3[q].bitcast(BF16).rearrange("p (g s e) -> p g s e", s=3, e=NE1),
                                       "m_c3")

                            find(0)
                            weigh(0)
                            place(0)
                            for q in PAIR:
                                for n in range(NE1):
                                    if q == 0 and n in MOE_ROUTING:
                                        (find, weigh, place)[MOE_ROUTING.index(n)](1)
                                    k = q * NE1 + n
                                    if k >= 3:
                                        dve.wait_ge(sg["m_down"], k - 2)
                                    dve.wait_ge(sg["m_silu"], k + 1)
                                    dve.wait_ge(sg["m_up"], k + 1)
                                    done(dve.tensor_tensor(mo_h[k % 3], mo_silu[k % 3], bank[2 + k % 2][:], ALU.mult))
                                    dve.wait_ge(sg["m_b"], k + 1)
                                    dve.tensor_tensor(mo_h[k % 3], mo_h[k % 3], bank[4 + k % 2][:],
                                                      ALU.mult).then_inc(sg["m_h"], 1)
                            for q in PAIR:
                                dve.wait_ge(sg["m_back_mm"], q + 1)
                                done(dve.tensor_tensor(X[q][:], X[q][:], pb3(q, 0), ALU.add))

                        def l2_attention():
                            for q in PAIR:
                                layernorm_stats(q)
                            for q in PAIR:
                                layernorm_apply(q, "l2_a")
                            for q in PAIR:
                                for s, (bias, table) in enumerate((("l2_bk", "l2_rope_k"), ("l2_bq", "l2_rope_q"))):
                                    dve.wait_ge(sg["l2_qk_mm"], 2 * q + s + 1)
                                    done(dve.scalar_tensor_tensor(at_kq[q][s], pb(q, s), W[bias], W[table],
                                                                  ALU.add, ALU.mult))
                                    thirds(at_kq[q][s].unsqueeze(1), at_parts[q][:, s].unsqueeze(1), "l2_parts")
                                dve.wait_ge(sg["l2_v_mm"], q + 1)
                                dve.memset(at_va[q][:, :, D:], 0.0)
                                dve.tensor_tensor(at_va[q][:, :, 0:D], pb3(q, 2), W["l2_bv"].unsqueeze(1).broadcast_to(
                                    [P, NT, D]), ALU.add).then_inc(sg["l2_v"], 1)
                            attention("l2")
                            for q in PAIR:
                                done(dve.tensor_tensor(X[q][:], X[q][:],
                                                       W["l2_bo"].unsqueeze(1).broadcast_to([P, NT, D]), ALU.add))
                                dve.wait_ge(sg["l2_out_mm"], q + 1)
                                done(dve.tensor_tensor(X[q][:], X[q][:], pb3(q, 1), ALU.add))
                                layernorm_stats(q)

                        def gated_input(q, e, k, tag, used):
                            dve.wait_ge(sg[tag + "_weights"], k + 1)
                            if e >= 2:
                                dve.wait_ge(sg[tag + "_up"], used)
                            dve.tensor_tensor(mo_fb[q][:, e % 2], F[q][:, PAD:], pb(q, 1 + e % 2),
                                              ALU.mult).then_inc(sg[tag + "_fb"], 1)

                        def l2_moe():
                            for q in PAIR:
                                layernorm_apply(q, "n_a")
                            def find(q):
                                lg = mo_lg[q][:, 0:NT, 0:NE2]
                                dve.wait_ge(sg["n_logits_mm"], q + 1)
                                done(dve.tensor_copy(lg, pb(q, 1)[:, 0:NT * NE2].rearrange("p (t e) -> p t e", t=NT)))
                                top2(q, lg, NT)

                            def weigh(q):
                                w = top2_weights(q, mo_lg[q][:, 0:NT, 0:NE2], NE2, NT)
                                p0, p1, total, bias = (w[:, r, 0:NT] for r in range(4))
                                w0, w1 = w[:, 0, NT:2 * NT], w[:, 1, NT:2 * NT]
                                done(dve.tensor_tensor(total, p0, p1, ALU.add))
                                done(dve.tensor_scalar(total, total, 1e-6, None, ALU.add))
                                done(dve.reciprocal(total, total))
                                dve.tensor_tensor(w0, p0, total, ALU.mult)
                                done(dve.tensor_tensor(w1, p1, total, ALU.mult))
                                dve.tensor_tensor(p0, p0, w0, ALU.mult)
                                done(dve.tensor_tensor(p1, p1, w1, ALU.mult))
                                done(dve.tensor_tensor(bias, p0, p1, ALU.add))
                                done(dve.tensor_tensor(X[q][:], X[q][:], bias.unsqueeze(2).broadcast_to([P, NT, D]),
                                                       ALU.add))

                            def place(q):
                                c, w = mo_c[q][:, 0:NT, 0:NE2], mo_w[q]
                                onehots(q, c, mo_t[q][:, 0:NT, 0:NE2], mo_if[q], w[:, 0, NT:2 * NT],
                                        w[:, 1, NT:2 * NT], NE2, NT)
                                thirds(c, mo_c3[q][:, 0:NT * 12].bitcast(BF16).rearrange("p (g s e) -> p g s e", s=3, e=NE2),
                                       "n_c3")

                            def experts(q, numbers):
                                for e in numbers:
                                    gated_input(q, e, NE2 * q + e, "n", NE2 * q + e - 1)

                            def add(q):
                                dve.wait_ge(sg["n_up"], NE2 * (q + 1))
                                done(dve.tensor_tensor(X[q][:], X[q][:], pb3(q, 3), ALU.add))
                                layernorm_stats(q)

                            find(0)
                            weigh(0)
                            place(0)
                            find(1)
                            experts(0, (0, 1))
                            weigh(1)
                            experts(0, (2, 3, 4))
                            place(1)
                            experts(0, (5, 6, 7))
                            experts(1, (0, 1))
                            add(0)
                            experts(1, range(2, NE2))
                            add(1)

                        def l3_mamba():
                            for q in PAIR:
                                layernorm_apply(q, None)
                                rms_stats(q, A[q][:], B[q][:])
                            for q in PAIR:
                                rms_apply(q, A[q], B[q], "l3_b")
                            for q in PAIR:
                                sm = ma_sm[q]
                                dtr, neg, dt = (sm[:, i].rearrange("p (t h) -> p t h", t=NT) for i in range(3))
                                dve.wait_ge(sg["l3_dt_mm"], q + 1)
                                done(dve.tensor_tensor(dtr, pb(q, 3)[:, 0:NT * NH3].rearrange("p (t h) -> p t h", t=NT),
                                                       W["l3_dtb"].unsqueeze(1).broadcast_to([P, NT, NH3]), ALU.add))
                                done(dve.tensor_scalar(neg, dtr, -1.0, None, ALU.mult))
                                dve.tensor_tensor(neg, neg, dtr, ALU.min).then_inc(sg["l3_absdt"], 1)
                            for q in PAIR:
                                sm = ma_sm[q]
                                dtr, neg, dt, da = (sm[:, i].rearrange("p (t h) -> p t h", t=NT) for i in range(4))
                                dve.wait_ge(sg["l3_ln"], q + 1)
                                done(dve.scalar_tensor_tensor(dt, dtr, 0.0, neg, ALU.max, ALU.add))
                                dve.tensor_tensor(da, dt, neg_a[:].unsqueeze(1).broadcast_to([P, NT, NH3]),
                                                  ALU.mult).then_inc(sg["l3_da"], 1)
                                dve.wait_ge(sg["l3_cum_mm"], q + 1)
                                dve.tensor_copy(sm[:, 4:6], pb(q, 3)[:, 16:48].rearrange("p (a b) -> p a b", a=2)
                                                ).then_inc(sg["l3_cum"], 1)
                                dve.wait_ge(sg["l3_cum"], q + 1)
                                dve.tensor_tensor(sm[:, 6], sm[:, 5], sm[:, 4], ALU.subtract).then_inc(sg["l3_dif"], 1)
                                for t in range(NT):
                                    dve.wait_ge(sg["l3_turn"], NT * q + t + 1)
                                    dve.tensor_copy(ma_xt[q][:, t], pb(q, t % 2)[:, 0:DI])
                                    dve.tensor_copy(ma_bt[q][:, t], pb(q, t % 2)[:, DI:DI + P]).then_inc(sg["l3_xt"], 1)
                                dve.wait_ge(sg["l3_xt"], NT * (q + 1))
                                for t in range(NT):
                                    xh = ma_xt[q][:, t].rearrange("p (h c) -> p h c", h=NH3)
                                    dve.tensor_tensor(ma_y[q][:, t], ma_xt[q][:, t], W["l3_d"], ALU.mult)
                                    dve.tensor_tensor(ma_xd[q][:, t].rearrange("p (h c) -> p h c", h=NH3), xh,
                                                      sm[:, 2, 4 * t:4 * t + 4].unsqueeze(2).broadcast_to([P, NH3, HP3]),
                                                      ALU.mult).then_inc(sg["l3_xd"], 1)
                                dve.wait_ge(sg["l3_xd"], NT * (q + 1))
                                dve.wait_ge(sg["l3_edec"], q + 1)
                                for t in range(NT):
                                    i = dve.tensor_tensor(ma_xt[q][:, t].rearrange("p (h c) -> p h c", h=NH3),
                                                          ma_xd[q][:, t].rearrange("p (h c) -> p h c", h=NH3),
                                                          sm[:, 9, 4 * t:4 * t + 4].unsqueeze(2).broadcast_to([P, NH3, HP3]),
                                                          ALU.mult)
                                i.then_inc(sg["l3_xw"], 1)
                            n = 0
                            for t in range(NT):
                                for q in PAIR:
                                    sm = ma_sm[q]
                                    dve.wait_ge(sg["l3_decay"], n + 1)
                                    dve.wait_ge(sg["l3_g_mm"], n + 1)
                                    dve.tensor_tensor(PT[q][:], PR[q][:].rearrange("p (h t) -> p h t", h=NH3),
                                                      pb(q, 1)[:, 0:P].unsqueeze(1).broadcast_to([P, NH3, P]),
                                                      ALU.mult).then_inc(sg["l3_w"], 1)
                                    if t > 0:
                                        ec = sm[:, 7, 4 * t:4 * t + 4].unsqueeze(2).broadcast_to([P, NH3, HP3])
                                        done(dve.tensor_tensor(ma_tmp[q].rearrange("p (h c) -> p h c", h=NH3),
                                                               pb(q, 1)[:, P:P + DI].rearrange("p (h c) -> p h c", h=NH3),
                                                               ec, ALU.mult))
                                        done(dve.tensor_tensor(ma_y[q][:, t], ma_y[q][:, t], ma_tmp[q], ALU.add))
                                    dve.wait_ge(sg["l3_intra"], n + 1)
                                    y = dve.tensor_tensor(ma_y[q][:, t], ma_y[q][:, t], pb(q, 2)[:, 0:DI], ALU.add)
                                    y.then_inc(sg["l3_yread"], 1)
                                    dve.wait_ge(sg["l3_yread"], n + 1)
                                    if t < NT - 1:
                                        dve.wait_ge(sg["l3_state_mm"], n + 1)
                                        st = HR[q][:].rearrange("p t d -> p (t d)")[:, 0:DI]
                                        s_ps = pb(q, 3)[:, 64:64 + DI]
                                        if t == 0:
                                            dve.tensor_copy(st, s_ps).then_inc(sg["l3_state"], 1)
                                        else:
                                            et = sm[:, 8, 4 * t:4 * t + 4].unsqueeze(2).broadcast_to([P, NH3, HP3])
                                            sth = st.rearrange("p (h c) -> p h c", h=NH3)
                                            done(dve.tensor_tensor(sth, sth, et, ALU.mult))
                                            dve.tensor_tensor(st, st, s_ps, ALU.add).then_inc(sg["l3_state"], 1)
                                    n += 1
                            for q in PAIR:
                                done(dve.tensor_tensor(ma_y[q], ma_y[q], ma_z[q], ALU.mult))
                                done(dve.tensor_tensor(ma_xd[q], ma_y[q], ma_y[q], ALU.mult))
                                dve.tensor_reduce(SSQ[q][:], ma_xd[q], AX, ALU.add).then_inc(sg["stats_ready"], 1)
                                done(dve.tensor_tensor(X[q][:], X[q][:], A[q][:], ALU.add))
                            for q in PAIR:
                                rms_apply(q, ma_y[q], ma_y[q], "l3_y")
                            for q in PAIR:
                                dve.wait_ge(sg["l3_out_mm"], q + 1)
                                done(dve.tensor_tensor(X[q][:], X[q][:], pb3(q, 2), ALU.add))
                                layernorm_stats(q)

                        def l3_ffn():
                            for q in PAIR:
                                layernorm_apply(q, None)
                                rms_stats(q, A[q][:], B[q][:])
                            for q in PAIR:
                                rms_apply(q, A[q], B[q], "f_b")
                                done(dve.tensor_tensor(HR[q][:], A[q][:],
                                                       W["l3f_bo"].unsqueeze(1).broadcast_to([P, NT, D]), ALU.add))
                            for q in PAIR:
                                dve.wait_ge(sg["f_q_mm"], q + 1)
                                done(dve.tensor_tensor(ht_q[q], pb3(q, 1),
                                                       W["l3f_bq"].unsqueeze(1).broadcast_to([P, NT, D]), ALU.add))
                                for t in range(NT):
                                    dve.wait_ge(sg["f_kv_mm"], NT * q + 2 * (t // 2) + 2)
                                    pr = ht_pr[q].rearrange("p (h g d) -> p h g d", h=H, g=H)
                                    qb = ht_q[q][:, t].rearrange("p (h d) -> p h d", h=H).unsqueeze(2)
                                    kb = pb3(q, 2 + t // 2, 2)[:, t % 2, 0:D].rearrange("p (g d) -> p g d", g=H).unsqueeze(1)
                                    done(dve.tensor_tensor(pr, qb.broadcast_to([P, H, H, DH]), kb.broadcast_to([P, H, H, DH]),
                                                           ALU.mult))
                                    done(dve.tensor_reduce(ht_sc[q][:, t], pr, AX, ALU.add))
                                sc = ht_sc[q].rearrange("p t h g -> p (t h) g")
                                red = ht_sm[q][:, 0]
                                done(dve.tensor_reduce(red, sc, AX, ALU.max))
                                dve.tensor_tensor(sc, sc, red.unsqueeze(2).broadcast_to([P, NT * H, H]),
                                                  ALU.subtract).then_inc(sg["f_sc"], 1)
                            def weigh_values(q, t):
                                pr = ht_pr[q].rearrange("p (h d g) -> p h d g", h=H, d=DH)
                                ab = ht_sc[q][:, t].unsqueeze(2)
                                vb = pb3(q, 2 + t // 2, 2)[:, t % 2, D:2 * D].rearrange("p (g d) -> p d g", g=H).unsqueeze(1)
                                done(dve.tensor_tensor(pr, ab.broadcast_to([P, H, DH, H]), vb.broadcast_to([P, H, DH, H]),
                                                       ALU.mult))
                                done(dve.tensor_reduce(ht_o[q][:, t].rearrange("p (h d) -> p h d", h=H), pr, AX, ALU.add))

                            def residual(q):
                                dve.wait_ge(sg["f_out_mm"], q + 1)
                                done(dve.tensor_tensor(HR[q][:], HR[q][:], pb3(q, 1), ALU.add))
                                rms_stats(q, HR[q][:], B[q][:])
                                done(dve.tensor_tensor(X[q][:], X[q][:], HR[q][:], ALU.add))

                            def second_norm(q):
                                rms_apply(q, HR[q], B[q], "f_b2")

                            def gate(q):
                                lg = mo_lg[q][:, 0:NT, 0:NE2]
                                red = mo_w[q][:, 0, 0:NT]
                                dve.wait_ge(sg["f_gate_mm"], q + 1)
                                done(dve.tensor_tensor(lg, pb(q, 1)[:, 0:NT * NE2].rearrange("p (t e) -> p t e", t=NT),
                                                       W["l3f_bg"].unsqueeze(1).broadcast_to([P, NT, NE2]), ALU.add))
                                done(dve.tensor_reduce(red, lg, AX, ALU.max))
                                dve.tensor_tensor(lg, lg, red.unsqueeze(2).broadcast_to([P, NT, NE2]),
                                                  ALU.subtract).then_inc(sg["f_gate"], 1)

                            def gate_weights(q):
                                lg = mo_lg[q][:, 0:NT, 0:NE2]
                                red = mo_w[q][:, 0, 0:NT]
                                dve.wait_ge(sg["f_gexp"], q + 1)
                                done(dve.tensor_reduce(red, lg, AX, ALU.add))
                                done(dve.reciprocal(red, red))
                                done(dve.tensor_tensor(lg, lg, red.unsqueeze(2).broadcast_to([P, NT, NE2]), ALU.mult))
                                thirds(lg, mo_c3[q][:, 0:NT * 12].bitcast(BF16).rearrange("p (g s e) -> p g s e", s=3, e=NE2),
                                       "f_c3")

                            for q in PAIR:
                                sc = ht_sc[q].rearrange("p t h g -> p (t h) g")
                                red = ht_sm[q][:, 1]
                                dve.wait_ge(sg["f_exp"], q + 1)
                                done(dve.tensor_reduce(red, sc, AX, ALU.add))
                                done(dve.reciprocal(red, red))
                                for t in range(NT):
                                    weigh_values(q, t)
                                    if q == 1:
                                        (residual, second_norm, gate, gate_weights)[t](0)
                                o = ht_o[q].rearrange("p t (h d) -> p (t h) d", h=H)
                                dve.tensor_tensor(o, o, red.unsqueeze(2).broadcast_to([P, NT * H, DH]),
                                                  ALU.mult).then_inc(sg["f_o"], 1)
                            def experts(q, numbers):
                                for e in numbers:
                                    gated_input(q, e, NE2 * q + e, "f", NE2 * q + e - 1)

                            residual(1)
                            experts(0, (0, 1))
                            second_norm(1)
                            experts(0, (2,))
                            gate(1)
                            experts(0, (3, 4))
                            gate_weights(1)
                            experts(0, (5, 6, 7))
                            for q in PAIR:
                                if q == 1:
                                    experts(1, range(NE2))
                                dve.wait_ge(sg["f_up"], NE2 * (q + 1))
                                dve.tensor_tensor(X[q][:], X[q][:], pb3(q, 3), ALU.add).then_inc(sg["layers_done"], 1)

                        for layer in (l0_attention, l0_channel_mix, l1_attention, l1_moe, l2_attention, l2_moe,
                                      l3_mamba, l3_ffn)[first:last]:
                            layer()

                    @block.scalar
                    def _(act):
                        top = [0]

                        def to_f(q, wait, n, ready, scale=1.0, b=0):
                            act.wait_ge(sg[wait], n)
                            act.activation(F[q][:, PAD:], pb(q, b), ACT.Copy, scale=scale).then_inc(sg[ready], 1)

                        def attention(tag):
                            for unit, block, used, ended in STEPS:
                                if unit is not None:
                                    k, i, heads = unit
                                    c = k // len(UNITS)
                                    act.wait_ge(sg[tag + "_max"], k + 1)
                                    if k >= len(at_pr):
                                        act.wait_ge(sg[tag + "_turned"], last_block(k - len(at_pr)) + 1)
                                    if k % len(UNITS) == 0 and c >= 2:
                                        act.wait_ge(sg[tag + "_rec"], c - 1)
                                    w = P * (i + 1)
                                    for u, g in enumerate(heads):
                                        e = act.activation(at_pr[k % len(at_pr)][:, u * w:(u + 1) * w],
                                                           bank[k % 3][:, u * w:(u + 1) * w], ACT.Exp,
                                                           bias=NMAX[k % 4][:, u:u + 1],
                                                           accum_out=at_sum[:, c % 2, HG * i + g:HG * i + g + 1])
                                    e.then_inc(sg[tag + "_exp"], 1)
                                if block is not None and on_act(block[0]):
                                    b = block[0]
                                    act.wait_ge(sg[tag + "_turned"], b + 1)
                                    if b >= 3:
                                        act.wait_ge(sg[tag + "_av"], b - 2)
                                    act.activation(PT[b % 3][:].rearrange("p t d -> p (t d)"), bank[3 + b % 3][:],
                                                   ACT.Copy).then_inc(sg[tag + "_probt_act"], 1)
                                if ended is not None:
                                    act.wait_ge(sg[tag + "_rec_mm"], ended + 1)
                                    if ended >= 1:
                                        act.wait_ge(sg[tag + "_y"], ended)
                                    act.activation(F[ended // HG][:, PAD:], bank[7][:], ACT.Copy
                                                   ).then_inc(sg[tag + "_rec_rows"], 1)

                        def top2_exp(q, ex, w):
                            top[0] += 1
                            act.wait_ge(sg["top_shift"], top[0])
                            act.activation(ex, ex, ACT.Exp)
                            act.activation(w, w, ACT.Exp).then_inc(sg["top_exp"], 1)

                        def l0_attention():
                            for q in PAIR:
                                to_f(q, "l0_turn", q + 1, "l0_f", W["l0_n1"][:, 0:1])
                            for q in PAIR:
                                act.wait_ge(sg["l0_k_mm"], q + 1)
                                act.activation(l0_k[q], pb(q, 0), ACT.Relu, bias=W["l0_bk"][:, 0:1]
                                               ).then_inc(sg["l0_k"], 1)
                                act.wait_ge(sg["l0_q_mm"], q + 1)
                                act.activation(l0_q[q], pb(q, 1), ACT.Relu, bias=W["l0_bq"][:, 0:1]
                                               ).then_inc(sg["l0_q"], 1)
                            for c in range(QUARTETS + 2):
                                if c >= 2:
                                    act.wait_ge(sg["l0_av"], NT * (c - 1))
                                    act.activation(l0_y[(c - 2) // HG][(c - 2) % HG], bank[5 + c % 2][:], ACT.Copy
                                                   ).then_inc(sg["l0_y"], 1)
                                if c < QUARTETS:
                                    q, j = divmod(c, HG)
                                    act.wait_ge(sg["l0_k"], q + 1)
                                    for g in range(HG):
                                        h = HG * g + j
                                        act.activation(l0_km[c % 2][g], l0_k[q], ACT.Copy,
                                                       scale=W["of_head"][:, h:h + 1]).then_inc(sg["l0_km"], 1)
                            for q in PAIR:
                                to_f(q, "l0_turn3", q + 1, "l0_f3", W["l0_n2"][:, 0:1])
                            for q in PAIR:
                                for m in range(4):
                                    act.wait_ge(sg["l0_up_mm"], 4 * q + m + 1)
                                    act.activation(l0_gelu[q][:, m], pb(q, 2 + m % 2), ACT.Gelu_apprx_tanh,
                                                   bias=W["l0_b1"][:, m:m + 1]).then_inc(sg["l0_gelu"], 1)

                        def l0_channel_mix():
                            for q in PAIR:
                                to_f(q, "c_turn", q + 1, "c_f")
                            for q in PAIR:
                                act.wait_ge(sg["c_k_mm"], q + 1)
                                act.activation(l0_gelu[q][:, 0], pb(q, 2), ACT.Relu).then_inc(sg["c_relu"], 1)
                            for q in PAIR:
                                act.wait_ge(sg["c_r_mm"], q + 1)
                                act.activation(B[q][:], pb3(q, 3), ACT.Tanh, scale=0.5).then_inc(sg["c_tanh"], 1)

                        def l1_attention():
                            for q in PAIR:
                                to_f(q, "l1_turn", q + 1, "l1_f")
                            for q in PAIR:
                                for g in range(HG):
                                    act.wait_ge(sg["l1_q_mm"], q * HG + g + 1)
                                    act.activation(at_q[q][:, g], pb(q, g % 2), ACT.Copy,
                                                   scale=HD1 ** -0.5).then_inc(sg["l1_q"], 1)
                            attention("l1")

                        def l1_moe():
                            for q in PAIR:
                                to_f(q, "m_turn", q + 1, "m_f")
                            def combine_weights(q):
                                act.wait_ge(sg["m_ct_mm"], q + 1)
                                act.activation(mo_ct[q].bitcast(BF16)[0:96, :], bank[7][:].bitcast(BF16)[0:96, :],
                                               ACT.Copy).then_inc(sg["m_ct"], 1)
                            top2_exp(0, mo_ex[0], mo_w[0][:, 3])
                            combine_weights(0)
                            for q in PAIR:
                                for n in range(NE1):
                                    k = q * NE1 + n
                                    act.wait_ge(sg["m_gate"], k + 1)
                                    if k >= 3:
                                        act.wait_ge(sg["m_h"], k - 2)
                                    act.activation(mo_silu[k % 3], bank[k % 2][:], ACT.Silu).then_inc(sg["m_silu"], 1)
                                    if k == MOE_ROUTING[1] - 1:
                                        top2_exp(1, mo_ex[1], mo_w[1][:, 3])
                                    if k == MOE_TURN:
                                        combine_weights(1)
                            for q in PAIR:
                                act.wait_ge(sg["m_down"], NE1 * (q + 1))
                                act.activation(mo_acc[q], bank[6 + q][:], ACT.Copy).then_inc(sg["m_acc"], 1)

                        def l2_attention():
                            for q in PAIR:
                                to_f(q, "l2_turn", q + 1, "l2_f", b=3)
                            attention("l2")

                        def small_ct(q, tag):
                            act.wait_ge(sg[tag + "_ct_mm"], q + 1)
                            act.activation(mo_ct[q].bitcast(BF16)[0:24, 0:T], pb(q, 2).bitcast(BF16)[0:24, 0:T],
                                           ACT.Copy).then_inc(sg[tag + "_ct"], 1)

                        def l2_moe():
                            for q in PAIR:
                                to_f(q, "n_turn", q + 1, "n_f")
                            for q in PAIR:
                                top2_exp(q, mo_ex[q][:, 0:NT, 0:NE2], mo_w[q][:, 3, 0:NT])
                                small_ct(q, "n")

                        def l3_mamba():
                            for q in PAIR:
                                to_f(q, "l3_turn_b", q + 1, "l3_f", W["l3_nw"][:, 0:1])
                            for q in PAIR:
                                act.wait_ge(sg["l3_absdt"], q + 1)
                                act.activation(ma_sm[q][:, 10], ma_sm[q][:, 1], ACT.Exp).then_inc(sg["l3_expdt"], 1)
                            for q in PAIR:
                                act.wait_ge(sg["l3_expdt"], q + 1)
                                act.activation(ma_sm[q][:, 1], ma_sm[q][:, 10], ACT.Ln, bias=1.0).then_inc(sg["l3_ln"], 1)
                            for q in PAIR:
                                for c in range(4):
                                    act.wait_ge(sg["l3_xb_mm"], 4 * q + c + 1)
                                    act.activation(ma_xc[q][:, c], pb(q, c % 2), ACT.Silu,
                                                   bias=W["l3_cb"][:, c:c + 1]).then_inc(sg["l3_xc"], 1)
                                for half in range(2):
                                    act.wait_ge(sg["l3_z_mm"], 2 * q + half + 1)
                                    act.activation(ma_z[q][:, 2 * half:2 * half + 2], pb3(q, 2, 2),
                                                   ACT.Silu).then_inc(sg["l3_z"], 1)
                                sm = ma_sm[q]
                                act.wait_ge(sg["l3_cum"], q + 1)
                                act.activation(sm[:, 7:9], sm[:, 4:6], ACT.Exp)
                                act.wait_ge(sg["l3_dif"], q + 1)
                                act.activation(sm[:, 9], sm[:, 6], ACT.Exp).then_inc(sg["l3_edec"], 1)
                            n = 0
                            for t in range(NT):
                                for q in PAIR:
                                    act.wait_ge(sg["l3_decay_mm"], n + 1)
                                    if n >= 2:
                                        act.wait_ge(sg["l3_w"], n - 1)
                                    act.activation(PR[q][:], pb(q, 0), ACT.Exp).then_inc(sg["l3_decay"], 1)
                                    n += 1
                            for q in PAIR:
                                for c in range(2):
                                    act.wait_ge(sg["l3_yt_mm"], 2 * q + c + 1)
                                    act.activation(ma_xc[q][:, c], pb(q, c), ACT.Copy,
                                                   scale=W["l3_gw"][:, c:c + 1]).then_inc(sg["l3_yt"], 1)

                        def l3_ffn():
                            for q in PAIR:
                                to_f(q, "f_turn", q + 1, "f_f", W["l3f_g1"][:, 0:1])
                            for q in PAIR:
                                act.wait_ge(sg["f_down_mm"], q + 1)
                                act.activation(ht_dt[q][0:64], pb(q, 0)[0:64], ACT.Identity,
                                               bias=W["l3f_bd"][0:64, 0:1]).then_inc(sg["f_dt"], 1)
                            for q in PAIR:
                                act.wait_ge(sg["f_sc"], q + 1)
                                act.activation(ht_sc[q], ht_sc[q], ACT.Exp, scale=DH ** -0.5).then_inc(sg["f_exp"], 1)
                            for q in PAIR:
                                to_f(q, "f_turn2", q + 1, "f_f2")
                                to_f(q, "f_turn3", q + 1, "f_f3", W["l3f_g2"][:, 0:1])
                                act.wait_ge(sg["f_gate"], q + 1)
                                act.activation(mo_lg[q][:, 0:NT, 0:NE2], mo_lg[q][:, 0:NT, 0:NE2],
                                               ACT.Exp).then_inc(sg["f_gexp"], 1)
                                small_ct(q, "f")

                        for layer in (l0_attention, l0_channel_mix, l1_attention, l1_moe, l2_attention, l2_moe,
                                      l3_mamba, l3_ffn)[first:last]:
                            layer()

                    @block.tensor
                    def _(pe):
                        def turn(q, src, wait, n, ready, b=0):
                            pe.wait_ge(sg[wait], n)
                            for t in range(NT):
                                i = pe.transpose(pb(q, b)[:, t * P:(t + 1) * P], src[:, t], ident)
                            i.then_inc(sg[ready], 1)

                        def tokens_by(q, b, w, width):
                            for t in range(NT):
                                i = pe.matmul(pb(q, b)[:, t * width:(t + 1) * width],
                                              F[q][:, PAD + t * P:PAD + (t + 1) * P], w, start=True, stop=True)
                            return i

                        def spread_inverses():
                            for t in range(NT):
                                for g in range(HG):
                                    n = HG * t + g
                                    i = pe.matmul(bank[7][32 * g:32 * (g + 1), P * t:P * (t + 1)],
                                                  at_rec[:, n:n + 1].broadcast_to([P, 32]), ident, start=True, stop=True)
                            return i

                        def probt_ready(tag, b):
                            n = sum(on_act(m) for m in range(b + 1))
                            if on_act(b):
                                pe.wait_ge(sg[tag + "_probt_act"], n)
                            else:
                                pe.wait_ge(sg[tag + "_probt_dve"], b + 1 - n)

                        def attention(tag, scores, values):
                            for unit, block, used, ended in STEPS:
                                if unit is not None:
                                    k, i, heads = unit
                                    q, j = divmod(k // len(UNITS), HG)
                                    w = P * (i + 1)
                                    if k >= 3:
                                        pe.wait_ge(sg[tag + "_exp"], k - 2)
                                    for u, g in enumerate(heads):
                                        lhs, rhs = scores(q, i, HG * g + j)
                                        pe.matmul(bank[k % 3][:, u * w:(u + 1) * w], lhs, rhs, start=(u == 0),
                                                  stop=False, skip_group_check=True)
                                    s = bank[k % 3][:, 0:w * len(heads)].rearrange("p (h c) -> p h c", h=len(heads))
                                    pe.matmul(s[:, :, P * i:], ident_b,
                                              W["mask_b"].unsqueeze(1).broadcast_to([P, len(heads), P]), start=False,
                                              stop=True, skip_group_check=True).then_inc(sg[tag + "_scores"], 1)
                                if block is not None:
                                    b, i, m = block
                                    c = b // len(BLOCKS)
                                    pe.wait_ge(sg[tag + "_exp"], len(UNITS) * c + last_unit_of(i) + 1)
                                    if b >= 3:
                                        probt_ready(tag, b - 3)
                                    for g in range(HG):
                                        k, u = unit_of(c, i, g)
                                        at = P * (u * (i + 1) + m)
                                        ins = pe.transpose(bank[3 + b % 3][:, g * P:(g + 1) * P],
                                                           at_pr[k % len(at_pr)][:, at:at + P], ident)
                                    ins.then_inc(sg[tag + "_turned"], 1)
                                if used is not None:
                                    b, i, m = used
                                    c = b // len(BLOCKS)
                                    q, j = divmod(c, HG)
                                    probt_ready(tag, b)
                                    if b % len(BLOCKS) == 0 and c >= 1:
                                        pe.wait_ge(sg[tag + "_y"], c)
                                    for g in range(HG):
                                        ins = pe.matmul(bank[6][32 * g:32 * (g + 1), P * i:P * (i + 1)],
                                                        values(q, m, HG * g + j), PT[b % 3][:, g],
                                                        start=(i == NT - 1 and m == 0), stop=(m == i),
                                                        skip_group_check=True)
                                    ins.then_inc(sg[tag + "_av"], 1)
                                if ended is not None:
                                    pe.wait_ge(sg[tag + "_rec"], ended + 1)
                                    if ended >= 1:
                                        pe.wait_ge(sg[tag + "_rec_rows"], ended)
                                    spread_inverses().then_inc(sg[tag + "_rec_mm"], 1)

                        def l0_attention():
                            for q in PAIR:
                                turn(q, B[q], "l0_b", q + 1, "l0_turn")
                            for q in PAIR:
                                pe.wait_ge(sg["l0_f"], q + 1)
                                pe.matmul(pb(q, 0), W["l0_wqkv"][:, D:2 * D], F[q][:, PAD:], start=True,
                                          stop=True).then_inc(sg["l0_k_mm"], 1)
                                pe.matmul(pb(q, 1), W["l0_wqkv"][:, 0:D], F[q][:, PAD:], start=True,
                                          stop=True).then_inc(sg["l0_q_mm"], 1)
                                for half in range(2):
                                    for u in range(2):
                                        t = 2 * half + u
                                        i = pe.matmul(pb(q, 2 + half)[:, u * 2 * D:(u + 1) * 2 * D],
                                                      F[q][:, PAD + t * P:PAD + (t + 1) * P], W["l0_wqkv"][:, D:3 * D],
                                                      start=True, stop=True)
                                    i.then_inc(sg["l0_kv_mm"], 1)
                            for q in PAIR:
                                pe.wait_ge(sg["l0_kcs"], q + 1)
                                pe.wait_ge(sg["l0_q"], q + 1)
                                for c in range(NT - 1):
                                    for s in range(2):
                                        i = pe.matmul(pb(q, c)[:, s * H * (DH + 1):(s + 1) * H * (DH + 1)],
                                                      l0_kcs[q][:, c, s], VA[q][:, H * (DH + 1) * c:H * (DH + 1) * (c + 1)],
                                                      start=True, stop=True)
                                    i.then_inc(sg["l0_state_mm"], 1)
                            pe.wait_ge(sg["l0_state"], 2)
                            pe.wait_ge(sg["l0_qcs"], 2)
                            units = NT * QUARTETS
                            for n in range(units + 4):
                                if n < units:
                                    (q, j), c = divmod(n // NT, HG), n % NT
                                    tok = slice(c * P, (c + 1) * P)
                                    if n >= 3:
                                        pe.wait_ge(sg["l0_probt"], n - 2)
                                    for g in range(HG):
                                        if c == 0:
                                            pe.wait_ge(sg["l0_km"], n + g + 1)
                                        i = pe.matmul(bank[n % 3][:, g * P:(g + 1) * P], l0_km[n // NT % 2][g][:, tok],
                                                      l0_q[q][:, tok], start=True, stop=True)
                                    i.then_inc(sg["l0_scores"], 1)
                                if 2 <= n < units + 2:
                                    m = n - 2
                                    c4, c = divmod(m, NT)
                                    q, j = divmod(c4, HG)
                                    tok = slice(c * P, (c + 1) * P)
                                    pe.wait_ge(sg["l0_probt"], m + 1)
                                    if c == 0 and c4 >= 2:
                                        pe.wait_ge(sg["l0_y"], c4 - 1)
                                    out_of = [bank[5 + c4 % 2][32 * g:32 * (g + 1), tok] for g in range(HG)]
                                    for s in range(2 if c else 0):
                                        for g in range(HG):
                                            at = (DH + 1) * (HG * g + j)
                                            pe.matmul(out_of[g], l0_st[q][:, c - 1, s, at:at + 32], l0_qcs[q][:, s, tok],
                                                      start=False, stop=False, skip_group_check=True)
                                    for g in range(HG):
                                        at = (DH + 1) * (H * c + HG * g + j)
                                        i = pe.matmul(out_of[g], VA[q][:, at:at + 32], PT[m % 3][:, g], start=(c == 0),
                                                      stop=True, skip_group_check=True)
                                    i.then_inc(sg["l0_av"], 1)
                                if n >= NT + 2 and n % NT == 2:
                                    c4 = n // NT - 1
                                    pe.wait_ge(sg["l0_y"], c4 + 1)
                                    if c4 >= 1:
                                        pe.wait_ge(sg["l0_rec"], c4)
                                    for t in range(NT):
                                        i = pe.matmul(bank[4][:, HG * t:HG * (t + 1)],
                                                      l0_y[c4 // HG][c4 % HG][:, t * P:(t + 1) * P], W["sel_norm"],
                                                      start=True, stop=True)
                                    i.then_inc(sg["l0_norm_mm"], 1)
                                if n >= NT + 2 and n % NT == 3:
                                    c4 = n // NT - 1
                                    pe.wait_ge(sg["l0_rec"], c4 + 1)
                                    if c4 >= 1:
                                        pe.wait_ge(sg["l0_ctx"], c4)
                                    spread_inverses().then_inc(sg["l0_rec_mm"], 1)
                            for q in PAIR:
                                pe.wait_ge(sg["l0_ctx"], HG * (q + 1))
                                for t in range(NT):
                                    for j in range(HG):
                                        i = pe.matmul(pb3(q, 1)[:, t], l0_y[q][j][:, t * P:(t + 1) * P],
                                                      W["l0_wo4"][:, j], start=(j == 0), stop=(j == HG - 1),
                                                      skip_group_check=True)
                                i.then_inc(sg["l0_out_mm"], 1)
                            for q in PAIR:
                                turn(q, B[q], "l0_b2", q + 1, "l0_turn3")
                            for q in PAIR:
                                pe.wait_ge(sg["l0_f3"], q + 1)
                                for m in range(4):
                                    if m >= 2:
                                        pe.wait_ge(sg["l0_gelu"], 4 * q + m - 1)
                                    pe.matmul(pb(q, 2 + m % 2), W["l0_w1"][:, m * P:(m + 1) * P], F[q][:, PAD:], start=True,
                                              stop=True).then_inc(sg["l0_up_mm"], 1)
                            for q in PAIR:
                                pe.wait_ge(sg["l0_gelu"], 4 * (q + 1))
                                for t in range(NT):
                                    for m in range(4):
                                        i = pe.matmul(pb3(q, 1)[:, t], l0_gelu[q][:, m, t * P:(t + 1) * P],
                                                      W["l0_w2"][:, m], start=(m == 0), stop=(m == 3),
                                                      skip_group_check=True)
                                i.then_inc(sg["l0_mlp_mm"], 1)

                        def l0_channel_mix():
                            for q in PAIR:
                                turn(q, A[q], "c_a", q + 1, "c_turn")
                            for q in PAIR:
                                pe.wait_ge(sg["c_x"], 2 * q + 2)
                                pe.matmul(pb(q, 2), W["l0f_wk"], l0_qcs[q][:, 1], start=True,
                                          stop=True).then_inc(sg["c_k_mm"], 1)
                                for t in range(NT):
                                    i = pe.matmul(pb3(q, 3)[:, t], l0_qcs[q][:, 0, t * P:(t + 1) * P], W["l0f_wr"],
                                                  start=True, stop=True)
                                i.then_inc(sg["c_r_mm"], 1)
                            for q in PAIR:
                                pe.wait_ge(sg["c_k"], q + 1)
                                for t in range(NT):
                                    i = pe.matmul(pb3(q, 1)[:, t], l0_gelu[q][:, 0, t * P:(t + 1) * P], W["l0f_wv"],
                                                  start=True, stop=True)
                                i.then_inc(sg["c_v_mm"], 1)

                        def l1_attention():
                            for q in PAIR:
                                turn(q, A[q], "l1_a", q + 1, "l1_turn")
                            for q in PAIR:
                                pe.wait_ge(sg["l1_f"], q + 1)
                                pe.matmul(pb(q, 2), W["l1_wd4"], F[q][:, PAD:], start=True, stop=True)
                                tokens_by(q, 3, W["l1_wd4"][:, 0:LAT], LAT).then_inc(sg["l1_lat_mm"], 1)
                                for g in range(HG):
                                    if g >= 2:
                                        pe.wait_ge(sg["l1_q"], q * HG + g - 1)
                                    pe.matmul(pb(q, g % 2), absorbed_q[:, g], F[q][:, PAD:], start=True,
                                              stop=True).then_inc(sg["l1_q_mm"], 1)
                            pe.wait_ge(sg["l1_q"], 2 * HG)
                            pe.wait_ge(sg["l1_lat"], 2)
                            def scores(q, i, h):
                                return at_q[q][:, h // HG, P * i:P * (i + 1)], at_lm[q][:, h % HG, 0:P * (i + 1)]

                            def values(q, m, h):
                                return at_lv[q][:, m]
                            attention("l1", scores, values)
                            for q in PAIR:
                                pe.wait_ge(sg["l1_y"], 2 * HG)
                                for t in range(NT):
                                    for j in range(HG):
                                        i = pe.matmul(pb3(q, 2)[:, t], at_y[q][j][:, t * P:(t + 1) * P],
                                                      absorbed_o[:, j], start=(j == 0), stop=(j == HG - 1),
                                                      skip_group_check=True)
                                i.then_inc(sg["l1_out_mm"], 1)

                        def l1_moe():
                            for q in PAIR:
                                turn(q, A[q], "m_a", q + 1, "m_turn")
                            for q in PAIR:
                                pe.wait_ge(sg["m_f"], q + 1)
                                tokens_by(q, 1, W["mo_router"], 2 * NE1).then_inc(sg["m_logits_mm"], 1)
                            def turn_weights(q):
                                pe.wait_ge(sg["m_c3"], q + 1)
                                c3 = mo_c3[q].bitcast(BF16).rearrange("p (g e) -> p g e", e=96)
                                for g in range(2):
                                    for t in range(NT):
                                        at = g * T + t * P
                                        i = pe.transpose(bank[7][:].bitcast(BF16)[0:96, at:at + P], c3[:, 2 * t + g], ident_b)
                                i.then_inc(sg["m_ct_mm"], 1)
                            turn_weights(0)
                            for q in PAIR:
                                pe.wait_ge(sg["m_ct"], q + 1)
                                for n in range(NE1 + 2):
                                    if q == 0 and n == MOE_TURN:
                                        turn_weights(1)
                                    if n < NE1:
                                        k = q * NE1 + n
                                        if k >= 2:
                                            pe.wait_ge(sg["m_silu"], k - 1)
                                        pe.matmul(bank[k % 2][:], W["mo_wg"][:, n * P:(n + 1) * P], F[q][:, PAD:], start=True,
                                                  stop=True).then_inc(sg["m_gate"], 1)
                                        if k >= 2:
                                            pe.wait_ge(sg["m_h"], k - 1)
                                        pe.matmul(bank[2 + k % 2][:], W["mo_wu"][:, n * P:(n + 1) * P], F[q][:, PAD:],
                                                  start=True, stop=True).then_inc(sg["m_up"], 1)
                                        g, p = n // (NE1 // 2), n % (NE1 // 2)
                                        pe.matmul(bank[4 + k % 2][:], W["sel32"][:, p * P:(p + 1) * P],
                                                  mo_ct[q].bitcast(BF16)[0:96, g * T:(g + 1) * T], start=True,
                                                  stop=True).then_inc(sg["m_b"], 1)
                                    if n >= 2:
                                        k = q * NE1 + n - 2
                                        pe.wait_ge(sg["m_h"], k + 1)
                                        pe.matmul(bank[6 + q][:], W["mo_wd"][:, (n - 2) * P:(n - 1) * P], mo_h[k % 3],
                                                  start=(n == 2), stop=(n == NE1 + 1),
                                                  skip_group_check=True).then_inc(sg["m_down"], 1)
                            for q in PAIR:
                                pe.wait_ge(sg["m_acc"], 2)
                                for t in range(NT):
                                    i = pe.transpose(pb3(q, 0)[:, t], mo_acc[q][:, t * P:(t + 1) * P], ident)
                                i.then_inc(sg["m_back_mm"], 1)

                        def l2_attention():
                            for q in PAIR:
                                turn(q, A[q], "l2_a", q + 1, "l2_turn", b=3)
                            for q in PAIR:
                                pe.wait_ge(sg["l2_f"], q + 1)
                                for s, w in enumerate(("l2_wk", "l2_wq")):
                                    pe.matmul(pb(q, s), W[w], F[q][:, PAD:], start=True,
                                              stop=True).then_inc(sg["l2_qk_mm"], 1)
                                tokens_by(q, 2, W["l2_wv"], D).then_inc(sg["l2_v_mm"], 1)
                            pe.wait_ge(sg["l2_v"], 2)
                            def scores(q, i, h):
                                half, r, g = h % HG // 2, h % 2, h // HG
                                if i == NT - 1:
                                    pe.wait_ge(sg[f"l2_stacked{q}{half}{r}"], 16 * STACK_LOADS)
                                stack = at_stack[half][64 * r:64 * (r + 1)]
                                return stack[:, 1, g, P * i:P * (i + 1)], stack[:, 0, g, 0:P * (i + 1)]

                            def values(q, m, h):
                                return at_va[q][:, m, DH * h:DH * h + 32]
                            attention("l2", scores, values)
                            for q in PAIR:
                                pe.wait_ge(sg["l2_y"], 2 * HG)
                                for t in range(NT):
                                    for j in range(HG):
                                        i = pe.matmul(pb3(q, 1)[:, t], at_y[q][j][:, t * P:(t + 1) * P],
                                                      W["l2_wo4"][:, j], start=(j == 0), stop=(j == HG - 1),
                                                      skip_group_check=True)
                                i.then_inc(sg["l2_out_mm"], 1)

                        def expert_step(q, e, tag, weights):
                            if e < NE2:
                                if e >= 2:
                                    pe.wait_ge(sg[tag + "_fb"], NE2 * q + e - 1)
                                pe.matmul(pb(q, 1 + e % 2), W["sel8"][:, e * P:(e + 1) * P],
                                          mo_ct[q].bitcast(BF16)[0:24, 0:T], start=True,
                                          stop=True).then_inc(sg[tag + "_weights"], 1)
                            if e >= 1:
                                pe.wait_ge(sg[tag + "_fb"], NE2 * q + e)
                                for t in range(NT):
                                    i = pe.matmul(pb3(q, 3)[:, t], mo_fb[q][:, (e - 1) % 2, t * P:(t + 1) * P],
                                                  weights[:, (e - 1) * P:e * P], start=(e == 1 and t == 0),
                                                  stop=(e == NE2), skip_group_check=True)
                                i.then_inc(sg[tag + "_up"], 1)

                        def small_turn(q, tag):
                            pe.wait_ge(sg[tag + "_c3"], q + 1)
                            c3 = mo_c3[q][:, 0:NT * 12].bitcast(BF16).rearrange("p (g e) -> p g e", e=24)
                            for t in range(NT):
                                i = pe.transpose(pb(q, 2).bitcast(BF16)[0:24, t * P:(t + 1) * P], c3[:, t], ident_b)
                            i.then_inc(sg[tag + "_ct_mm"], 1)

                        def l2_moe():
                            for q in PAIR:
                                turn(q, A[q], "n_a", q + 1, "n_turn")
                            for q in PAIR:
                                pe.wait_ge(sg["n_f"], q + 1)
                                tokens_by(q, 1, W["l2f_router"], NE2).then_inc(sg["n_logits_mm"], 1)
                            for q in PAIR:
                                small_turn(q, "n")
                                pe.wait_ge(sg["n_ct"], q + 1)
                                for e in range(NE2 + 1):
                                    expert_step(q, e, "n", W["l2f_we"])

                        def l3_mamba():
                            for q in PAIR:
                                turn(q, B[q], "l3_b", q + 1, "l3_turn_b")
                            for q in PAIR:
                                pe.wait_ge(sg["l3_f"], q + 1)
                                tokens_by(q, 3, W["l3_win"][:, 768:772], NH3).then_inc(sg["l3_dt_mm"], 1)
                            for q in PAIR:
                                for c in range(4):
                                    if c >= 2:
                                        pe.wait_ge(sg["l3_xc"], 4 * q + c - 1)
                                    for k in range(TAPS):
                                        i = pe.matmul(pb(q, c % 2), taps_in[:, k, c * P:(c + 1) * P], F[q][:, k:k + T],
                                                      start=(k == 0), stop=(k == TAPS - 1))
                                    i.then_inc(sg["l3_xb_mm"], 1)
                                for half in range(2):
                                    if half:
                                        pe.wait_ge(sg["l3_z"], 2 * q + 1)
                                    for u in range(2):
                                        t = 2 * half + u
                                        i = pe.matmul(pb(q, 2)[:, u * DI:(u + 1) * DI], F[q][:, PAD + t * P:PAD + (t + 1) * P],
                                                      W["l3_win"][:, 0:DI], start=True, stop=True)
                                    i.then_inc(sg["l3_z_mm"], 1)
                                pe.wait_ge(sg["l3_da"], q + 1)
                                da = ma_sm[q][:, 3]
                                pe.matmul(pb(q, 3)[:, 16:32], W["tri"], da, start=True, stop=True)
                                pe.matmul(pb(q, 3)[:, 32:48], W["ones"], da, start=True, stop=True
                                          ).then_inc(sg["l3_cum_mm"], 1)
                                pe.wait_ge(sg["l3_xc"], 4 * (q + 1))
                                for t in range(NT):
                                    if t >= 2:
                                        pe.wait_ge(sg["l3_xt"], NT * q + t - 1)
                                    for c in range(3):
                                        i = pe.transpose(pb(q, t % 2)[:, c * P:(c + 1) * P],
                                                         ma_xc[q][:, c, t * P:(t + 1) * P], ident)
                                    i.then_inc(sg["l3_turn"], 1)
                            n = 0
                            for t in range(NT):
                                tok = slice(t * P, (t + 1) * P)
                                for q in PAIR:
                                    sm = ma_sm[q]
                                    if t == 0:
                                        pe.wait_ge(sg["l3_xt"], NT * (q + 1))
                                    else:
                                        pe.wait_ge(sg["l3_decay"], n - 1)
                                    for h in range(NH3):
                                        pe.matmul(pb3(q, 0)[:, h],
                                                  sm[:, 3, NH3 * t + h:NH3 * t + h + 1].broadcast_to([P, P]), W["tri"],
                                                  start=(h == 0), stop=False, skip_group_check=True)
                                    pe.matmul(pb(q, 0), W["neg_tri"],
                                              sm[:, 3, NH3 * t:NH3 * (t + 1)].unsqueeze(2).broadcast_to([P, NH3, P]),
                                              start=False, stop=False, skip_group_check=True)
                                    pe.matmul(pb(q, 0), ident_b, W["mask_tb"].unsqueeze(1).broadcast_to([P, NH3, P]),
                                              start=False, stop=True,
                                              skip_group_check=True).then_inc(sg["l3_decay_mm"], 1)
                                    if t == 0:
                                        pe.wait_ge(sg["l3_xc"], 4 * (q + 1))
                                    else:
                                        pe.wait_ge(sg["l3_w"], n - 1)
                                        pe.wait_ge(sg["l3_yread"], n - 1)
                                    i = pe.matmul(pb(q, 1)[:, 0:P], ma_xc[q][:, 2, tok], ma_xc[q][:, 3, tok],
                                                  start=True, stop=True)
                                    st = HR[q][:].rearrange("p t d -> p (t d)")[:, 0:DI]
                                    if t == 0:
                                        pe.wait_ge(sg["l3_z"], 2 * (q + 1))
                                        pe.wait_ge(sg["l3_xw"], q + 1)
                                    else:
                                        pe.wait_ge(sg["l3_state"], n - 1)
                                        i = pe.matmul(pb(q, 1)[:, P:P + DI], ma_xc[q][:, 3, tok], st, start=True,
                                                      stop=True)
                                    i.then_inc(sg["l3_g_mm"], 1)
                                    if t < NT - 1:
                                        pe.matmul(pb(q, 3)[:, 64:64 + DI], ma_bt[q][:, t], ma_xt[q][:, t], start=True,
                                                  stop=True).then_inc(sg["l3_state_mm"], 1)
                                    pe.wait_ge(sg["l3_w"], n + 1)
                                    for h in range(NH3):
                                        i = pe.matmul(pb(q, 2)[:, h * HP3:(h + 1) * HP3], PT[q][:, h],
                                                      ma_xd[q][:, t, h * HP3:(h + 1) * HP3], start=True, stop=True)
                                    i.then_inc(sg["l3_intra"], 1)
                                    n += 1
                            for q in PAIR:
                                pe.wait_ge(sg["l3_y"], q + 1)
                                for c in range(2):
                                    for t in range(NT):
                                        i = pe.transpose(pb3(q, c)[:, t], ma_y[q][:, t, c * P:(c + 1) * P], ident)
                                    i.then_inc(sg["l3_yt_mm"], 1)
                            for q in PAIR:
                                pe.wait_ge(sg["l3_yt"], 2 * (q + 1))
                                for t in range(NT):
                                    for c in range(2):
                                        i = pe.matmul(pb3(q, 2)[:, t], ma_xc[q][:, c, t * P:(t + 1) * P], W["l3_wout"][:, c],
                                                      start=(c == 0), stop=(c == 1), skip_group_check=True)
                                i.then_inc(sg["l3_out_mm"], 1)

                        def l3_ffn():
                            for q in PAIR:
                                turn(q, B[q], "f_b", q + 1, "f_turn")
                            for q in PAIR:
                                pe.wait_ge(sg["f_f"], q + 1)
                                pe.matmul(pb(q, 0)[0:64], W["l3f_wd"], F[q][:, PAD:], start=True,
                                          stop=True).then_inc(sg["f_down_mm"], 1)
                                tokens_by(q, 1, W["l3f_wq"], D).then_inc(sg["f_q_mm"], 1)
                                pe.wait_ge(sg["f_dt"], q + 1)
                                for t in range(NT):
                                    o = pb3(q, 2 + t // 2, 2)[:, t % 2]
                                    pe.matmul(o, ht_dt[q][0:64, t * P:(t + 1) * P], W["l3f_wup"], start=True, stop=False,
                                              skip_group_check=True)
                                    pe.matmul(o, W["ones"][0:1, :], W["l3f_bup"], start=False, stop=True,
                                              skip_group_check=True).then_inc(sg["f_kv_mm"], 1)
                            def output(q):
                                turn(q, ht_o[q], "f_o", q + 1, "f_turn2")
                                pe.wait_ge(sg["f_f2"], q + 1)
                                tokens_by(q, 1, W["l3f_wo"], D).then_inc(sg["f_out_mm"], 1)

                            def gate(q):
                                turn(q, B[q], "f_b2", q + 1, "f_turn3")
                                pe.wait_ge(sg["f_f3"], q + 1)
                                tokens_by(q, 1, W["l3f_wg"], NE2).then_inc(sg["f_gate_mm"], 1)

                            def experts(q, steps):
                                for e in steps:
                                    expert_step(q, e, "f", W["l3f_we"])

                            output(0)
                            gate(0)
                            small_turn(0, "f")
                            output(1)
                            pe.wait_ge(sg["f_ct"], 1)
                            experts(0, (0, 1, 2))
                            gate(1)
                            experts(0, (3, 4, 5))
                            small_turn(1, "f")
                            experts(0, (6, 7, 8))
                            pe.wait_ge(sg["f_ct"], 2)
                            experts(1, range(NE2 + 1))

                        for layer in (l0_attention, l0_channel_mix, l1_attention, l1_moe, l2_attention, l2_moe,
                                      l3_mamba, l3_ffn)[first:last]:
                            layer()

                numbers = sorted(s.num for s in pool_of_signals)
                assert numbers == list(range(numbers[0], numbers[-1] + 1)), numbers
                nc.vector.sem_clear(range(numbers[0], numbers[-1] + 1))
                nc.all_engine_barrier()


UNITS = ([(3, (g,)) for g in range(HG)] + [(2, (g,)) for g in range(HG)] + [(1, (0, 1)), (1, (2, 3)), (0, (0, 1, 2, 3))])
BLOCKS = [(i, m) for i in (3, 2, 1, 0) for m in range(i + 1)]
QUARTETS = len(PAIR) * HG


def last_unit_of(i):
    return max(n for n, unit in enumerate(UNITS) if unit[0] == i)


def unit_of(c, i, g):
    n, heads = next((n, heads) for n, (tile, heads) in enumerate(UNITS) if tile == i and g in heads)
    return len(UNITS) * c + n, heads.index(g)


def last_block(k):
    c, n = divmod(k, len(UNITS))
    return len(BLOCKS) * c + BLOCKS.index((UNITS[n][0], UNITS[n][0]))


def steps():
    units, blocks = len(UNITS) * QUARTETS, len(BLOCKS) * QUARTETS
    made, turned, b = [], [], 0
    while b < blocks:
        n = len(made)
        i, m = BLOCKS[b % len(BLOCKS)]
        ready = len(UNITS) * (b // len(BLOCKS)) + last_unit_of(i) + 2 <= n
        made.append((n,) + UNITS[n % len(UNITS)] if n < units else None)
        turned.append((b, i, m) if ready else None)
        b += ready
    used = [None] * AV_LAG + turned
    ended = [u[0] // len(BLOCKS) if u and u[1:] == BLOCKS[-1] else None for u in used]
    return list(zip(made + [None] * AV_LAG, turned + [None] * AV_LAG, used, ended))


AV_LAG = 2
STEPS = steps()
PRODUCTS = (3, 2, 1)
STACK_LOADS = sum(PRODUCTS) + len(PRODUCTS)
MOE_ROUTING = (2, 5, 8)
MOE_TURN = 12
SETUP_ONLY = ("l3_cw", "l1_wq_t", "l1_wk_t", "l1_wv_t", "l1_wout")


def on_act(b):
    return b % 10 in (1, 3, 6, 8)


def tables():
    f4 = np.float32
    bf = mybir.dt.np(BF16)
    pos = np.arange(T, dtype=np.float64)
    cs = np.stack([np.cos(np.pi / 2 * pos / T), np.sin(np.pi / 2 * pos / T)])
    c = {"ident": np.eye(P, dtype=f4), "ident_b": np.eye(P).astype(bf)}
    c["l0_cs_tok"] = cs.reshape(2, NT, P).transpose(2, 0, 1).astype(f4)
    c["l0_cs_feat"] = np.broadcast_to(cs, (P, 2, T)).astype(f4)
    i = np.arange(P)
    lag = i[None, :] - i[:, None]
    c["l0_mask"] = np.where(lag >= 0, np.cos(np.pi / 2 * lag / T), 0).astype(f4)
    c["l0_diag"] = (i[:, None] // DH == np.arange(H * (DH + 1))[None, :] // (DH + 1)).astype(f4)
    c["mask_b"] = np.where(i[None, :] > i[:, None], NEG, 0).astype(bf)
    c["mask_tb"] = np.where(i[None, :] < i[:, None], NEG, 0).astype(bf)
    c["tri"] = (i[:, None] <= i[None, :]).astype(f4)
    c["neg_tri"] = -c["tri"]
    c["ones"] = np.ones((P, P), f4)
    c["sel_norm"] = (i[:, None] == 32 * np.arange(HG)[None, :] + DH).astype(f4)
    c["iota"] = np.broadcast_to(np.arange(NE1), (P, NE1)).astype(f4)
    theta = (np.arange(T, dtype=f4)[:, None] * np.power(f4(10000.0), f4(-2.0) * np.arange(DH // 2, dtype=f4) / f4(DH)))
    rope = (np.cos(theta.astype(np.float64)) + np.sin(theta.astype(np.float64)))
    rows = np.stack([rope[:, p % (DH // 2)] for p in range(P)])
    c["quarter"] = (i[:, None] // 32 == np.arange(HG)[None, :]).astype(f4)
    c["of_head"] = (i[:, None] // DH == np.arange(H)[None, :]).astype(f4)
    c["l2_rope_k"] = rows.astype(f4)
    c["l2_rope_q"] = (rows / np.sqrt(DH)).astype(f4)
    sel32 = np.zeros((3, NE1, NE1 // 2, P))
    for p in range(NE1 // 2):
        for m in range(P):
            sel32[:, 2 * p + m // HID, p, m] = 1
    c["sel32"] = sel32.reshape(96, -1).astype(bf)
    sel8 = np.zeros((3, NE2, NE2, P))
    for e in range(NE2):
        sel8[:, e, e] = 1
    c["sel8"] = sel8.reshape(24, -1).astype(bf)
    return c


def kernel(**inputs):
    import concourse.bacc as bacc
    from concourse.bass_utils import run_bass_kernel_spmd as run

    g = {k: np.asarray(v) for k, v in inputs.items()}

    def by_quartet(w):
        o = np.zeros((HG, 32, HG, D), w.dtype)
        o[:, 0:DH] = w.reshape(HG, HG, DH, D).transpose(0, 2, 1, 3)
        return o.reshape(P, HG, D)

    def rows(v):
        return np.broadcast_to(v.reshape(1, -1), (P, v.size))

    def col(v):
        return v.reshape(-1, P).T

    a = dict(tables())
    w = g["L0_attn_qkv_w"]
    b = g["L0_attn_qkv_b"]
    a["l0_wqkv"] = w
    a["l0_bq"], a["l0_bk"] = col(b[0:D]), col(b[D:2 * D])
    a["l0_bkv"] = rows(b[D:])
    a["l0_wo4"], a["l0_bo"] = by_quartet(g["L0_attn_out_w"]), rows(g["L0_attn_out_b"])
    a["l0_n1"], a["l0_n2"] = col(g["L0_attn_norm1_w"]), col(g["L0_attn_norm2_w"])
    a["l0_w1"], a["l0_b1"] = g["L0_attn_mlp_w1"], col(g["L0_attn_mlp_b1"])
    a["l0_w2"] = g["L0_attn_mlp_w2"].reshape(4, P, D).transpose(1, 0, 2)
    a["l0_b2"] = rows(g["L0_attn_mlp_b2"])
    a["l0f_wr"], a["l0f_wk"], a["l0f_wv"] = (g["L0_ffn_W_" + s].T for s in "rkv")
    a["l0f_mu"] = np.stack([g["L0_ffn_mu_r"], g["L0_ffn_mu_k"]], 1)
    a["l1_wq_t"] = g["L1_attn_Wq"].transpose(1, 2, 0).reshape(H // 2, P, D).transpose(1, 0, 2)
    a["l1_wk_t"] = g["L1_attn_Wk_up"].transpose(1, 2, 0).reshape(H // 2, P, LAT).transpose(1, 0, 2)
    a["l1_wv_t"] = g["L1_attn_Wv_up"].transpose(1, 2, 0).reshape(H // 2, P, LAT).transpose(1, 0, 2)
    a["l1_wout"] = g["L1_attn_Wout"].reshape(H // 2, P, D).transpose(1, 0, 2)
    a["l1_wd4"] = np.tile(g["L1_attn_Wkv_down"], (1, 4))
    a["mo_router"] = np.concatenate([g["L1_ffn_router_w0"], g["L1_ffn_router_w1"]], 1)
    for s in "gu":
        a["mo_w" + s] = np.concatenate([g[f"L1_ffn_w{s}{i}"].transpose(1, 0, 2).reshape(D, -1) for i in range(2)], 1)
    a["mo_wd"] = np.concatenate([g[f"L1_ffn_wd{i}"].reshape(NE1 // 2, P, D).transpose(1, 0, 2).reshape(P, -1)
                                 for i in range(2)], 1)
    a["l2_wq"], a["l2_wk"] = g["L2_attn_Wq"].T, g["L2_attn_Wk"].T
    a["l2_bq"], a["l2_bk"] = col(g["L2_attn_bq"]), col(g["L2_attn_bk"])
    a["l2_wv"] = g["L2_attn_Wv"].T
    a["l2_wo4"] = by_quartet(g["L2_attn_Wo"].T)
    a["l2_bv"], a["l2_bo"] = rows(g["L2_attn_bv"]), rows(g["L2_attn_bo"])
    a["l2f_router"] = g["L2_ffn_router_w"].T
    a["l2f_we"] = g["L2_ffn_expert_weights"].transpose(1, 0, 2).reshape(D, -1)
    a["l3_nw"] = col(g["L3_attn_norm_w"])
    a["l3_win"] = g["L3_attn_in_proj_w"].T
    a["l3_cw"] = np.broadcast_to(g["L3_attn_conv_w"].T, (P, TAPS, 4 * P))
    a["l3_cb"] = col(g["L3_attn_conv_b"])
    a["l3_dtb"], a["l3_alog"] = rows(g["L3_attn_dt_bias"]), rows(g["L3_attn_A_log"])
    a["l3_d"] = rows(np.repeat(g["L3_attn_D_param"], HP3))
    a["l3_gw"] = col(g["L3_attn_gate_w"])
    a["l3_wout"] = g["L3_attn_out_proj_w"].T.reshape(2, P, D).transpose(1, 0, 2)
    a["l3f_g1"], a["l3f_g2"] = col(g["L3_ffn_gamma1"]), col(g["L3_ffn_gamma2"])
    a["l3f_wq"], a["l3f_bq"] = g["L3_ffn_Wq"], rows(g["L3_ffn_bq"])
    a["l3f_wd"], a["l3f_bd"] = g["L3_ffn_Wdown"], g["L3_ffn_bdown"].reshape(-1, 1)
    a["l3f_wup"] = g["L3_ffn_Wup"].reshape(64, H, 2, DH).transpose(0, 2, 1, 3).reshape(64, 2 * D)
    a["l3f_bup"] = g["L3_ffn_bup"].reshape(H, 2, DH).transpose(1, 0, 2).reshape(1, 2 * D)
    a["l3f_wo"], a["l3f_bo"] = g["L3_ffn_Wo"], rows(g["L3_ffn_bo"])
    a["l3f_wg"], a["l3f_bg"] = g["L3_ffn_Wg"], rows(g["L3_ffn_bg"])
    a["l3f_we"] = g["L3_ffn_We"].transpose(1, 0, 2).reshape(D, -1)
    a = {k: np.ascontiguousarray(v) for k, v in a.items()}

    nc = bacc.Bacc("TRN2", target_bir_lowering=False, num_devices=1)
    dram = {k: nc.dram_tensor(k, v.shape, mybir.dt.from_np(v.dtype), kind="ExternalInput").ap() for k, v in a.items()}
    x = np.ascontiguousarray(g["L0_attn_x"]).reshape(SEQS // 2, 2, T, D)
    x_in = nc.dram_tensor("x_in", x.shape, F32, kind="ExternalInput").ap()
    out = nc.dram_tensor("x_out", x.shape, F32, kind="ExternalOutput").ap()
    scratch = nc.dram_tensor("scratch", (2, 2, H, 3, DH, T), BF16).ap()
    program(nc, dram, x_in, out, scratch)
    a["x_in"] = x
    return run(nc, [a], core_ids=[0]).results[0]["x_out"].reshape(SEQS, T, D)
```
